# Optimizing a Trainium2 kernel written in Bass

```python
import numpy as np
import jax
import jax.numpy as jnp

def _softmax(x, axis=-1):
    return jax.nn.softmax(x, axis=axis)

def _gelu(x):
    return jax.nn.gelu(x, approximate=True)

def _silu(x):
    return jax.nn.silu(x)

def _sigmoid(x):
    return jax.nn.sigmoid(x)

def _layernorm(x, axis=-1, eps=1e-05):
    m = jnp.mean(x, axis=axis, keepdims=True)
    v = jnp.var(x, axis=axis, keepdims=True)
    return (x - m) / jnp.sqrt(v + eps)

def _scatter_add(tgt, idx, src, axis=0):
    return tgt.at[idx].add(src)

def _segment_sum(src, seg, n):
    return jax.ops.segment_sum(src, seg, n)
kernel_name = 'mk_adaln_ffn_d4_seqx_r8_ee7ecc'

def setup_inputs(seed: int=0):
    np.random.seed(seed)
    _w = jnp.asarray

    def _rec_inputs():
        import jax
        import jax.numpy as jnp
        _rk = jax.random.key(seed)
        x = -0.000125 + 0.9999 * jax.random.normal(jax.random.fold_in(_rk, 1), (4, 256, 256), jnp.float32)
        _lenS = 256 - jax.random.randint(jax.random.fold_in(_rk, 7), (4,), 0, max(1, 256 // 4) + 1, jnp.int32)
        _lenS2 = 256 - jax.random.randint(jax.random.fold_in(_rk, 8), (4,), 0, max(1, 256 // 4) + 1, jnp.int32)
        fside_BxSxS_0 = -1.52775e-05 + 0.999936 * jax.random.normal(jax.random.fold_in(_rk, 11), (4, 256, 256), jnp.float32)
        cond_512 = -5.03954e-05 + 1.00559 * jax.random.normal(jax.random.fold_in(_rk, 12), (4, 64), jnp.float32)
        return (x, fside_BxSxS_0, cond_512)
    x, fside_BxSxS_0, cond_512 = _rec_inputs()

    def _L0_cond_setup():
        import jax, jax.numpy as jnp
        from jax import lax
        import numpy as np
        B, T, C, TD = (8, 256, 256, 64)

        def _bi_wkv(r, k, v, w, u, time_emb):
            tf = jax.nn.sigmoid(jnp.sum(time_emb, axis=-1))[:, None, None]
            decay = jnp.exp(-jnp.exp(w.astype(jnp.float32)))[None, :] * (0.5 + 0.5 * tf[:, :, 0])
            kf = k.astype(jnp.float32)
            vf = v.astype(jnp.float32)
            ek = jnp.exp(jnp.minimum(kf, 30.0))
            ekv = ek * vf

            def step(carry, x):
                a, b = carry
                ekv_t, ek_t = x
                a = a * decay + ekv_t
                b = b * decay + ek_t
                return ((a, b), (a, b))
            ekv_t = jnp.swapaxes(ekv, 0, 1)
            ek_t = jnp.swapaxes(ek, 0, 1)
            init = (jnp.zeros_like(decay), jnp.zeros_like(decay))
            _, (nf, df) = lax.scan(step, init, (ekv_t, ek_t))
            _, (nb, db) = lax.scan(step, init, (ekv_t, ek_t), reverse=True)
            nf = jnp.swapaxes(nf, 0, 1)
            df = jnp.swapaxes(df, 0, 1)
            nb = jnp.swapaxes(nb, 0, 1)
            db = jnp.swapaxes(db, 0, 1)
            euk = jnp.exp(jnp.minimum(u.astype(jnp.float32)[None, None, :] + kf, 30.0))
            num = nf + nb - ekv + euk * vf
            den = df + db - ek + euk
            base = jax.nn.sigmoid(r.astype(jnp.float32)) * (num / jnp.maximum(den, 1e-08))
            out = base * (0.8 + 0.2 * tf)
            return out.astype(r.dtype)
        key = jax.random.key(seed)
        ks = jax.random.split(key, 6)
        return {'r': jax.random.normal(ks[0], (B, T, C), dtype=jnp.float32), 'k': jax.random.normal(ks[1], (B, T, C), dtype=jnp.float32), 'v': jax.random.normal(ks[2], (B, T, C), dtype=jnp.float32), 'w': jax.random.normal(ks[3], (C,), dtype=jnp.float32), 'u': jax.random.normal(ks[4], (C,), dtype=jnp.float32), 'time_emb': jax.random.normal(ks[5], (B, TD), dtype=jnp.float32)}
    _L0_cond_all = _L0_cond_setup()
    _L0_cond_in = {k: v for k, v in _L0_cond_all.items() if k in ('w', 'u')}
    del _L0_cond_all

    def _L0_ffn_setup():
        import jax, jax.numpy as jnp
        import numpy as np
        E = 8
        H = 256
        F = 512
        B, S = (2, 128)
        JITTER = 0.01
        TOP_K = 2

        def _masked_sampling_omp(scores):
            vals, idx = jax.lax.top_k(scores, TOP_K)
            abs_s = jnp.abs(scores)
            thr1 = vals[:, 0:1]
            factor1 = jnp.maximum(abs_s, thr1)
            mask1 = (thr1 - scores) / factor1 > 2.0 * JITTER
            p1 = jax.nn.softmax(jnp.where(mask1, -jnp.inf, scores), axis=-1)
            m1 = jnp.take_along_axis(p1, idx[:, 0:1], axis=-1)
            thr2 = vals[:, 1:2]
            factor2 = jnp.maximum(abs_s, thr2)
            mask2 = (thr2 - scores) / factor2 > 2.0 * JITTER
            is_top1 = jnp.arange(scores.shape[-1])[None, :] == idx[:, 0:1]
            p2 = jax.nn.softmax(jnp.where(is_top1 | mask2, -jnp.inf, scores), axis=-1)
            m2 = jnp.take_along_axis(p2, idx[:, 1:2], axis=-1)
            return (jnp.concatenate([m1, m2], axis=-1), idx)
        key = jax.random.key(seed)
        k0, k1, k2, k3, k4 = jax.random.split(key, 5)
        s = 0.02
        return {'hidden_states': jax.random.normal(k0, (B, S, H), jnp.float32), 'gate_w': jax.random.normal(k1, (E, H), jnp.float32) * s, 'w1': jax.random.normal(k2, (E, F, H), jnp.float32) * s, 'w2': jax.random.normal(k3, (E, H, F), jnp.float32) * s, 'w3': jax.random.normal(k4, (E, F, H), jnp.float32) * s}
    _L0_ffn_all = _L0_ffn_setup()
    _L0_ffn_in = {k: v for k, v in _L0_ffn_all.items() if k in ('gate_w', 'w1', 'w2', 'w3')}
    del _L0_ffn_all

    def _L1_cond_setup():
        import jax, jax.numpy as jnp
        from jax import lax
        import numpy as np
        B, T, C, TD = (8, 256, 256, 64)

        def _bi_wkv(r, k, v, w, u, time_emb):
            tf = jax.nn.sigmoid(jnp.sum(time_emb, axis=-1))[:, None, None]
            decay = jnp.exp(-jnp.exp(w.astype(jnp.float32)))[None, :] * (0.5 + 0.5 * tf[:, :, 0])
            kf = k.astype(jnp.float32)
            vf = v.astype(jnp.float32)
            ek = jnp.exp(jnp.minimum(kf, 30.0))
            ekv = ek * vf

            def step(carry, x):
                a, b = carry
                ekv_t, ek_t = x
                a = a * decay + ekv_t
                b = b * decay + ek_t
                return ((a, b), (a, b))
            ekv_t = jnp.swapaxes(ekv, 0, 1)
            ek_t = jnp.swapaxes(ek, 0, 1)
            init = (jnp.zeros_like(decay), jnp.zeros_like(decay))
            _, (nf, df) = lax.scan(step, init, (ekv_t, ek_t))
            _, (nb, db) = lax.scan(step, init, (ekv_t, ek_t), reverse=True)
            nf = jnp.swapaxes(nf, 0, 1)
            df = jnp.swapaxes(df, 0, 1)
            nb = jnp.swapaxes(nb, 0, 1)
            db = jnp.swapaxes(db, 0, 1)
            euk = jnp.exp(jnp.minimum(u.astype(jnp.float32)[None, None, :] + kf, 30.0))
            num = nf + nb - ekv + euk * vf
            den = df + db - ek + euk
            base = jax.nn.sigmoid(r.astype(jnp.float32)) * (num / jnp.maximum(den, 1e-08))
            out = base * (0.8 + 0.2 * tf)
            return out.astype(r.dtype)
        key = jax.random.key(seed)
        ks = jax.random.split(key, 6)
        return {'r': jax.random.normal(ks[0], (B, T, C), dtype=jnp.float32), 'k': jax.random.normal(ks[1], (B, T, C), dtype=jnp.float32), 'v': jax.random.normal(ks[2], (B, T, C), dtype=jnp.float32), 'w': jax.random.normal(ks[3], (C,), dtype=jnp.float32), 'u': jax.random.normal(ks[4], (C,), dtype=jnp.float32), 'time_emb': jax.random.normal(ks[5], (B, TD), dtype=jnp.float32)}
    _L1_cond_all = _L1_cond_setup()
    _L1_cond_in = {k: v for k, v in _L1_cond_all.items() if k in ('w', 'u')}
    del _L1_cond_all

    def _L1_ffn_setup():
        import jax, jax.numpy as jnp
        import numpy as np
        B, S, D = (4, 256, 256)
        E = 8
        H = 352
        CAP_F = 1.0

        def _moe(x, Wg, W1, W3, W2, sw1, sw3, sw2):
            b, sl, d = x.shape
            T = b * sl
            C = int(CAP_F * T / E)
            xt = x.reshape(T, d)
            probs = jax.nn.softmax(xt @ Wg, axis=-1)
            eidx = jnp.argmax(probs, axis=-1)
            gate = jnp.take_along_axis(probs, eidx[:, None], 1)[:, 0]
            oh = jax.nn.one_hot(eidx, E, dtype=jnp.int32)
            pos = (jnp.cumsum(oh, axis=0) * oh).sum(-1) - 1
            keep = pos < C
            flat = jnp.where(keep, eidx * C + pos, E * C)
            xd = jnp.zeros((E * C, d), x.dtype).at[flat].set(xt, mode='drop')
            xd = xd.reshape(E, C, d)
            h = jax.nn.silu(jnp.einsum('ecd,edh->ech', xd, W1)) * jnp.einsum('ecd,edh->ech', xd, W3)
            oe = jnp.einsum('ech,ehd->ecd', h, W2).reshape(E * C, d)
            out = jnp.take(oe, jnp.minimum(flat, E * C - 1), axis=0)
            out = out * (gate * keep.astype(x.dtype))[:, None]
            shared = jax.nn.silu(xt @ sw1) * (xt @ sw3) @ sw2
            return (out + shared).reshape(b, sl, d)
        key = jax.random.key(seed)
        ks = jax.random.split(key, 8)
        s = lambda fan: 1.0 / np.sqrt(fan)
        return {'x': jax.random.normal(ks[0], (B, S, D), jnp.float32), 'Wg': jax.random.normal(ks[1], (D, E), jnp.float32) * s(D), 'W1': jax.random.normal(ks[2], (E, D, H), jnp.float32) * s(D), 'W3': jax.random.normal(ks[3], (E, D, H), jnp.float32) * s(D), 'W2': jax.random.normal(ks[4], (E, H, D), jnp.float32) * s(H), 'sw1': jax.random.normal(ks[5], (D, H), jnp.float32) * s(D), 'sw3': jax.random.normal(ks[6], (D, H), jnp.float32) * s(D), 'sw2': jax.random.normal(ks[7], (H, D), jnp.float32) * s(H)}
    _L1_ffn_all = _L1_ffn_setup()
    _L1_ffn_in = {k: v for k, v in _L1_ffn_all.items() if k in ('Wg', 'W1', 'W3', 'W2', 'sw1', 'sw3', 'sw2')}
    del _L1_ffn_all

    def _L2_cond_setup():
        import jax, jax.numpy as jnp
        from jax import lax
        import numpy as np
        B, T, C, TD = (8, 256, 256, 64)

        def _bi_wkv(r, k, v, w, u, time_emb):
            tf = jax.nn.sigmoid(jnp.sum(time_emb, axis=-1))[:, None, None]
            decay = jnp.exp(-jnp.exp(w.astype(jnp.float32)))[None, :] * (0.5 + 0.5 * tf[:, :, 0])
            kf = k.astype(jnp.float32)
            vf = v.astype(jnp.float32)
            ek = jnp.exp(jnp.minimum(kf, 30.0))
            ekv = ek * vf

            def step(carry, x):
                a, b = carry
                ekv_t, ek_t = x
                a = a * decay + ekv_t
                b = b * decay + ek_t
                return ((a, b), (a, b))
            ekv_t = jnp.swapaxes(ekv, 0, 1)
            ek_t = jnp.swapaxes(ek, 0, 1)
            init = (jnp.zeros_like(decay), jnp.zeros_like(decay))
            _, (nf, df) = lax.scan(step, init, (ekv_t, ek_t))
            _, (nb, db) = lax.scan(step, init, (ekv_t, ek_t), reverse=True)
            nf = jnp.swapaxes(nf, 0, 1)
            df = jnp.swapaxes(df, 0, 1)
            nb = jnp.swapaxes(nb, 0, 1)
            db = jnp.swapaxes(db, 0, 1)
            euk = jnp.exp(jnp.minimum(u.astype(jnp.float32)[None, None, :] + kf, 30.0))
            num = nf + nb - ekv + euk * vf
            den = df + db - ek + euk
            base = jax.nn.sigmoid(r.astype(jnp.float32)) * (num / jnp.maximum(den, 1e-08))
            out = base * (0.8 + 0.2 * tf)
            return out.astype(r.dtype)
        key = jax.random.key(seed)
        ks = jax.random.split(key, 6)
        return {'r': jax.random.normal(ks[0], (B, T, C), dtype=jnp.float32), 'k': jax.random.normal(ks[1], (B, T, C), dtype=jnp.float32), 'v': jax.random.normal(ks[2], (B, T, C), dtype=jnp.float32), 'w': jax.random.normal(ks[3], (C,), dtype=jnp.float32), 'u': jax.random.normal(ks[4], (C,), dtype=jnp.float32), 'time_emb': jax.random.normal(ks[5], (B, TD), dtype=jnp.float32)}
    _L2_cond_all = _L2_cond_setup()
    _L2_cond_in = {k: v for k, v in _L2_cond_all.items() if k in ('w', 'u')}
    del _L2_cond_all

    def _L2_ffn_setup():
        import jax, jax.numpy as jnp
        import numpy as np
        FP8_MAX = 448.0
        GLOBAL_DIV = 448.0 * 6.0

        def _fp8(x):
            return x.astype(jnp.float8_e4m3fn).astype(jnp.float32)

        def _reorder_quantize_x(x, idx):
            scale = jnp.max(jnp.abs(x)) / GLOBAL_DIV
            xr = (x / scale)[:, idx]
            scale_x = jnp.max(jnp.abs(xr), axis=1, keepdims=True) / FP8_MAX
            qx = _fp8(xr / scale_x)
            return (qx, scale_x, scale)

        def _qlinear(qx, scale_x, scale, W, idx, out_idx=None):
            Wr = W[:, idx]
            w_scale = jnp.max(jnp.abs(Wr), axis=1, keepdims=True) / FP8_MAX
            qw = _fp8(Wr / w_scale)
            y = qx * scale_x @ (qw * w_scale).T * scale
            if out_idx is not None:
                y = y[:, out_idx]
            return y
        key = jax.random.key(seed)
        ks = jax.random.split(key, 6)
        B, S, H, I = (2, 128, 256, 704)
        return {'x': jax.random.normal(ks[0], (B, S, H), jnp.float32), 'w_gate': jax.random.normal(ks[1], (I, H), jnp.float32) * 0.02, 'w_up': jax.random.normal(ks[2], (I, H), jnp.float32) * 0.02, 'w_down': jax.random.normal(ks[3], (H, I), jnp.float32) * 0.02, 'up_reorder_index': jax.random.permutation(ks[4], jnp.arange(H, dtype=jnp.int64)), 'down_reorder_index': jax.random.permutation(ks[5], jnp.arange(I, dtype=jnp.int64))}
    _L2_ffn_all = _L2_ffn_setup()
    _L2_ffn_in = {k: v for k, v in _L2_ffn_all.items() if k in ('w_gate', 'w_up', 'w_down', 'up_reorder_index', 'down_reorder_index')}
    del _L2_ffn_all

    def _L3_cond_setup():
        import jax, jax.numpy as jnp
        from jax import lax
        import numpy as np
        B, T, C, TD = (8, 256, 256, 64)

        def _bi_wkv(r, k, v, w, u, time_emb):
            tf = jax.nn.sigmoid(jnp.sum(time_emb, axis=-1))[:, None, None]
            decay = jnp.exp(-jnp.exp(w.astype(jnp.float32)))[None, :] * (0.5 + 0.5 * tf[:, :, 0])
            kf = k.astype(jnp.float32)
            vf = v.astype(jnp.float32)
            ek = jnp.exp(jnp.minimum(kf, 30.0))
            ekv = ek * vf

            def step(carry, x):
                a, b = carry
                ekv_t, ek_t = x
                a = a * decay + ekv_t
                b = b * decay + ek_t
                return ((a, b), (a, b))
            ekv_t = jnp.swapaxes(ekv, 0, 1)
            ek_t = jnp.swapaxes(ek, 0, 1)
            init = (jnp.zeros_like(decay), jnp.zeros_like(decay))
            _, (nf, df) = lax.scan(step, init, (ekv_t, ek_t))
            _, (nb, db) = lax.scan(step, init, (ekv_t, ek_t), reverse=True)
            nf = jnp.swapaxes(nf, 0, 1)
            df = jnp.swapaxes(df, 0, 1)
            nb = jnp.swapaxes(nb, 0, 1)
            db = jnp.swapaxes(db, 0, 1)
            euk = jnp.exp(jnp.minimum(u.astype(jnp.float32)[None, None, :] + kf, 30.0))
            num = nf + nb - ekv + euk * vf
            den = df + db - ek + euk
            base = jax.nn.sigmoid(r.astype(jnp.float32)) * (num / jnp.maximum(den, 1e-08))
            out = base * (0.8 + 0.2 * tf)
            return out.astype(r.dtype)
        key = jax.random.key(seed)
        ks = jax.random.split(key, 6)
        return {'r': jax.random.normal(ks[0], (B, T, C), dtype=jnp.float32), 'k': jax.random.normal(ks[1], (B, T, C), dtype=jnp.float32), 'v': jax.random.normal(ks[2], (B, T, C), dtype=jnp.float32), 'w': jax.random.normal(ks[3], (C,), dtype=jnp.float32), 'u': jax.random.normal(ks[4], (C,), dtype=jnp.float32), 'time_emb': jax.random.normal(ks[5], (B, TD), dtype=jnp.float32)}
    _L3_cond_all = _L3_cond_setup()
    _L3_cond_in = {k: v for k, v in _L3_cond_all.items() if k in ('w', 'u')}
    del _L3_cond_all

    def _L3_ffn_setup():
        import jax, jax.numpy as jnp
        import numpy as np
        _FP8_MAX = 448.0
        _BLOCK = 32
        _EPS = 1e-30

        def _mx_dequant(t):
            rows, feat = t.shape
            blocks = t.reshape(rows, feat // _BLOCK, _BLOCK)
            max_abs = jnp.max(jnp.abs(blocks), axis=-1)
            scales = jnp.maximum(max_abs / _FP8_MAX, _EPS)
            q = (blocks / scales[..., None]).astype(jnp.float8_e4m3fn).astype(jnp.float32)
            return (q * scales[..., None]).reshape(rows, feat)

        def _mx_linear(x2d, w):
            return _mx_dequant(x2d) @ _mx_dequant(w).T
        key = jax.random.key(seed)
        k1, k2, k3, k4 = jax.random.split(key, 4)
        B, S, H, I = (2, 128, 256, 1024)
        return {'x': jax.random.normal(k1, (B, S, H), dtype=jnp.float32), 'gate_w': jax.random.normal(k2, (I, H), dtype=jnp.float32) * 0.02, 'up_w': jax.random.normal(k3, (I, H), dtype=jnp.float32) * 0.02, 'down_w': jax.random.normal(k4, (H, I), dtype=jnp.float32) * 0.02}
    _L3_ffn_all = _L3_ffn_setup()
    _L3_ffn_in = {k: v for k, v in _L3_ffn_all.items() if k in ('gate_w', 'up_w', 'down_w')}
    del _L3_ffn_all
    return {'x': x, 'fside_BxSxS_0': fside_BxSxS_0, 'cond_512': cond_512, 'L0_cond_w': _L0_cond_in['w'], 'L0_cond_u': _L0_cond_in['u'], 'L0_ffn_gate_w': _L0_ffn_in['gate_w'], 'L0_ffn_w1': _L0_ffn_in['w1'], 'L0_ffn_w2': _L0_ffn_in['w2'], 'L0_ffn_w3': _L0_ffn_in['w3'], 'L1_cond_w': _L1_cond_in['w'], 'L1_cond_u': _L1_cond_in['u'], 'L1_ffn_Wg': _L1_ffn_in['Wg'], 'L1_ffn_W1': _L1_ffn_in['W1'], 'L1_ffn_W3': _L1_ffn_in['W3'], 'L1_ffn_W2': _L1_ffn_in['W2'], 'L1_ffn_sw1': _L1_ffn_in['sw1'], 'L1_ffn_sw3': _L1_ffn_in['sw3'], 'L1_ffn_sw2': _L1_ffn_in['sw2'], 'L2_cond_w': _L2_cond_in['w'], 'L2_cond_u': _L2_cond_in['u'], 'L2_ffn_w_gate': _L2_ffn_in['w_gate'], 'L2_ffn_w_up': _L2_ffn_in['w_up'], 'L2_ffn_w_down': _L2_ffn_in['w_down'], 'L2_ffn_up_reorder_index': _L2_ffn_in['up_reorder_index'], 'L2_ffn_down_reorder_index': _L2_ffn_in['down_reorder_index'], 'L3_cond_w': _L3_cond_in['w'], 'L3_cond_u': _L3_cond_in['u'], 'L3_ffn_gate_w': _L3_ffn_in['gate_w'], 'L3_ffn_up_w': _L3_ffn_in['up_w'], 'L3_ffn_down_w': _L3_ffn_in['down_w']}

def reference(x, fside_BxSxS_0, cond_512, L0_cond_w, L0_cond_u, L0_ffn_gate_w, L0_ffn_w1, L0_ffn_w2, L0_ffn_w3, L1_cond_w, L1_cond_u, L1_ffn_Wg, L1_ffn_W1, L1_ffn_W3, L1_ffn_W2, L1_ffn_sw1, L1_ffn_sw3, L1_ffn_sw2, L2_cond_w, L2_cond_u, L2_ffn_w_gate, L2_ffn_w_up, L2_ffn_w_down, L2_ffn_up_reorder_index, L2_ffn_down_reorder_index, L3_cond_w, L3_cond_u, L3_ffn_gate_w, L3_ffn_up_w, L3_ffn_down_w):
    import jax
    import jax.numpy as jnp

    def _L0_cond_ref(r, k, v, w, u, time_emb):
        import jax, jax.numpy as jnp
        from jax import lax
        import numpy as np
        B, T, C, TD = (8, 256, 256, 64)

        def _bi_wkv(r, k, v, w, u, time_emb):
            tf = jax.nn.sigmoid(jnp.sum(time_emb, axis=-1))[:, None, None]
            decay = jnp.exp(-jnp.exp(w.astype(jnp.float32)))[None, :] * (0.5 + 0.5 * tf[:, :, 0])
            kf = k.astype(jnp.float32)
            vf = v.astype(jnp.float32)
            ek = jnp.exp(jnp.minimum(kf, 30.0))
            ekv = ek * vf

            def step(carry, x):
                a, b = carry
                ekv_t, ek_t = x
                a = a * decay + ekv_t
                b = b * decay + ek_t
                return ((a, b), (a, b))
            ekv_t = jnp.swapaxes(ekv, 0, 1)
            ek_t = jnp.swapaxes(ek, 0, 1)
            init = (jnp.zeros_like(decay), jnp.zeros_like(decay))
            _, (nf, df) = lax.scan(step, init, (ekv_t, ek_t))
            _, (nb, db) = lax.scan(step, init, (ekv_t, ek_t), reverse=True)
            nf = jnp.swapaxes(nf, 0, 1)
            df = jnp.swapaxes(df, 0, 1)
            nb = jnp.swapaxes(nb, 0, 1)
            db = jnp.swapaxes(db, 0, 1)
            euk = jnp.exp(jnp.minimum(u.astype(jnp.float32)[None, None, :] + kf, 30.0))
            num = nf + nb - ekv + euk * vf
            den = df + db - ek + euk
            base = jax.nn.sigmoid(r.astype(jnp.float32)) * (num / jnp.maximum(den, 1e-08))
            out = base * (0.8 + 0.2 * tf)
            return out.astype(r.dtype)
        return _bi_wkv(r, k, v, w, u, time_emb)

    def _L0_ffn_ref(hidden_states, gate_w, w1, w2, w3):
        import jax, jax.numpy as jnp
        import numpy as np
        E = 8
        H = 256
        F = 512
        B, S = (2, 128)
        JITTER = 0.01
        TOP_K = 2

        def _masked_sampling_omp(scores):
            vals, idx = jax.lax.top_k(scores, TOP_K)
            abs_s = jnp.abs(scores)
            thr1 = vals[:, 0:1]
            factor1 = jnp.maximum(abs_s, thr1)
            mask1 = (thr1 - scores) / factor1 > 2.0 * JITTER
            p1 = jax.nn.softmax(jnp.where(mask1, -jnp.inf, scores), axis=-1)
            m1 = jnp.take_along_axis(p1, idx[:, 0:1], axis=-1)
            thr2 = vals[:, 1:2]
            factor2 = jnp.maximum(abs_s, thr2)
            mask2 = (thr2 - scores) / factor2 > 2.0 * JITTER
            is_top1 = jnp.arange(scores.shape[-1])[None, :] == idx[:, 0:1]
            p2 = jax.nn.softmax(jnp.where(is_top1 | mask2, -jnp.inf, scores), axis=-1)
            m2 = jnp.take_along_axis(p2, idx[:, 1:2], axis=-1)
            return (jnp.concatenate([m1, m2], axis=-1), idx)
        Bd, Sd, Hd = hidden_states.shape
        x = hidden_states.reshape(-1, Hd)
        scores = x @ gate_w.T
        mult, sel = _masked_sampling_omp(scores)
        h = jax.nn.silu(jnp.einsum('th,efh->etf', x, w1)) * jnp.einsum('th,efh->etf', x, w3)
        y = jnp.einsum('etf,ehf->eth', h, w2)
        coef = (jax.nn.one_hot(sel, gate_w.shape[0], dtype=x.dtype) * mult[..., None]).sum(axis=1)
        out = jnp.einsum('te,eth->th', coef, y)
        return out.reshape(Bd, Sd, Hd)

    def _L1_cond_ref(r, k, v, w, u, time_emb):
        import jax, jax.numpy as jnp
        from jax import lax
        import numpy as np
        B, T, C, TD = (8, 256, 256, 64)

        def _bi_wkv(r, k, v, w, u, time_emb):
            tf = jax.nn.sigmoid(jnp.sum(time_emb, axis=-1))[:, None, None]
            decay = jnp.exp(-jnp.exp(w.astype(jnp.float32)))[None, :] * (0.5 + 0.5 * tf[:, :, 0])
            kf = k.astype(jnp.float32)
            vf = v.astype(jnp.float32)
            ek = jnp.exp(jnp.minimum(kf, 30.0))
            ekv = ek * vf

            def step(carry, x):
                a, b = carry
                ekv_t, ek_t = x
                a = a * decay + ekv_t
                b = b * decay + ek_t
                return ((a, b), (a, b))
            ekv_t = jnp.swapaxes(ekv, 0, 1)
            ek_t = jnp.swapaxes(ek, 0, 1)
            init = (jnp.zeros_like(decay), jnp.zeros_like(decay))
            _, (nf, df) = lax.scan(step, init, (ekv_t, ek_t))
            _, (nb, db) = lax.scan(step, init, (ekv_t, ek_t), reverse=True)
            nf = jnp.swapaxes(nf, 0, 1)
            df = jnp.swapaxes(df, 0, 1)
            nb = jnp.swapaxes(nb, 0, 1)
            db = jnp.swapaxes(db, 0, 1)
            euk = jnp.exp(jnp.minimum(u.astype(jnp.float32)[None, None, :] + kf, 30.0))
            num = nf + nb - ekv + euk * vf
            den = df + db - ek + euk
            base = jax.nn.sigmoid(r.astype(jnp.float32)) * (num / jnp.maximum(den, 1e-08))
            out = base * (0.8 + 0.2 * tf)
            return out.astype(r.dtype)
        return _bi_wkv(r, k, v, w, u, time_emb)

    def _L1_ffn_ref(x, Wg, W1, W3, W2, sw1, sw3, sw2):
        import jax, jax.numpy as jnp
        import numpy as np
        B, S, D = (4, 256, 256)
        E = 8
        H = 352
        CAP_F = 1.0

        def _moe(x, Wg, W1, W3, W2, sw1, sw3, sw2):
            b, sl, d = x.shape
            T = b * sl
            C = int(CAP_F * T / E)
            xt = x.reshape(T, d)
            probs = jax.nn.softmax(xt @ Wg, axis=-1)
            eidx = jnp.argmax(probs, axis=-1)
            gate = jnp.take_along_axis(probs, eidx[:, None], 1)[:, 0]
            oh = jax.nn.one_hot(eidx, E, dtype=jnp.int32)
            pos = (jnp.cumsum(oh, axis=0) * oh).sum(-1) - 1
            keep = pos < C
            flat = jnp.where(keep, eidx * C + pos, E * C)
            xd = jnp.zeros((E * C, d), x.dtype).at[flat].set(xt, mode='drop')
            xd = xd.reshape(E, C, d)
            h = jax.nn.silu(jnp.einsum('ecd,edh->ech', xd, W1)) * jnp.einsum('ecd,edh->ech', xd, W3)
            oe = jnp.einsum('ech,ehd->ecd', h, W2).reshape(E * C, d)
            out = jnp.take(oe, jnp.minimum(flat, E * C - 1), axis=0)
            out = out * (gate * keep.astype(x.dtype))[:, None]
            shared = jax.nn.silu(xt @ sw1) * (xt @ sw3) @ sw2
            return (out + shared).reshape(b, sl, d)
        return _moe(x, Wg, W1, W3, W2, sw1, sw3, sw2)

    def _L2_cond_ref(r, k, v, w, u, time_emb):
        import jax, jax.numpy as jnp
        from jax import lax
        import numpy as np
        B, T, C, TD = (8, 256, 256, 64)

        def _bi_wkv(r, k, v, w, u, time_emb):
            tf = jax.nn.sigmoid(jnp.sum(time_emb, axis=-1))[:, None, None]
            decay = jnp.exp(-jnp.exp(w.astype(jnp.float32)))[None, :] * (0.5 + 0.5 * tf[:, :, 0])
            kf = k.astype(jnp.float32)
            vf = v.astype(jnp.float32)
            ek = jnp.exp(jnp.minimum(kf, 30.0))
            ekv = ek * vf

            def step(carry, x):
                a, b = carry
                ekv_t, ek_t = x
                a = a * decay + ekv_t
                b = b * decay + ek_t
                return ((a, b), (a, b))
            ekv_t = jnp.swapaxes(ekv, 0, 1)
            ek_t = jnp.swapaxes(ek, 0, 1)
            init = (jnp.zeros_like(decay), jnp.zeros_like(decay))
            _, (nf, df) = lax.scan(step, init, (ekv_t, ek_t))
            _, (nb, db) = lax.scan(step, init, (ekv_t, ek_t), reverse=True)
            nf = jnp.swapaxes(nf, 0, 1)
            df = jnp.swapaxes(df, 0, 1)
            nb = jnp.swapaxes(nb, 0, 1)
            db = jnp.swapaxes(db, 0, 1)
            euk = jnp.exp(jnp.minimum(u.astype(jnp.float32)[None, None, :] + kf, 30.0))
            num = nf + nb - ekv + euk * vf
            den = df + db - ek + euk
            base = jax.nn.sigmoid(r.astype(jnp.float32)) * (num / jnp.maximum(den, 1e-08))
            out = base * (0.8 + 0.2 * tf)
            return out.astype(r.dtype)
        return _bi_wkv(r, k, v, w, u, time_emb)

    def _L2_ffn_ref(x, w_gate, w_up, w_down, up_reorder_index, down_reorder_index):
        import jax, jax.numpy as jnp
        import numpy as np
        FP8_MAX = 448.0
        GLOBAL_DIV = 448.0 * 6.0

        def _fp8(x):
            return x.astype(jnp.float8_e4m3fn).astype(jnp.float32)

        def _reorder_quantize_x(x, idx):
            scale = jnp.max(jnp.abs(x)) / GLOBAL_DIV
            xr = (x / scale)[:, idx]
            scale_x = jnp.max(jnp.abs(xr), axis=1, keepdims=True) / FP8_MAX
            qx = _fp8(xr / scale_x)
            return (qx, scale_x, scale)

        def _qlinear(qx, scale_x, scale, W, idx, out_idx=None):
            Wr = W[:, idx]
            w_scale = jnp.max(jnp.abs(Wr), axis=1, keepdims=True) / FP8_MAX
            qw = _fp8(Wr / w_scale)
            y = qx * scale_x @ (qw * w_scale).T * scale
            if out_idx is not None:
                y = y[:, out_idx]
            return y
        B, S, H = x.shape
        xf = x.reshape(B * S, H)
        qx, sx, sc = _reorder_quantize_x(xf, up_reorder_index)
        g = _qlinear(qx, sx, sc, w_gate, up_reorder_index, out_idx=down_reorder_index)
        u = _qlinear(qx, sx, sc, w_up, up_reorder_index, out_idx=down_reorder_index)
        t = jax.nn.silu(g) * u
        qt, st, sct = _reorder_quantize_x(t, down_reorder_index)
        y = _qlinear(qt, st, sct, w_down, down_reorder_index)
        return y.reshape(B, S, H)

    def _L3_cond_ref(r, k, v, w, u, time_emb):
        import jax, jax.numpy as jnp
        from jax import lax
        import numpy as np
        B, T, C, TD = (8, 256, 256, 64)

        def _bi_wkv(r, k, v, w, u, time_emb):
            tf = jax.nn.sigmoid(jnp.sum(time_emb, axis=-1))[:, None, None]
            decay = jnp.exp(-jnp.exp(w.astype(jnp.float32)))[None, :] * (0.5 + 0.5 * tf[:, :, 0])
            kf = k.astype(jnp.float32)
            vf = v.astype(jnp.float32)
            ek = jnp.exp(jnp.minimum(kf, 30.0))
            ekv = ek * vf

            def step(carry, x):
                a, b = carry
                ekv_t, ek_t = x
                a = a * decay + ekv_t
                b = b * decay + ek_t
                return ((a, b), (a, b))
            ekv_t = jnp.swapaxes(ekv, 0, 1)
            ek_t = jnp.swapaxes(ek, 0, 1)
            init = (jnp.zeros_like(decay), jnp.zeros_like(decay))
            _, (nf, df) = lax.scan(step, init, (ekv_t, ek_t))
            _, (nb, db) = lax.scan(step, init, (ekv_t, ek_t), reverse=True)
            nf = jnp.swapaxes(nf, 0, 1)
            df = jnp.swapaxes(df, 0, 1)
            nb = jnp.swapaxes(nb, 0, 1)
            db = jnp.swapaxes(db, 0, 1)
            euk = jnp.exp(jnp.minimum(u.astype(jnp.float32)[None, None, :] + kf, 30.0))
            num = nf + nb - ekv + euk * vf
            den = df + db - ek + euk
            base = jax.nn.sigmoid(r.astype(jnp.float32)) * (num / jnp.maximum(den, 1e-08))
            out = base * (0.8 + 0.2 * tf)
            return out.astype(r.dtype)
        return _bi_wkv(r, k, v, w, u, time_emb)

    def _L3_ffn_ref(x, gate_w, up_w, down_w):
        import jax, jax.numpy as jnp
        import numpy as np
        _FP8_MAX = 448.0
        _BLOCK = 32
        _EPS = 1e-30

        def _mx_dequant(t):
            rows, feat = t.shape
            blocks = t.reshape(rows, feat // _BLOCK, _BLOCK)
            max_abs = jnp.max(jnp.abs(blocks), axis=-1)
            scales = jnp.maximum(max_abs / _FP8_MAX, _EPS)
            q = (blocks / scales[..., None]).astype(jnp.float8_e4m3fn).astype(jnp.float32)
            return (q * scales[..., None]).reshape(rows, feat)

        def _mx_linear(x2d, w):
            return _mx_dequant(x2d) @ _mx_dequant(w).T
        B, S, H = x.shape
        x2d = x.reshape(B * S, H)
        gate = _mx_linear(x2d, gate_w)
        up = _mx_linear(x2d, up_w)
        h = jax.nn.silu(gate) * up
        out = _mx_linear(h, down_w)
        return out.reshape(B, S, H)
    x = x + _L0_ffn_ref(_L0_cond_ref(x, fside_BxSxS_0, fside_BxSxS_0, L0_cond_w, L0_cond_u, cond_512), L0_ffn_gate_w, L0_ffn_w1, L0_ffn_w2, L0_ffn_w3)
    x = x + _L1_ffn_ref(_L1_cond_ref(x, fside_BxSxS_0, fside_BxSxS_0, L1_cond_w, L1_cond_u, cond_512), L1_ffn_Wg, L1_ffn_W1, L1_ffn_W3, L1_ffn_W2, L1_ffn_sw1, L1_ffn_sw3, L1_ffn_sw2)
    x = x + _L2_ffn_ref(_L2_cond_ref(x, fside_BxSxS_0, fside_BxSxS_0, L2_cond_w, L2_cond_u, cond_512), L2_ffn_w_gate, L2_ffn_w_up, L2_ffn_w_down, L2_ffn_up_reorder_index, L2_ffn_down_reorder_index)
    x = x + _L3_ffn_ref(_L3_cond_ref(x, fside_BxSxS_0, fside_BxSxS_0, L3_cond_w, L3_cond_u, cond_512), L3_ffn_gate_w, L3_ffn_up_w, L3_ffn_down_w)
    return x

_drawn_inputs = setup_inputs


def setup_inputs(seed=0):
    import zlib

    import numpy as np

    out = dict(_drawn_inputs(seed))
    spreads = {}
    factors = {'cond_512': 4.987,
     'L0_cond_w': 8.0,
     'L0_cond_u': 8.0,
     'L0_ffn_gate_w': 7.973,
     'L0_ffn_w1': 7.572,
     'L0_ffn_w2': 7.442,
     'L0_ffn_w3': 7.478,
     'L1_ffn_Wg': 2.762,
     'L2_cond_w': 8.0,
     'L2_cond_u': 8.0,
     'L2_ffn_w_gate': 8.0,
     'L2_ffn_w_up': 8.0,
     'L2_ffn_w_down': 8.0,
     'L3_cond_w': 8.0,
     'L3_cond_u': 8.0,
     'L3_ffn_gate_w': 7.505,
     'L3_ffn_up_w': 7.6,
     'L3_ffn_down_w': 7.469}
    for name, (base, spread) in spreads.items():
        noise = np.random.default_rng([zlib.crc32(name.encode()), seed]).standard_normal(out[name].shape)
        drawn = base * np.exp(spread * noise) if base else spread * noise
        out[name] = jnp.asarray(drawn.astype(out[name].dtype))
    for name, factor in factors.items():
        out[name] = (out[name] * factor).astype(out[name].dtype)
    return out
```

```python
import concourse.bass as bass
from concourse import mybir
from contextlib import ExitStack

FP32 = mybir.dt.float32
BF16 = mybir.dt.bfloat16
I32 = mybir.dt.int32
U32 = mybir.dt.uint32
ALU = mybir.AluOpType
ACT = mybir.ActivationFunctionType
AX = mybir.AxisListType

P = 128
BATCH, TIME, CH = 4, 256, 256
TOK = BATCH * TIME
TILES = TOK // P
KT = CH // P
LAYERS = 4
E = 8
GROUPS = KT * BATCH
F0, F1, F2, F3 = 512, 352, 704, 1024
J0, J1, J2, J3 = 4, 3, 6, 8
CAP = TOK // E
T0 = (2 * TOK + E * (P - 1)) // P + 1
T1 = TILES + E
GU2 = 2 * F2 // P
W3 = 512
U3 = 3 * F3 * CH // (P * W3)
FP8_MAX = 448.0
EXPONENT = 0x7F800000
MIN_NORMAL = 2.0 ** -6
ROUND = 1.5 * 2.0 ** 20


def program(nc, x_in, side_in, cond_in, wu_in, gw0_in, w1_0_in, w3_0_in, w2_0_in, gw1_in, w1_1_in, w3_1_in,
            w2_1_in, gu2_in, down2_in, idx2_in, w3q_in, out):
    ctx = ExitStack()
    with ctx:
        def sb(name, shape, dt=FP32):
            return ctx.enter_context(nc.sbuf_tensor(name, shape, dt))

        def sem(name):
            return ctx.enter_context(nc.semaphore(name))

        slots0 = nc.dram_tensor("slots0", [T0 * P, CH], FP32, kind="Internal").ap()
        ys0 = nc.dram_tensor("ys0", [T0 * P, CH], FP32, kind="Internal").ap()
        slots1 = nc.dram_tensor("slots1", [2 * TOK, CH], FP32, kind="Internal").ap()
        ys1 = nc.dram_tensor("ys1", [TOK, CH], FP32, kind="Internal").ap()

        big = sb("big", [P, 24576])
        r3 = sb("r3", [P, 6144])
        x_tok = sb("x_tok", [P, TILES, CH])
        ratio = sb("ratio", [P, LAYERS * GROUPS, TIME])
        v_cb = sb("v_cb", [P, GROUPS, TIME])
        ek = sb("ek", [P, GROUPS, TIME])
        spare = sb("spare", [P, 2432])
        scan_in = spare[:, 0:2 * TIME].rearrange("p (i t) -> p i t", i=2)
        own = spare[:, 2 * TIME:3 * TIME]

        w1_0 = big[:, 0:8192].rearrange("p (k e f) -> p k e f", k=KT, e=E)
        w3_0 = big[:, 8192:16384].rearrange("p (k e f) -> p k e f", k=KT, e=E)
        w2_0 = big[:, 16384:24576].rearrange("p (k e f) -> p k e f", k=J0, e=E)
        NE1 = E + 1
        a1 = KT * NE1 * F1
        w1_1 = big[:, 0:a1].rearrange("p (k e f) -> p k e f", k=KT, e=NE1)
        w3_1 = big[:, a1:2 * a1].rearrange("p (k e f) -> p k e f", k=KT, e=NE1)
        w2_1 = big[:, 2 * a1:2 * a1 + J1 * NE1 * CH].rearrange("p (k e f) -> p k e f", k=J1, e=NE1)
        o2 = 2 * a1 + J1 * NE1 * CH
        gu2 = big[:, o2:o2 + KT * 2 * F2].rearrange("p (k f) -> p k f", k=KT)
        down2 = big[:, o2 + KT * 2 * F2:o2 + KT * 2 * F2 + J2 * CH].rearrange("p (k f) -> p k f", k=J2)
        gate3 = r3[:, 0:2048].rearrange("p (k f) -> p k f", k=KT)
        up3 = r3[:, 2048:4096].rearrange("p (k f) -> p k f", k=KT)
        down3 = r3[:, 4096:6144].rearrange("p (k f) -> p k f", k=J3)

        zeros = r3[:, 0:2048]
        c0 = r3[:, 2048:4096].rearrange("p (t c) -> p t c", t=TILES)
        sig0 = r3[:, 4096:6144].rearrange("p (t c) -> p t c", t=TILES)
        raw2 = r3[:, 0:GU2 * CH].rearrange("p (t c) -> p t c", t=GU2)
        rawd2 = r3[:, GU2 * CH:GU2 * CH + 2 * F2].rearrange("p (t c) -> p t c", t=2)
        c_tok = v_cb[:, :, :].rearrange("p g t -> p (g t)").rearrange("p (t c) -> p t c", t=TILES)
        sig = ek[:, :, :].rearrange("p g t -> p (g t)").rearrange("p (t c) -> p t c", t=TILES)
        raw3 = spare[:, 0:2 * W3].rearrange("p (i c) -> p i c", i=2)
        wt_a, wt_b = spare[:, 1024:1728], spare[:, 1728:2432]
        wq = sb("wq", [P, F2])

        xg = sb("xg", [P, CH])
        xgT = sb("xgT", [P, KT, P])
        both_b = sb("both_b", [P, 2 * F0])
        silu_b, h_b = both_b[:, 0:F0], both_b[:, F0:2 * F0]
        hT_b = sb("hT_b", [P, J0, P])
        y_b = sb("y_b", [P, CH])
        back_a, back_b = (x[:, :, :].rearrange("p g t -> p (g t)").rearrange("p (t c) -> p t c", t=TILES)
                          for x in (v_cb, ek))
        back1 = big[:, 0:2048].rearrange("p (t c) -> p t c", t=TILES)
        silu_w, h_w, q_a, q_b = (big[:, i * 1024:(i + 1) * 1024] for i in range(4))
        c_tile = big[:, 5120:5376]
        hT_w = big[:, 4096:5120].rearrange("p (j t) -> p j t", j=J3)

        acc = sb("acc", [P, 2, TIME])
        later = sb("later", [P, 2, TIME + 1])
        ones_row = spare[:, 3 * TIME:4 * TIME]
        rbuf = sb("rbuf", [P, TIME])
        cond = acc[:, 0, :].rearrange("p (b d) -> p b d", b=BATCH)
        wu = sb("wu", [P, 2, LAYERS, KT])
        tf = sb("tf", [P, 4, BATCH])
        tfo = sb("tfo", [P, GROUPS])
        dec = sb("dec", [P, LAYERS * KT])
        decay = sb("decay", [P, LAYERS * GROUPS])
        gw = [sb("gw0", [P, KT, E]), sb("gw1", [P, KT, E])]

        ident = sb("ident", [P, P])
        ones = sb("ones", [P, P], BF16)
        tri = sb("tri", [P, P], BF16)
        rev8 = sb("rev8", [P, E])
        e128 = sb("e128", [P, E])
        tile_no = sb("tile_no", [1, T0])
        tok_no = sb("tok_no", [P, TILES])
        row_no = sb("row_no", [P, GU2])
        idx2 = sb("idx2", [P, GU2], I32)
        idx2f = sb("idx2f", [P, GU2])
        one_hot = sb("one_hot", [P, TILES + 1, E], BF16)
        NR = 12
        rt = both_b[:, 0:NR * TILES * E].rearrange("p (n t e) -> p n t e", n=NR, t=TILES)
        rs = sb("rs", [P, 16, TILES])
        cnt = sb("cnt", [P, 4, E])
        cmpb = sb("cmpb", [P, E, TILES])
        cmpt = sb("cmpt", [1, T0, E])
        eid_f = sb("eid_f", [1, T0])
        eid = sb("eid", [1, T0], I32)
        slot_a = sb("slot_a", [P, TILES], I32)
        slot_b = sb("slot_b", [P, TILES], I32)
        slot_w1 = sb("slot_w1", [P, TILES], I32)
        slot_r1 = sb("slot_r1", [P, TILES], I32)
        qs = sb("qs", [P, 3, 32])

        psA = ctx.enter_context(nc.psum_tensor("psA", [P, 1024], FP32))
        psB = ctx.enter_context(nc.psum_tensor("psB", [P, 1024], FP32))
        psH = ctx.enter_context(nc.psum_tensor("psH", [P, 1024], FP32))
        psX = ctx.enter_context(nc.psum_tensor("psX", [P, KT, P], FP32))
        psY = ctx.enter_context(nc.psum_tensor("psY", [P, CH], FP32))
        psR = psA[:, 512:768]
        psW = psH[:, 512:1024].rearrange("p (k c) -> p k c", k=4)
        psS = psB[:, 512:576].rearrange("p (t e) -> p t e", t=TILES)
        psK = psB[:, 768:840].rearrange("p (t e) -> p t e", t=TILES + 1)

        ld_x, ld_side, ld_small, ld_gate, ld_w0, ld_w1, ld_idx2 = (sem(n) for n in (
            "x_loaded", "side_loaded", "small_loaded", "router_loaded", "w0_loaded", "w1_loaded", "idx2_loaded"))
        consts, zeros_set, zeros_put, ld_raw2, ld_rawd2 = (sem(n) for n in (
            "consts_set", "zeros_set", "slots_zeroed", "raw2_gathered", "raw_down2_loaded"))
        ld_raw3 = [sem("raw3_loaded_even"), sem("raw3_loaded_odd")]
        pool_step = sem("pool_step")
        dve_step = sem("dve_step")
        tf_sum, tf_exp, w_exp, dec_exp, ek_min, ek_exp, euk_min, euk_exp, sig_done = (sem(n) for n in (
            "tf_summed", "tf_exp", "w_exp", "decay_exp", "k_clamped", "ek_done", "euk_clamped",
            "euk_done", "sigmoid_done"))
        grp_made, grp_turned, grp_kept = sem("wkv_group_made"), sem("wkv_group_transposed"), sem("wkv_group_kept")
        c_made = sem("c_made")
        cT_turned, cT_kept = sem("cT_transposed"), sem("cT_kept")
        scored, logits_out, exps_in, exps_out, hot_set, ranked, routed = (sem(n) for n in (
            "scored", "scores_read", "exp_args_made", "exps_made", "one_hot_made", "ranked", "routed"))
        scattered0, scattered1 = sem("scattered0"), sem("scattered1")
        gathered, gather_used = [sem(f"gathered_{t}") for t in range(TILES)], sem("gathered_rows_used")
        scan_ready, own_ready, scanned, own_added, fwd_scanned = (sem(n) for n in (
            "wkv_scan_inputs_made", "wkv_own_terms_made", "wkv_scanned", "wkv_own_terms_added", "wkv_forward_scanned"))
        bwd_scanned = [scanned, sem("wkv_backward_scanned_k")]
        wq_made, wq_turned, wq_kept = sem("weights_quantised"), sem("weights_transposed"), sem("weights_kept")
        idx2_set = sem("idx2_set")
        out_put = sem("out_stored")

        class Stage:

            def __init__(self, name, up_read=None):
                self.x_in = sem(f"{name}_x_in")
                self.x_copied = sem(f"{name}_x_copied")
                self.xT_ps = sem(f"{name}_xT_ps")
                self.xT_sb = sem(f"{name}_xT_sb")
                self.gate_ps = sem(f"{name}_gate_ps")
                self.up_ps = sem(f"{name}_up_ps")
                self.silu_sb = sem(f"{name}_silu_sb")
                self.h_sb = sem(f"{name}_h_sb")
                self.hT_ps = sem(f"{name}_hT_ps")
                self.hT_sb = sem(f"{name}_hT_sb")
                self.y_ps = sem(f"{name}_y_ps")
                self.y_sb = sem(f"{name}_y_sb")
                self.y_out = sem(f"{name}_y_out")
                self.up_read = sem(f"{name}_up_read") if up_read else self.h_sb

        S0, S1, S2, S3 = Stage("l0"), Stage("l1"), Stage("l2", True), Stage("l3", True)

        class Steps:

            def __init__(self, engine, semaphore):
                self.engine, self.semaphore, self.base, self.n = engine, semaphore, 0, 0

            def link(self, instruction):
                self.n += 1
                instruction.then_inc(self.semaphore, 1)
                self.engine.wait_ge(self.semaphore, self.base + self.n)

            def enter(self, index, per):
                self.start, self.n0, self.per = self.base + self.n, self.n, per
                self.base, self.n = self.start + index * per, 0

            def leave(self, rounds):
                assert self.n == self.per, (self.n, self.per)
                self.base, self.n = self.start + rounds * self.per, 0

        def col(tile, i):
            return tile[:, bass.ds(i, 1)]

        def row(tile, i):
            return tile[:, bass.ds(i, 1), :].rearrange("p a t -> p (a t)")

        block = ctx.enter_context(nc.Block())

        @block.sync
        def _(sp):
            sp.dma_start(wu[:, :, :, :], wu_in).then_inc(ld_small, 16)
            sp.dma_start(cond, cond_in).then_inc(ld_small, 16)
            sp.dma_start(v_cb[:, :, :], side_in).then_inc(ld_side, 16)
            sp.dma_start(x_tok[:, :, :], x_in.rearrange("(t p) c -> p t c", p=P)).then_inc(ld_x, 16)
            sp.dma_start(gw[0][:, :, :], gw0_in).then_inc(ld_gate, 16)
            sp.dma_start(gw[1][:, :, :], gw1_in).then_inc(ld_gate, 16)
            sp.dma_start(idx2[:, :], idx2_in).then_inc(ld_idx2, 16)
            sp.wait_ge(zeros_set, 1)
            for i in range(T0 // TILES):
                sp.dma_start(slots0[i * TOK:(i + 1) * TOK, :].rearrange("(p r) c -> p (r c)", p=P), zeros)\
                  .then_inc(zeros_put, 16)
            sp.dma_start(slots1[0:TOK, :].rearrange("(p r) c -> p (r c)", p=P), zeros).then_inc(zeros_put, 16)
            for src, dst in ((w1_0_in, w1_0), (w3_0_in, w3_0), (w2_0_in, w2_0)):
                sp.dma_start(dst, src).then_inc(ld_w0, 16)

            def load_slots(S, slots, t, turned):
                if turned is not None:
                    sp.wait_ge(S.xT_ps, turned)
                sp.dma_start(xg[:, :], slots[bass.ds(t * P, P), :]).then_inc(S.x_in, 16)

            def store_results(S, ys, t, made):
                sp.wait_ge(S.y_sb, made)
                sp.dma_start(ys[bass.ds(t * P, P), :], y_b[:, :]).then_inc(S.y_out, 16)

            sp.wait_ge(scattered0, 16 * 2 * TILES)
            load_slots(S0, slots0, 0, None)
            load_slots(S0, slots0, 1, 1)
            with sp.Fori(0, T0 - 2) as t:
                load_slots(S0, slots0, t + 2, t + 2)
                store_results(S0, ys0, t, t + 1)
            for t in (T0 - 2, T0 - 1):
                store_results(S0, ys0, t, t + 1)

            for e0, e1 in ((0, 1), (1, 3), (3, 6), (6, 9)):
                for src, dst in ((w1_1_in, w1_1), (w3_1_in, w3_1), (w2_1_in, w2_1)):
                    sp.dma_start(dst[:, :, e0:e1, :], src[:, :, e0:e1, :]).then_inc(ld_w1, 16)
            sp.wait_ge(scattered1, 16 * TILES)
            load_slots(S1, slots1, 0, TILES)
            load_slots(S1, slots1, 1, TILES + 1)
            with sp.Fori(0, E - 2) as t:
                load_slots(S1, slots1, t + 2, t + TILES + 2)
                store_results(S1, ys1, t, t + TILES + 1)
            for t in (E - 2, E - 1):
                store_results(S1, ys1, t, t + TILES + 1)

            with sp.Fori(0, TILES) as t:
                sp.wait_ge(S3.y_sb, t + 1)
                sp.dma_start(out[bass.ds(t * P, P), :], x_tok[:, bass.ds(t, 1), :].rearrange("p a c -> p (a c)"))\
                  .then_inc(out_put, 16)
            sp.wait_ge(out_put, 16 * TILES)

        @block.gpsimd
        def _(pool):
            steps = Steps(pool, pool_step)
            pool.memset(zeros, 0.0).then_inc(zeros_set, 1)
            steps.link(pool.memset(ident[:, :], 0.0))
            steps.link(pool.memset(ones[:, :], 1.0))
            steps.link(pool.memset(ones_row, 1.0))
            pool.memset(one_hot[:, :, :], 0.0).then_inc(consts, 1)
            pool.memset(later[:, :, TIME:TIME + 1], 0.0).then_inc(consts, 1)
            pool.affine_select(out=ident[:, :], in_=ident[:, :], compare_op=ALU.not_equal, fill=1.0, base=0,
                               pattern=[[-1, P]], channel_multiplier=1).then_inc(consts, 1)
            pool.affine_select(out=tri[:, :], in_=ones[:, :], compare_op=ALU.is_ge, fill=0.0, base=-1,
                               pattern=[[1, P]], channel_multiplier=-1).then_inc(consts, 1)
            for tile, base, pattern, mult in (
                    (rev8[:, :], E, [[-1, E]], 0), (e128[:, :], 0, [[P, E]], 0), (tile_no[:, :], 0, [[1, T0]], 0),
                    (tok_no[:, :], TOK, [[P, TILES]], 1), (row_no[:, :], 0, [[P, GU2]], 1)):
                pool.iota(tile, pattern=pattern, base=base, channel_multiplier=mult,
                          allow_small_or_imprecise_dtypes=True).then_inc(consts, 1)

            def wkv_inputs(j, g, first=False):
                if not first:
                    pool.wait_ge(bwd_scanned[1], j)
                pool.tensor_tensor(scan_in[:, 0, :], row(ek, g), row(v_cb, g), ALU.mult).then_inc(scan_ready, 1)
                pool.tensor_tensor(scan_in[:, 1, :], row(ek, g), ones_row, ALU.mult).then_inc(scan_ready, 1)
                if not first:
                    pool.wait_ge(own_added, j)
                pool.tensor_tensor(own, row(ratio, j), row(v_cb, g), ALU.mult).then_inc(own_ready, 1)

            def gather2(r):
                pool.indirect_dma_start(
                    out=raw2[:, r, :], out_offset=None, in_=gu2_in,
                    in_offset=bass.IndirectOffsetOnAxis(ap=idx2[:, r:r + 1].bitcast(U32), axis=0)).then_inc(ld_raw2, 16)

            pool.wait_ge(ek_exp, 1)
            pool.wait_ge(euk_exp, KT)
            wkv_inputs(0, 0, first=True)
            with pool.Fori(1, GROUPS) as g:
                wkv_inputs(g, g)
            pool.wait_ge(zeros_put, 16 * (T0 // TILES + 1))
            pool.wait_ge(routed, 1)
            for t in range(TILES):
                for slot in (slot_a, slot_b):
                    pool.indirect_dma_start(
                        out=slots0, out_offset=bass.IndirectOffsetOnAxis(ap=slot[:, t:t + 1].bitcast(U32), axis=0),
                        in_=c0[:, t, :], in_offset=None).then_inc(scattered0, 16)
            pool.wait_ge(euk_exp, LAYERS * KT)
            for g in range(GROUPS):
                wkv_inputs(GROUPS + g, g)
                if g == 0:
                    pool.wait_ge(scattered0, 16 * 2 * TILES)
                    pool.wait_ge(idx2_set, 1)
                gather2(g)
            for r in range(GROUPS, GU2):
                gather2(r)
            pool.dma_start(rawd2, down2_in).then_inc(ld_rawd2, 16)
            for layer in (2, 3):
                with pool.Fori(0, GROUPS) as g:
                    wkv_inputs(layer * GROUPS + g, g)
            pool.wait_ge(S0.y_out, 16 * T0)
            pool.wait_ge(grp_made, LAYERS * GROUPS)
            pool.wait_ge(own_ready, LAYERS * GROUPS)
            for t in range(TILES):
                for rows, slot in ((back_a, slot_a), (back_b, slot_b)):
                    pool.indirect_dma_start(
                        out=rows[:, t, :], out_offset=None, in_=ys0,
                        in_offset=bass.IndirectOffsetOnAxis(ap=slot[:, t:t + 1].bitcast(U32), axis=0))\
                        .then_inc(gathered[t], 16)
            pool.wait_ge(routed, 2)
            for t in range(TILES):
                pool.indirect_dma_start(
                    out=slots1, out_offset=bass.IndirectOffsetOnAxis(ap=slot_w1[:, t:t + 1].bitcast(U32), axis=0),
                    in_=c_tok[:, t, :], in_offset=None).then_inc(scattered1, 16)
            def load_unit3(u, i, quantised):
                pool.wait_ge(wq_made, quantised)
                pool.dma_start(raw3[:, i, :], w3q_in[bass.ds(u, 1), :, :].rearrange("a p c -> (a p) c"))\
                    .then_inc(ld_raw3[i], 16)

            for i in range(2):
                load_unit3(i, i, GU2 + 2)
            with pool.Fori(1, U3 // 2) as pair:
                for i in range(2):
                    load_unit3(2 * pair + i, i, GU2 + 2 + 2 * pair + i - 1)
            pool.wait_ge(S1.y_out, 16 * E)
            for t in range(TILES):
                pool.indirect_dma_start(
                    out=back1[:, t, :], out_offset=None, in_=ys1,
                    in_offset=bass.IndirectOffsetOnAxis(ap=slot_r1[:, t:t + 1].bitcast(U32), axis=0))\
                    .then_inc(gathered[t], 16)

        @block.tensor
        def _(pe):
            def turn(dst, src, rows=P):
                return pe.transpose(dst, src, ident[0:rows, 0:rows])

            def turn_group(j):
                pe.wait_ge(grp_made, j + 1)
                pe.wait_ge(grp_kept, j)
                for h in range(2):
                    mm = turn(psR[:, h * P:(h + 1) * P], rbuf[:, h * P:(h + 1) * P])
                mm.then_inc(grp_turned, 1)

            def turn_weights(n, pieces):
                pe.wait_ge(wq_made, n + 1)
                pe.wait_ge(wq_kept, n)
                for k, cols in enumerate(pieces):
                    mm = turn(psW[0:cols, k, :], wq[:, k * P:k * P + cols])
                mm.then_inc(wq_turned, 1)

            def turn_weights_first(pieces):
                pe.wait_ge(wq_made, 1)
                for k, cols in enumerate(pieces):
                    mm = turn(psW[0:cols, k, :], wq[:, k * P:k * P + cols])
                mm.then_inc(wq_turned, 1)

            def score(layer, c):
                cT = ratio[:, layer * GROUPS:(layer + 1) * GROUPS, :].rearrange("p g t -> p (g t)")\
                    .rearrange("p (k n) -> p k n", k=KT)
                pe.wait_ge(c_made, layer + 1)
                banks = ((psA, 0), (psB, 0), (psH, 0), (psH, 512))
                for i, (ps, o) in enumerate(banks):
                    for t in range(4):
                        mm = turn(ps[:, o + t * P:o + (t + 1) * P],
                                  c[:, (i % 2) * 4 + t, (i // 2) * P:(i // 2 + 1) * P])
                    mm.then_inc(cT_turned, 1)
                pe.wait_ge(cT_kept, 4 * (layer + 1))
                for t in range(TILES):
                    for k in range(KT):
                        mm = pe.matmul(psS[:, t, :], cT[:, k, t * P:(t + 1) * P], gw[layer][:, k, :],
                                       start=(k == 0), stop=(k == KT - 1))
                mm.then_inc(scored, 1)

            def rank(layer):
                pe.wait_ge(hot_set, layer + 1)
                mm = pe.matmul(psK[:, :, :], tri[:, :], one_hot[:, :, :], start=True, stop=False)
                for i in range(TILES):
                    n = TILES - i
                    mm = pe.matmul(psK[:, i + 1:TILES + 1, :], ones[:, :],
                                   one_hot[:, i:i + 1, :].to_broadcast([P, n, E]), start=False, stop=(i == TILES - 1))
                mm.then_inc(ranked, 1)

            def x_turn(S, t, ready, first=False):
                ready(t)
                if not first:
                    pe.wait_ge(S.xT_sb, t)
                for k in range(KT):
                    mm = turn(psX[:, k, :], xg[:, k * P:(k + 1) * P])
                mm.then_inc(S.xT_ps, 1)

            def in_product(S, ps, F, weights, done):
                for c in range(0, F, 512):
                    n = min(512, F - c)
                    for k in range(KT):
                        mm = pe.matmul(ps[:, c:c + n], xgT[:, k, :], weights(k, c, n), start=(k == 0), stop=(k == KT - 1))
                mm.then_inc(done, 1)

            def gate_up(S, t, F, wg, wu_, first=False):
                pe.wait_ge(S.xT_sb, t + 1)
                if not first:
                    pe.wait_ge(S.silu_sb, t)
                in_product(S, psA, F, wg, S.gate_ps)
                if not first:
                    pe.wait_ge(S.up_read, t)
                in_product(S, psB, F, wu_, S.up_ps)

            def h_turn(S, t, h, F, first=False):
                pe.wait_ge(S.h_sb, t + 1)
                if not first:
                    pe.wait_ge(S.hT_sb, t)
                for j in range((F + P - 1) // P):
                    n = min(P, F - j * P)
                    mm = turn(psH[0:n, j * P:(j + 1) * P], h[:, j * P:j * P + n])
                mm.then_inc(S.hT_ps, 1)

            def down(S, t, hT, F, wd, first=False):
                pe.wait_ge(S.hT_sb, t + 1)
                if not first:
                    pe.wait_ge(S.y_sb, t)
                J = (F + P - 1) // P
                for j in range(J):
                    n = min(P, F - j * P)
                    mm = pe.matmul(psY[:, :], hT[0:n, j, :], wd(j, n), start=(j == 0), stop=(j == J - 1))
                mm.then_inc(S.y_ps, 1)

            pe.wait_ge(consts, 9)
            pe.wait_ge(grp_made, 1)
            for h in range(2):
                mm = turn(psR[:, h * P:(h + 1) * P], rbuf[:, h * P:(h + 1) * P])
            mm.then_inc(grp_turned, 1)
            with pe.Fori(1, GROUPS) as j:
                turn_group(j)
            pe.wait_ge(ld_gate, 32)
            score(0, c0)
            rank(0)

            def slots_in(S):
                return lambda t: pe.wait_ge(S.x_in, 16 * t + 16)

            def w0(t):
                e = pe.value_load(eid[0:1, bass.ds(t, 1)], min_val=0, max_val=E - 1)
                return [lambda k, c, n, w=w: w[:, k, bass.ds(e, 1), c:c + n].rearrange("p a f -> p (a f)")
                        for w in (w1_0, w3_0)]

            def wd0(t):
                e = pe.value_load(eid[0:1, bass.ds(t, 1)], min_val=0, max_val=E - 1)
                return lambda j, n: w2_0[0:n, j, bass.ds(e, 1), :].rearrange("p a f -> p (a f)")

            pe.wait_ge(ld_w0, 48)
            pe.wait_ge(routed, 1)
            x_turn(S0, 0, slots_in(S0), first=True)
            gate_up(S0, 0, F0, *w0(0), first=True)
            x_turn(S0, 1, slots_in(S0))

            def step0(t, first=False, last=False):
                h_turn(S0, t - 1, h_b, F0, first=first)
                gate_up(S0, t, F0, *w0(t))
                turn_group(t + GROUPS - 1)
                if not last:
                    x_turn(S0, t + 1, slots_in(S0))
                down(S0, t - 1, hT_b, F0, wd0(t - 1), first=first)

            step0(1, first=True)
            with pe.Fori(2, T0 - 1) as t:
                step0(t)
            step0(T0 - 1, last=True)
            h_turn(S0, T0 - 1, h_b, F0)
            turn_group(LAYERS * GROUPS - 1)
            down(S0, T0 - 1, hT_b, F0, wd0(T0 - 1))

            turn_weights_first([P, P])
            with pe.Fori(1, GU2) as n:
                turn_weights(n, [P, P])
            for r in range(2):
                for i in range(J2 // 2):
                    n = GU2 + r * J2 // 2 + i
                    pe.wait_ge(wq_made, GU2 + r + 1)
                    pe.wait_ge(wq_kept, n)
                    for k in range(2):
                        j = 2 * i + k
                        cols = min(P, F2 - j * P)
                        mm = turn(psW[0:cols, k, :], wq[:, j * P:j * P + cols])
                    mm.then_inc(wq_turned, 1)
            N2 = GU2 + J2
            M2 = GU2 + 2

            score(1, c_tok)
            rank(1)

            def turn_unit3(u):
                pe.wait_ge(wq_made, M2 + u + 1)
                pe.wait_ge(wq_kept, N2 + u)
                for k in range(4):
                    mm = turn(psW[:, k, :], wq[:, k * P:(k + 1) * P])
                mm.then_inc(wq_turned, 1)

            def copied(t):
                pe.wait_ge(S1.x_copied, t + 1)

            def w1e(e):
                return [lambda k, c, n, w=w: w[:, k, bass.ds(e, 1), c:c + n].rearrange("p a f -> p (a f)")
                        for w in (w1_1, w3_1)]

            def wd1(e):
                return lambda j, n: w2_1[0:n, j, bass.ds(e, 1), :].rearrange("p a f -> p (a f)")

            def slot_tile(t):
                pe.wait_ge(S1.x_in, (t - TILES) * 16 + 16)

            pe.wait_ge(ld_w1, 16 * 3 * 4)
            x_turn(S1, 0, copied, first=True)
            gate_up(S1, 0, F1, *w1e(0), first=True)
            x_turn(S1, 1, copied)

            def step1(t, e_in, e_down, ready, unit=None, first=False, last=False):
                h_turn(S1, t - 1, h_b, F1, first=first)
                gate_up(S1, t, F1, *w1e(e_in))
                if unit is not None:
                    turn_unit3(unit)
                if not last:
                    x_turn(S1, t + 1, ready)
                down(S1, t - 1, hT_b, F1, wd1(e_down), first=first)

            step1(1, 0, 0, copied, 0, first=True)
            with pe.Fori(2, TILES - 1) as t:
                step1(t, 0, 0, copied, t - 1)
            step1(TILES - 1, 0, 0, slot_tile, TILES - 2)
            with pe.Fori(TILES, U3 + 1) as t:
                step1(t, t - TILES + 1, t - TILES, slot_tile, t - 1)
            with pe.Fori(U3 + 1, T1 - 1) as t:
                step1(t, t - TILES + 1, t - TILES, slot_tile)
            step1(T1 - 1, E, E - 1, slot_tile, last=True)
            h_turn(S1, T1 - 1, h_b, F1)
            down(S1, T1 - 1, hT_b, F1, wd1(E))

            for S, F, wg, wu_, wd in (
                    (S2, F2, lambda k, c, n: gu2[:, k, c:c + n], lambda k, c, n: gu2[:, k, F2 + c:F2 + c + n],
                     lambda j, n: down2[0:n, j, :]),
                    (S3, F3, lambda k, c, n: gate3[:, k, c:c + n], lambda k, c, n: up3[:, k, c:c + n],
                     lambda j, n: down3[0:n, j, :])):
                def tile_ready(t):
                    pe.wait_ge(S.x_copied, t + 1)

                def step(t, first=False, last=False):
                    gate_up(S, t, F, wg, wu_)
                    if not last:
                        x_turn(S, t + 1, tile_ready)
                    h_turn(S, t - 1, h_w, F, first=first)
                    down(S, t - 1, hT_w, F, wd, first=first)

                x_turn(S, 0, tile_ready, first=True)
                gate_up(S, 0, F, wg, wu_, first=True)
                x_turn(S, 1, tile_ready)
                step(1, first=True)
                with pe.Fori(2, TILES - 1) as t:
                    step(t)
                step(TILES - 1, last=True)
                h_turn(S, TILES - 1, h_w, F)
                down(S, TILES - 1, hT_w, F, wd)

        @block.scalar
        def _(act):
            def keep_group(j):
                act.wait_ge(grp_turned, j + 1)
                act.activation(ratio[:, bass.ds(j, 1), :].rearrange("p a t -> p (a t)"), psR, ACT.Copy)\
                   .then_inc(grp_kept, 1)

            def keep_cT(layer):
                cT = ratio[:, layer * GROUPS:(layer + 1) * GROUPS, :].rearrange("p g t -> p (g t)")
                for i, (ps, o) in enumerate(((psA, 0), (psB, 0), (psH, 0), (psH, 512))):
                    act.wait_ge(cT_turned, 4 * layer + i + 1)
                    act.activation(cT[:, i * 512:(i + 1) * 512], ps[:, o:o + 512], ACT.Copy).then_inc(cT_kept, 1)

            def keep_xT(S, t, first=False):
                act.wait_ge(S.xT_ps, t + 1)
                if not first:
                    act.wait_ge(S.up_ps, t)
                act.activation(xgT[:, :, :], psX[:, :, :], ACT.Copy).then_inc(S.xT_sb, 1)

            def silu(S, t, dst, F, first=False):
                act.wait_ge(S.gate_ps, t + 1)
                if not first:
                    act.wait_ge(S.up_read, t)
                act.activation(dst[:, 0:F], psA[:, 0:F], ACT.Silu).then_inc(S.silu_sb, 1)

            def keep_hT(S, t, hT, F, first=False):
                act.wait_ge(S.hT_ps, t + 1)
                if not first:
                    act.wait_ge(S.y_ps, t)
                full, rest = F // P, F % P
                done = act.activation(hT[:, 0:full, :].rearrange("p j t -> p (j t)"), psH[:, 0:full * P], ACT.Copy)
                if rest:
                    done = act.activation(hT[0:rest, full, :], psH[0:rest, full * P:(full + 1) * P], ACT.Copy)
                done.then_inc(S.hT_sb, 1)

            act.wait_ge(tf_sum, 1)
            act.activation(tf[:, 1, :], tf[:, 0, :], ACT.Exp, scale=-1.0).then_inc(tf_exp, 1)
            act.activation(wu[:, 0, :, :], wu[:, 0, :, :], ACT.Exp).then_inc(w_exp, 1)
            act.wait_ge(w_exp, 1)
            act.activation(dec[:, :], wu[:, 0, :, :].rearrange("p l k -> p (l k)"), ACT.Exp, scale=-1.0)\
               .then_inc(dec_exp, 1)
            act.wait_ge(ek_min, 1)
            act.activation(ek[:, :, :], ek[:, :, :], ACT.Exp).then_inc(ek_exp, 1)
            for i in range(LAYERS * KT):
                act.wait_ge(euk_min, i + 1)
                part = ratio[:, i * BATCH:(i + 1) * BATCH, :]
                act.activation(part, part, ACT.Exp).then_inc(euk_exp, 1)
            act.wait_ge(ld_x, 16)
            act.activation(sig0[:, :, :], x_tok[:, :, :], ACT.Sigmoid).then_inc(sig_done, 1)
            with act.Fori(0, GROUPS) as j:
                keep_group(j)
            keep_cT(0)
            act.wait_ge(exps_in, 1)
            act.activation(rt[:, 10:12, :, :], rt[:, 8:10, :, :], ACT.Exp, scale=-1.0).then_inc(exps_out, 1)

            keep_xT(S0, 0, first=True)
            silu(S0, 0, silu_b, F0, first=True)
            keep_xT(S0, 1)

            def step0(t, first=False, last=False):
                keep_hT(S0, t - 1, hT_b, F0, first=first)
                silu(S0, t, silu_b, F0)
                keep_group(t + GROUPS - 1)
                if not last:
                    keep_xT(S0, t + 1)

            step0(1, first=True)
            with act.Fori(2, T0 - 1) as t:
                step0(t)
            step0(T0 - 1, last=True)
            keep_hT(S0, T0 - 1, hT_b, F0)
            keep_group(LAYERS * GROUPS - 1)

            with act.Fori(0, GU2) as n:
                act.wait_ge(wq_turned, n + 1)
                act.activation(gu2[:, :, bass.ds(n * P, P)], psW[:, 0:KT, :], ACT.Copy).then_inc(wq_kept, 1)
            for r in range(2):
                for i in range(J2 // 2):
                    act.wait_ge(wq_turned, GU2 + r * J2 // 2 + i + 1)
                    if 2 * i + 2 < J2:
                        done = act.activation(down2[:, 2 * i:2 * i + 2, r * P:(r + 1) * P], psW[:, 0:2, :], ACT.Copy)
                    else:
                        act.activation(down2[:, 2 * i, r * P:(r + 1) * P], psW[:, 0, :], ACT.Copy)
                        done = act.activation(down2[0:F2 % P, 2 * i + 1, r * P:(r + 1) * P], psW[0:F2 % P, 1, :],
                                              ACT.Copy)
                    done.then_inc(wq_kept, 1)

            def sigmoid_x(t, semaphore, n):
                act.wait_ge(semaphore, n)
                act.activation(sig[:, t, :], x_tok[:, t, :], ACT.Sigmoid).then_inc(sig_done, 1)

            for t in range(TILES):
                sigmoid_x(t, gather_used, t + 1)
            keep_cT(1)
            act.wait_ge(exps_in, 2)
            act.activation(rt[:, 10, :, :], rt[:, 8, :, :], ACT.Exp, scale=-1.0).then_inc(exps_out, 1)
            N2 = GU2 + J2

            def keep_gu3(i):
                act.wait_ge(wq_turned, N2 + i + 1)
                act.activation(r3[:, 0:4096].rearrange("p (m f) -> p m f", f=F3)[:, :, bass.ds(i * P, P)], psW[:, :, :],
                               ACT.Copy).then_inc(wq_kept, 1)

            def keep_down3(r, c):
                act.wait_ge(wq_turned, N2 + TILES + 2 * r + c + 1)
                act.activation(down3[:, 4 * c:4 * c + 4, r * P:(r + 1) * P], psW[:, :, :], ACT.Copy).then_inc(wq_kept, 1)

            keep_xT(S1, 0, first=True)
            silu(S1, 0, silu_b, F1, first=True)
            keep_xT(S1, 1)

            def step1(t, unit=None, first=False, last=False):
                keep_hT(S1, t - 1, hT_b, F1, first=first)
                silu(S1, t, silu_b, F1)
                if unit:
                    unit()
                if not last:
                    keep_xT(S1, t + 1)

            step1(1, lambda: keep_gu3(0), first=True)
            with act.Fori(2, TILES + 1) as t:
                step1(t, lambda: keep_gu3(t - 1))
            for t in range(TILES + 1, U3 + 1):
                step1(t, lambda: keep_down3((t - 1 - TILES) // 2, (t - 1 - TILES) % 2))
            with act.Fori(U3 + 1, T1 - 1) as t:
                step1(t)
            step1(T1 - 1, last=True)
            keep_hT(S1, T1 - 1, hT_b, F1)

            for S, F, before, n in ((S2, F2, gather_used, TILES), (S3, F3, S2.y_sb, 0)):
                for t in range(TILES):
                    sigmoid_x(t, before, n + t + 1)
                keep_xT(S, 0, first=True)
                silu(S, 0, silu_w, F, first=True)
                keep_xT(S, 1)

                def step(t, first=False, last=False):
                    silu(S, t, silu_w, F)
                    if not last:
                        keep_xT(S, t + 1)
                    keep_hT(S, t - 1, hT_w, F, first=first)

                step(1, first=True)
                with act.Fori(2, TILES - 1) as t:
                    step(t)
                step(TILES - 1, last=True)
                keep_hT(S, TILES - 1, hT_w, F)

        @block.vector
        def _(dve):
            steps = Steps(dve, dve_step)
            link = steps.link
            tt, ts, stt = dve.tensor_tensor, dve.tensor_scalar, dve.scalar_tensor_tensor

            def wkv_group(j, g, first=False):
                d = col(decay, j)
                d_all = d.to_broadcast([P, TIME])
                if not first:
                    dve.wait_ge(grp_made, j)
                for i in range(2):
                    dve.wait_ge(scan_ready, 2 * j + i + 1)
                    dve.tensor_tensor_scan(acc[:, i, :], d_all, scan_in[:, i, :], 0.0, ALU.mult, ALU.add)\
                        .then_inc(fwd_scanned, 1)
                    dve.tensor_tensor_scan(later[:, i, TIME - 1::-1], d_all, scan_in[:, i, TIME - 1::-1], 0.0,
                                           ALU.mult, ALU.add).then_inc(bwd_scanned[i], 1)
                dve.wait_ge(fwd_scanned, 2 * j + 2)
                dve.wait_ge(bwd_scanned[0], j + 1)
                dve.wait_ge(bwd_scanned[1], j + 1)
                link(stt(acc[:, :, :], later[:, :, 1:TIME + 1], d, acc[:, :, :], ALU.mult, ALU.add))
                dve.wait_ge(own_ready, j + 1)
                link(tt(acc[:, 1, :], acc[:, 1, :], row(ratio, j), ALU.add))
                tt(acc[:, 0, :], acc[:, 0, :], own, ALU.add).then_inc(own_added, 1)
                link(ts(acc[:, 1, :], acc[:, 1, :], 1e-8, None, ALU.max))
                link(dve.reciprocal(acc[:, 1, :], acc[:, 1, :]))
                dve.wait_ge(own_added, j + 1)
                if not first:
                    dve.wait_ge(grp_turned, j)
                stt(rbuf[:, :], acc[:, 0, :], col(tfo, g), acc[:, 1, :], ALU.mult, ALU.mult).then_inc(grp_made, 1)

            WKV_STEPS = 4

            def ratio_of(layer):
                return ratio[:, layer * GROUPS:(layer + 1) * GROUPS, :].rearrange("p g t -> p (g t)")\
                    .rearrange("p (k t c) -> p t k c", k=KT, t=TILES)

            def make_c(layer, c, sg, sigmoids):
                dve.wait_ge(sig_done, sigmoids)
                dve.wait_ge(grp_kept, GROUPS * (layer + 1))
                s4 = sg.rearrange("p t (k c) -> p t k c", k=KT)
                c4 = c.rearrange("p t (k c) -> p t k c", k=KT)
                link(tt(c4[:, :, 0, :], s4[:, :, 0, :], ratio_of(layer)[:, :, 0, :], ALU.mult))
                return tt(c4[:, :, 1, :], s4[:, :, 1, :], ratio_of(layer)[:, :, 1, :], ALU.mult)

            R = [rt[:, i, :, :] for i in range(NR)]
            V = [rs[:, i, :] for i in range(16)]

            def over_e(vec):
                return vec.rearrange("p (t o) -> p t o", o=1).to_broadcast([P, TILES, E])

            def over_t(vec):
                return vec.rearrange("p (o e) -> p o e", o=1).to_broadcast([P, TILES, E])

            def reduce_e(dst, src, op):
                link(dve.tensor_reduce(out=dst, in_=src, axis=AX.X, op=op))

            def first_max(score, top, hot, tmp):
                reduce_e(top, score, ALU.max)
                link(tt(tmp, score, over_e(top), ALU.is_equal))
                link(tt(tmp, tmp, over_t(rev8[:, :]), ALU.mult))
                reduce_e(V[15], tmp, ALU.max)
                link(tt(hot, tmp, over_e(V[15]), ALU.is_equal))

            def route0():
                s, hot1, hot2, tmp, ab, s_rest, keep1, keep2 = R[0:8]
                dve.wait_ge(scored, 1)
                link(dve.tensor_copy(s, psS[:, :, :]))
                first_max(s, V[0], hot1, tmp)
                link(stt(s_rest, hot1, -1e30, s, ALU.mult, ALU.add))
                first_max(s_rest, V[1], hot2, tmp)
                dve.wait_ge(consts, 9)
                tt(one_hot[:, 0:TILES, :], hot1, hot2, ALU.add).then_inc(hot_set, 1)
                link(stt(ab, s, -1.0, s, ALU.mult, ALU.max))
                for top, keep, diff in ((V[0], keep1, R[8]), (V[1], keep2, R[9])):
                    link(tt(diff, over_e(top), s, ALU.subtract))
                    link(tt(tmp, ab, over_e(top), ALU.max))
                    link(ts(tmp, tmp, 0.02, None, ALU.mult))
                    link(tt(keep, diff, tmp, ALU.is_le))
                link(ts(R[9], R[9], 0.0, None, ALU.max))
                link(ts(tmp, hot1, -1.0, 1.0, ALU.mult, ALU.add))
                tt(keep2, keep2, tmp, ALU.mult).then_inc(exps_in, 1)
                dve.wait_ge(exps_in, 1)
                dve.wait_ge(exps_out, 1)
                for keep, ex, m in ((keep1, R[10], V[2]), (keep2, R[11], V[3])):
                    link(tt(ex, ex, keep, ALU.mult))
                    reduce_e(m, ex, ALU.add)
                    link(dve.reciprocal(m, m))
                dve.wait_ge(ranked, 1)
                link(dve.tensor_copy(cnt[:, 0, :], psK[:, TILES, :]))
                link(tt(cmpb[:, :, :], cnt[:, 0, :].rearrange("p (e o) -> p e o", o=1).to_broadcast([P, E, TILES]),
                        e128[:, :].rearrange("p (o t) -> p o t", o=1).to_broadcast([P, E, TILES]), ALU.is_gt))
                link(dve.tensor_reduce(out=cnt[:, 1, :], in_=cmpb[:, :, :], axis=AX.X, op=ALU.add))
                link(dve.memset(cnt[:, 3, :], 1.0))
                link(dve.tensor_tensor_scan(cnt[:, 2, :], cnt[:, 3, :], cnt[:, 1, :], 0.0, ALU.mult, ALU.add))
                link(tt(cnt[:, 3, :], cnt[:, 2, :], cnt[:, 1, :], ALU.subtract))
                link(ts(cnt[:, 3, :], cnt[:, 3, :], float(P), None, ALU.mult))
                link(tt(tmp, psK[:, 0:TILES, :], over_t(cnt[:, 3, :]), ALU.add))
                for hot, v, slot in ((hot1, V[4], slot_a), (hot2, V[5], slot_b)):
                    link(tt(ab, hot, tmp, ALU.mult))
                    reduce_e(v, ab, ALU.add)
                    link(dve.tensor_copy(slot[:, :], v))
                link(tt(cmpt[:, :, :], cnt[0:1, 2, :].rearrange("p (o e) -> p o e", o=1).to_broadcast([1, T0, E]),
                        tile_no[:, :].rearrange("p (t o) -> p t o", o=1).to_broadcast([1, T0, E]), ALU.is_le))
                link(dve.tensor_reduce(out=eid_f[:, :], in_=cmpt[:, :, :], axis=AX.X, op=ALU.add))
                link(ts(eid_f[:, :], eid_f[:, :], float(E - 1), None, ALU.min))
                dve.tensor_copy(eid[:, :], eid_f[:, :]).then_inc(routed, 1)

            def route1():
                s, hot1, _, tmp, ab = R[0:5]
                dve.wait_ge(scored, 2)
                link(dve.tensor_copy(s, psS[:, :, :]))
                first_max(s, V[6], hot1, tmp)
                dve.tensor_copy(one_hot[:, 0:TILES, :], hot1).then_inc(hot_set, 1)
                tt(R[8], over_e(V[6]), s, ALU.subtract).then_inc(exps_in, 1)
                dve.wait_ge(exps_out, 2)
                reduce_e(V[7], R[10], ALU.add)
                link(dve.reciprocal(V[7], V[7]))
                dve.wait_ge(ranked, 2)
                link(tt(ab, hot1, psK[:, 0:TILES, :], ALU.mult))
                reduce_e(V[8], ab, ALU.add)
                link(tt(ab, hot1, over_t(e128[:, :]), ALU.mult))
                reduce_e(V[9], ab, ALU.add)
                link(ts(V[10], V[8], float(CAP), None, ALU.is_lt))
                link(tt(V[7], V[7], V[10], ALU.mult))
                link(tt(V[11], V[8], V[9], ALU.add))
                link(tt(V[11], V[11], V[10], ALU.mult))
                link(ts(V[12], V[10], -1.0, 1.0, ALU.mult, ALU.add))
                link(tt(V[13], V[12], tok_no[:, :], ALU.mult))
                link(tt(V[13], V[13], V[11], ALU.add))
                link(dve.tensor_copy(slot_w1[:, :], V[13]))
                link(stt(V[14], V[12], float(TOK - 1), V[11], ALU.mult, ALU.add))
                dve.tensor_copy(slot_r1[:, :], V[14]).then_inc(routed, 1)

            def fp8_round(b, a):
                link(ts(a.bitcast(U32), b.bitcast(U32), EXPONENT, None, ALU.bitwise_and))
                link(ts(a, a, MIN_NORMAL, ROUND, ALU.max, ALU.mult))
                link(tt(b, b, a, ALU.add))
                link(tt(b, b, a, ALU.subtract))

            def quant_rows(dst, src, a, b, free):
                link(dve.tensor_reduce(out=qs[:, 0, 0:1], in_=src, axis=AX.X, op=ALU.max, apply_absolute_value=True))
                link(ts(qs[:, 1, 0:1], qs[:, 0, 0:1], 1.0 / FP8_MAX, None, ALU.mult))
                link(dve.reciprocal(qs[:, 2, 0:1], qs[:, 1, 0:1]))
                link(ts(b, src, qs[:, 2, 0:1], None, ALU.mult))
                fp8_round(b, a)
                free()
                return ts(dst, b, qs[:, 1, 0:1], None, ALU.mult)

            QUANT_STEPS = 8

            def quant_blocks(dst, src, a, b, free):
                nb = src.shape[-1] // 32

                def blocks(x):
                    return x.rearrange("p (b c) -> p b c", c=32)

                def per_block(i):
                    return qs[:, i, 0:nb].rearrange("p (b o) -> p b o", o=1).to_broadcast([P, nb, 32])

                link(dve.tensor_reduce(out=qs[:, 0, 0:nb], in_=blocks(src), axis=AX.X, op=ALU.max,
                                       apply_absolute_value=True))
                link(ts(qs[:, 1, 0:nb], qs[:, 0, 0:nb], 1.0 / FP8_MAX, 1e-30, ALU.mult, ALU.max))
                link(dve.reciprocal(qs[:, 2, 0:nb], qs[:, 1, 0:nb]))
                link(tt(blocks(b), blocks(src), per_block(2), ALU.mult))
                fp8_round(b, a)
                free()
                return tt(blocks(dst), blocks(b), per_block(1), ALU.mult)

            def make_h(S, t, src, dst, F, first=False):
                dve.wait_ge(S.silu_sb, t + 1)
                dve.wait_ge(S.up_ps, t + 1)
                if not first:
                    dve.wait_ge(S.hT_ps, t)
                return tt(dst[:, 0:F], src[:, 0:F], psB[:, 0:F], ALU.mult)

            dve.wait_ge(ld_small, 32)
            dve.tensor_reduce(out=tf[:, 0, :], in_=cond, axis=AX.X, op=ALU.add).then_inc(tf_sum, 1)
            dve.wait_ge(ld_side, 16)
            ts(ek[:, :, :], v_cb[:, :, :], 30.0, None, ALU.min).then_inc(ek_min, 1)

            def clamp_euk(layer):
                for k in range(KT):
                    g = layer * GROUPS + k * BATCH
                    ts(ratio[:, g:g + BATCH, :], v_cb[:, k * BATCH:(k + 1) * BATCH, :], wu[:, 1, layer, k:k + 1], 30.0,
                       ALU.add, ALU.min).then_inc(euk_min, 1)

            clamp_euk(0)
            dve.wait_ge(tf_exp, 1)
            link(ts(tf[:, 1, :], tf[:, 1, :], 1.0, None, ALU.add))
            link(dve.reciprocal(tf[:, 1, :], tf[:, 1, :]))
            link(ts(tf[:, 2, :], tf[:, 1, :], 0.5, 0.5, ALU.mult, ALU.add))
            link(ts(tf[:, 3, :], tf[:, 1, :], 0.2, 0.8, ALU.mult, ALU.add))
            link(dve.tensor_copy(tfo[:, :].rearrange("p (k b) -> p k b", k=KT),
                                 tf[:, 3:4, :].to_broadcast([P, KT, BATCH])))
            dve.wait_ge(dec_exp, 1)
            link(tt(decay[:, :].rearrange("p (l b) -> p l b", b=BATCH),
                    dec[:, :].rearrange("p (l o) -> p l o", o=1).to_broadcast([P, LAYERS * KT, BATCH]),
                    tf[:, 2:3, :].to_broadcast([P, LAYERS * KT, BATCH]), ALU.mult))
            for layer in range(1, LAYERS):
                clamp_euk(layer)
            dve.wait_ge(consts, 9)
            dve.wait_ge(ld_idx2, 16)
            link(ts(row_no[:, :], row_no[:, :], float(F2), float(F2), ALU.is_ge, ALU.mult))
            link(dve.tensor_copy(idx2f[:, :], idx2[:, :]))
            link(tt(idx2f[:, :], idx2f[:, :], row_no[:, :], ALU.add))
            dve.tensor_copy(idx2[:, :], idx2f[:, :]).then_inc(idx2_set, 1)

            wkv_group(0, 0, first=True)
            with dve.Fori(1, GROUPS) as g:
                steps.enter(g - 1, WKV_STEPS)
                wkv_group(g, g)
            steps.leave(GROUPS - 1)
            make_c(0, c0, sig0, 1).then_inc(c_made, 1)
            route0()

            def step0(t, layer, g, first=False):
                make_h(S0, t, silu_b, h_b, F0, first=first).then_inc(S0.h_sb, 1)
                if not first:
                    keep_y0(t - 1)
                wkv_group(layer * GROUPS + g, g)

            def keep_y0(t, first=False):
                dve.wait_ge(S0.y_ps, t + 1)
                if not first:
                    dve.wait_ge(S0.y_out, 16 * t)
                dve.tensor_copy(y_b[:, :], psY[:, :]).then_inc(S0.y_sb, 1)

            step0(0, 1, 0, first=True)
            make_h(S0, 1, silu_b, h_b, F0).then_inc(S0.h_sb, 1)
            keep_y0(0, first=True)
            wkv_group(GROUPS + 1, 1)
            with dve.Fori(2, GROUPS) as g:
                steps.enter(g - 2, WKV_STEPS)
                step0(g, 1, g)
            steps.leave(GROUPS - 2)
            for layer in (2, 3):
                with dve.Fori(0, GROUPS) as g:
                    steps.enter(g, WKV_STEPS)
                    step0((layer - 1) * GROUPS + g, layer, g)
                steps.leave(GROUPS)
            keep_y0(T0 - 1)

            dve.wait_ge(ld_raw2, 16 * GU2)
            dve.wait_ge(ld_rawd2, 16)

            def quant2(r, first=False):
                quant_rows(wq[:, 0:CH], row(raw2, r), wt_a[:, 0:CH], wt_b[:, 0:CH],
                           lambda: first or dve.wait_ge(wq_turned, r)).then_inc(wq_made, 1)

            quant2(0, first=True)
            with dve.Fori(1, GU2) as r:
                steps.enter(r - 1, QUANT_STEPS)
                quant2(r)
            steps.leave(GU2 - 1)
            for r in range(2):
                quant_rows(wq[:, :], rawd2[:, r, :], wt_a, wt_b,
                           lambda: dve.wait_ge(wq_turned, GU2 + r * J2 // 2)).then_inc(wq_made, 1)
            N2 = GU2 + J2

            for t in range(TILES):
                dve.wait_ge(gathered[t], 32)
                link(stt(x_tok[:, t, :], back_a[:, t, :], V[2][:, t:t + 1], x_tok[:, t, :], ALU.mult, ALU.add))
                stt(x_tok[:, t, :], back_b[:, t, :], V[3][:, t:t + 1], x_tok[:, t, :], ALU.mult, ALU.add)\
                    .then_inc(gather_used, 1)

            make_c(1, c_tok, sig, 1 + TILES).then_inc(c_made, 1)
            route1()

            def quant3(u, i, pair):
                dve.wait_ge(ld_raw3[i], 16 * pair + 16)
                quant_blocks(wq[:, 0:W3], raw3[:, i, :], wt_a[:, 0:W3], wt_b[:, 0:W3],
                             lambda: dve.wait_ge(wq_turned, N2 + u)).then_inc(wq_made, 1)

            def copy_x1(t, first=False):
                if not first:
                    dve.wait_ge(S1.xT_ps, t)
                dve.tensor_copy(xg[:, :], row(c_tok, t)).then_inc(S1.x_copied, 1)

            def add_y(S, t):
                dve.wait_ge(S.y_ps, t + 1)
                tt(row(x_tok, t), row(x_tok, t), psY[:, :], ALU.add).then_inc(S.y_sb, 1)

            def h1(t, first=False):
                make_h(S1, t, silu_b, h_b, F1, first=first).then_inc(S1.h_sb, 1)

            def keep_y1(t, first=False):
                dve.wait_ge(S1.y_ps, t + 1)
                if not first:
                    dve.wait_ge(S1.y_out, (t - TILES) * 16)
                dve.tensor_copy(y_b[:, :], psY[:, :]).then_inc(S1.y_sb, 1)

            def token_step(t, i, pair, first=False, last=False):
                h1(t, first=first)
                if not first:
                    add_y(S1, t - 1)
                quant3(t, i, pair)
                if not last:
                    copy_x1(t + 2)

            copy_x1(0, first=True)
            copy_x1(1)
            token_step(0, 0, 0, first=True)
            token_step(1, 1, 0)
            with dve.Fori(1, TILES // 2 - 1) as pair:
                steps.enter(pair - 1, 2 * QUANT_STEPS)
                for i in range(2):
                    token_step(2 * pair + i, i, pair)
            steps.leave(TILES // 2 - 2)
            token_step(TILES - 2, 0, TILES // 2 - 1, last=True)
            token_step(TILES - 1, 1, TILES // 2 - 1, last=True)
            h1(TILES)
            add_y(S1, TILES - 1)
            quant3(TILES, 0, TILES // 2)
            for t in range(TILES + 1, U3):
                h1(t)
                keep_y1(t - 1, first=(t == TILES + 1))
                quant3(t, t % 2, t // 2)
            with dve.Fori(U3, T1) as t:
                h1(t)
                keep_y1(t - 1)
            keep_y1(T1 - 1)
            for t in range(TILES):
                dve.wait_ge(gathered[t], 48)
                stt(x_tok[:, t, :], back1[:, t, :], V[7][:, t:t + 1], x_tok[:, t, :], ALU.mult, ALU.add)\
                    .then_inc(gather_used, 1)

            for layer, S, F, quant in ((2, S2, F2, quant_rows), (3, S3, F3, quant_blocks)):
                sigs = 1 + TILES * (layer - 1)

                def quant_x(t, first=False):
                    dve.wait_ge(sig_done, sigs + t + 1)
                    c2 = c_tile.rearrange("p (k c) -> p k c", k=KT)
                    link(tt(c2, row(sig, t).rearrange("p (k c) -> p k c", k=KT),
                            ratio_of(layer)[:, bass.ds(t, 1), :, :].rearrange("p a k c -> p (a k) c"), ALU.mult))
                    quant(xg[:, :], c_tile, q_a[:, 0:CH], q_b[:, 0:CH],
                          lambda: first or dve.wait_ge(S.xT_ps, t)).then_inc(S.x_copied, 1)

                def quant_h(t, first=False):
                    make_h(S, t, silu_w, h_w, F, first=first).then_inc(S.up_read, 1)
                    dve.wait_ge(S.up_read, t + 1)
                    quant(h_w[:, 0:F], h_w[:, 0:F], q_a[:, 0:F], q_b[:, 0:F], lambda: None).then_inc(S.h_sb, 1)

                quant_x(0, first=True)
                quant_x(1)
                quant_h(0, first=True)
                quant_x(2)
                with dve.Fori(1, TILES - 2) as t:
                    steps.enter(t - 1, 2 * QUANT_STEPS + 1)
                    quant_h(t)
                    add_y(S, t - 1)
                    quant_x(t + 2)
                steps.leave(TILES - 3)
                for t in (TILES - 2, TILES - 1):
                    quant_h(t)
                    add_y(S, t - 1)
                add_y(S, TILES - 1)


def kernel(**inputs):
    import numpy as np
    import concourse.bacc as bacc
    from concourse.bass_utils import run_bass_kernel_spmd

    a = {k: np.asarray(v) for k, v in inputs.items()}

    def k_first(w, k):
        e, rows, n = w.shape
        padded = np.zeros((e, k * P, n), w.dtype)
        padded[:, :rows] = w
        return padded.reshape(e, k, P, n).transpose(2, 1, 0, 3)

    def with_shared(w, shared):
        return np.concatenate([shared[None], w], axis=0)

    def gate(w):
        return w.reshape(KT, P, E).transpose(1, 0, 2)

    wu = np.stack([np.stack([a[f"L{i}_cond_{n}"].reshape(KT, P) for i in range(LAYERS)]) for n in "wu"])
    down3 = a["L3_ffn_down_w"].reshape(KT, P, F3 // W3, W3).transpose(0, 2, 1, 3).reshape(-1, P, W3)
    gate3, up3 = (a[f"L3_ffn_{n}_w"].reshape(F3 // P, P, CH) for n in ("gate", "up"))
    index = np.concatenate([a["L2_ffn_down_reorder_index"]] * 2)
    arrays = {
        "x_in": a["x"].reshape(TOK, CH),
        "side_in": a["fside_BxSxS_0"].reshape(BATCH, TIME, KT, P).transpose(3, 2, 0, 1).reshape(P, GROUPS, TIME),
        "cond_in": np.broadcast_to(a["cond_512"], (P, BATCH, 64)),
        "wu_in": wu.transpose(3, 0, 1, 2),
        "gw0_in": gate(a["L0_ffn_gate_w"].T),
        "w1_0_in": k_first(a["L0_ffn_w1"].transpose(0, 2, 1), KT),
        "w3_0_in": k_first(a["L0_ffn_w3"].transpose(0, 2, 1), KT),
        "w2_0_in": k_first(a["L0_ffn_w2"].transpose(0, 2, 1), J0),
        "gw1_in": gate(a["L1_ffn_Wg"]),
        "w1_1_in": k_first(with_shared(a["L1_ffn_W1"], a["L1_ffn_sw1"]), KT),
        "w3_1_in": k_first(with_shared(a["L1_ffn_W3"], a["L1_ffn_sw3"]), KT),
        "w2_1_in": k_first(with_shared(a["L1_ffn_W2"], a["L1_ffn_sw2"]), J1),
        "gu2_in": np.concatenate([a["L2_ffn_w_gate"], a["L2_ffn_w_up"]]),
        "down2_in": a["L2_ffn_w_down"].reshape(KT, P, F2).transpose(1, 0, 2),
        "idx2_in": index.reshape(GU2, P).T,
        "w3q_in": np.concatenate([np.concatenate([gate3, up3], axis=2), down3]),
    }
    arrays = {n: np.ascontiguousarray(v) for n, v in arrays.items()}
    nc = bacc.Bacc("TRN2", target_bir_lowering=False, num_devices=1)
    args = [nc.dram_tensor(n, v.shape, mybir.dt.from_np(v.dtype), kind="ExternalInput").ap() for n, v in arrays.items()]
    out = nc.dram_tensor("out", (TOK, CH), FP32, kind="ExternalOutput").ap()
    program(nc, *args, out)
    r = run_bass_kernel_spmd(nc, [arrays], core_ids=[0])
    return r.results[0]["out"].reshape(BATCH, TIME, CH)
```

```python
import concourse.bass as bass
from concourse import mybir
from contextlib import ExitStack

FP32 = mybir.dt.float32
BF16 = mybir.dt.bfloat16
I32 = mybir.dt.int32
U32 = mybir.dt.uint32
ALU = mybir.AluOpType
ACT = mybir.ActivationFunctionType
AX = mybir.AxisListType

P = 128
BATCH, TIME, CH = 4, 256, 256
TOK = BATCH * TIME
TILES = TOK // P
KT = CH // P
LAYERS = 4
E = 8
GROUPS = KT * BATCH
F0, F1, F2, F3 = 512, 352, 704, 1024
J0, J1, J2, J3 = 4, 3, 6, 8
CAP = TOK // E
T0 = (2 * TOK + E * (P - 1)) // P + 1
T1 = TILES + E
GU2 = 2 * F2 // P
WU = 512
U2 = GU2 * CH // WU
U3 = 3 * F3 * CH // (P * WU)
EARLY = 5
AHEAD = 4
FP8_MAX = 448.0
EXPONENT = 0x7F800000
MIN_NORMAL = 2.0 ** -6
ROUND = 1.5 * 2.0 ** 20


def program(nc, x_in, side_in, cond_in, wu_in, gw0_in, w1_0_in, w3_0_in, w2_0_in, gw1_in, w1_1_in, w3_1_in,
            w2_1_in, gu2_in, down2_in, idx2_in, w3q_in, out):
    ctx = ExitStack()
    with ctx:
        def sb(name, shape, dt=FP32):
            return ctx.enter_context(nc.sbuf_tensor(name, shape, dt))

        def sem(name):
            return ctx.enter_context(nc.semaphore(name))

        slots0 = nc.dram_tensor("slots0", [T0 * P, CH], FP32, kind="Internal").ap()
        ys0 = nc.dram_tensor("ys0", [T0 * P, CH], FP32, kind="Internal").ap()
        slots1 = nc.dram_tensor("slots1", [2 * TOK, CH], FP32, kind="Internal").ap()
        ys1 = nc.dram_tensor("ys1", [TOK, CH], FP32, kind="Internal").ap()

        big = sb("big", [P, 24576])
        r3 = sb("r3", [P, 6144])
        x_tok = sb("x_tok", [P, TILES, CH])
        ratio = sb("ratio", [P, LAYERS * GROUPS, TIME])
        v_cb = sb("v_cb", [P, GROUPS, TIME])
        ek = sb("ek", [P, GROUPS, TIME])
        spare = sb("spare", [P, 2432])
        scan_in = spare[:, 0:2 * TIME].rearrange("p (i t) -> p i t", i=2)
        own = spare[:, 2 * TIME:3 * TIME]

        w1_0 = big[:, 0:8192].rearrange("p (k e f) -> p k e f", k=KT, e=E)
        w3_0 = big[:, 8192:16384].rearrange("p (k e f) -> p k e f", k=KT, e=E)
        w2_0 = big[:, 16384:24576].rearrange("p (k e f) -> p k e f", k=J0, e=E)
        NE1 = E + 1
        a1 = KT * NE1 * F1
        w1_1 = big[:, 0:a1].rearrange("p (k e f) -> p k e f", k=KT, e=NE1)
        w3_1 = big[:, a1:2 * a1].rearrange("p (k e f) -> p k e f", k=KT, e=NE1)
        w2_1 = big[:, 2 * a1:2 * a1 + J1 * NE1 * CH].rearrange("p (k e f) -> p k e f", k=J1, e=NE1)
        o2 = 2 * a1 + J1 * NE1 * CH
        gu2 = big[:, o2:o2 + KT * 2 * F2].rearrange("p (k f) -> p k f", k=KT)
        down2 = big[:, o2 + KT * 2 * F2:o2 + KT * 2 * F2 + J2 * CH].rearrange("p (k f) -> p k f", k=J2)
        gate3 = r3[:, 0:2048].rearrange("p (k f) -> p k f", k=KT)
        up3 = r3[:, 2048:4096].rearrange("p (k f) -> p k f", k=KT)
        down3 = r3[:, 4096:6144].rearrange("p (k f) -> p k f", k=J3)

        zeros = r3[:, 0:2048]
        c0 = r3[:, 2048:4096].rearrange("p (t c) -> p t c", t=TILES)
        sig0 = r3[:, 4096:6144].rearrange("p (t c) -> p t c", t=TILES)
        raw2 = r3[:, 0:GU2 * CH].rearrange("p (t c) -> p t c", t=GU2)
        rawd2 = r3[:, GU2 * CH:GU2 * CH + 2 * F2].rearrange("p (t c) -> p t c", t=2)
        c_tok = v_cb[:, :, :].rearrange("p g t -> p (g t)").rearrange("p (t c) -> p t c", t=TILES)
        sig = ek[:, :, :].rearrange("p g t -> p (g t)").rearrange("p (t c) -> p t c", t=TILES)
        raw3 = spare[:, 0:2 * WU].rearrange("p (i c) -> p i c", i=2)
        wt_a, wt_b = spare[:, 1024:1728], spare[:, 1728:2432]
        wq = sb("wq", [P, F2])

        xg = sb("xg", [P, CH])
        xgT = sb("xgT", [P, KT, P])
        both_b = sb("both_b", [P, 2 * F0])
        silu_b, h_b = both_b[:, 0:F0], both_b[:, F0:2 * F0]
        hT_b = sb("hT_b", [P, J0, P])
        y_b = sb("y_b", [P, CH])
        back_a, back_b = (x[:, :, :].rearrange("p g t -> p (g t)").rearrange("p (t c) -> p t c", t=TILES)
                          for x in (v_cb, ek))
        back1 = w1_1[:, 0, 1:E + 1, :].rearrange("p e f -> p (e f)")[:, 0:TILES * CH]\
            .rearrange("p (t c) -> p t c", t=TILES)
        silu_w, h_w, h_q, q_a, q_b, hT_flat = (big[:, a1 + i * F3:a1 + (i + 1) * F3] for i in range(6))
        hT_w = hT_flat.rearrange("p (j t) -> p j t", j=J3)
        x_a, x_b = (big[:, a1 + 6 * F3 + i * CH:a1 + 6 * F3 + (i + 1) * CH] for i in range(2))

        acc = sb("acc", [P, 2, TIME])
        later = sb("later", [P, 2, TIME + 1])
        ones_row = spare[:, 3 * TIME:4 * TIME]
        rbuf = sb("rbuf", [P, TIME])
        cond = acc[:, 0, :].rearrange("p (b d) -> p b d", b=BATCH)
        wu = sb("wu", [P, 2, LAYERS, KT])
        tf = sb("tf", [P, 4, BATCH])
        tfo = sb("tfo", [P, GROUPS])
        dec = sb("dec", [P, LAYERS * KT])
        decay = sb("decay", [P, LAYERS * GROUPS])
        gw = [sb("gw0", [P, KT, E]), sb("gw1", [P, KT, E])]

        ident = sb("ident", [P, P])
        ones = sb("ones", [P, P], BF16)
        tri = sb("tri", [P, P], BF16)
        rev8 = sb("rev8", [P, E])
        e128 = sb("e128", [P, E])
        tile_no = sb("tile_no", [1, T0])
        tok_no = sb("tok_no", [P, TILES])
        row_no = sb("row_no", [P, GU2])
        idx2 = sb("idx2", [P, GU2], I32)
        idx2f = sb("idx2f", [P, GU2])
        one_hot = sb("one_hot", [P, TILES + 1, E], BF16)
        NR = 12
        rt0, rt1 = (x.rearrange("p (n t e) -> p n t e", n=NR, t=TILES)
                    for x in (both_b[:, 0:NR * TILES * E], r3[:, 6144 - NR * TILES * E:6144]))
        rs = sb("rs", [P, 16, TILES])
        cnt = sb("cnt", [P, 4, E])
        cmpb = sb("cmpb", [P, E, TILES])
        cmpt = sb("cmpt", [1, T0, E])
        eid_f = sb("eid_f", [1, T0])
        eid = sb("eid", [1, T0], I32)
        slot_a = sb("slot_a", [P, TILES], I32)
        slot_b = sb("slot_b", [P, TILES], I32)
        slot_w1 = sb("slot_w1", [P, TILES], I32)
        slot_r1 = sb("slot_r1", [P, TILES], I32)
        qs = sb("qs", [P, 3, 32])
        xs = sb("xs", [P, 3, 32])

        psA = ctx.enter_context(nc.psum_tensor("psA", [P, 1024], FP32))
        psB = ctx.enter_context(nc.psum_tensor("psB", [P, 1024], FP32))
        psH = ctx.enter_context(nc.psum_tensor("psH", [P, 1024], FP32))
        psX = ctx.enter_context(nc.psum_tensor("psX", [P, KT, P], FP32))
        psY = ctx.enter_context(nc.psum_tensor("psY", [P, CH], FP32))
        psR = psA[:, 512:768]
        psW = psH[:, 512:1024].rearrange("p (k c) -> p k c", k=4)
        psS = psB[:, 512:576].rearrange("p (t e) -> p t e", t=TILES)
        psK = psB[:, 768:840].rearrange("p (t e) -> p t e", t=TILES + 1)

        ld_x, ld_side, ld_small, ld_gate, ld_w0, ld_w1, ld_idx2 = (sem(n) for n in (
            "x_loaded", "side_loaded", "small_loaded", "router_loaded", "w0_loaded", "w1_loaded", "idx2_loaded"))
        consts, zeros_set, zeros_put, ld_raw2, ld_rawd2 = (sem(n) for n in (
            "consts_set", "zeros_set", "slots_zeroed", "raw2_gathered", "raw_down2_loaded"))
        ld_raw3 = [sem("raw3_loaded_even"), sem("raw3_loaded_odd")]
        pool_step = sem("pool_step")
        dve_step = sem("dve_step")
        tf_sum, tf_exp, w_exp, dec_exp, ek_min, ek_exp, euk_min, euk_exp, sig_done = (sem(n) for n in (
            "tf_summed", "tf_exp", "w_exp", "decay_exp", "k_clamped", "ek_done", "euk_clamped",
            "euk_done", "sigmoid_done"))
        grp_made, grp_turned, grp_kept = sem("wkv_group_made"), sem("wkv_group_transposed"), sem("wkv_group_kept")
        c_made = sem("c_made")
        c_tile_made = sem("c_tile_made")
        cT_turned, cT_kept = sem("cT_transposed"), sem("cT_kept")
        scored, logits_out, exps_in, exps_out, hot_set, ranked, routed = (sem(n) for n in (
            "scored", "scores_read", "exp_args_made", "exps_made", "one_hot_made", "ranked", "routed"))
        scattered0, scattered1 = sem("scattered0"), sem("scattered1")
        gathered, gather_used = [sem(f"gathered_{t}") for t in range(TILES)], sem("gathered_rows_used")
        scan_ready, own_ready, scanned, own_added, fwd_scanned = (sem(n) for n in (
            "wkv_scan_inputs_made", "wkv_own_terms_made", "wkv_scanned", "wkv_own_terms_added", "wkv_forward_scanned"))
        bwd_scanned = [scanned, sem("wkv_backward_scanned_k")]
        wq_made, wq_turned, wq_kept = sem("weights_quantised"), sem("weights_transposed"), sem("weights_kept")
        idx2_set = sem("idx2_set")
        out_put = sem("out_stored")

        class Stage:

            def __init__(self, name, up_read=None):
                self.x_in = sem(f"{name}_x_in")
                self.x_copied = sem(f"{name}_x_copied")
                self.xT_ps = sem(f"{name}_xT_ps")
                self.xT_sb = sem(f"{name}_xT_sb")
                self.gate_ps = sem(f"{name}_gate_ps")
                self.up_ps = sem(f"{name}_up_ps")
                self.silu_sb = sem(f"{name}_silu_sb")
                self.h_sb = sem(f"{name}_h_sb")
                self.hT_ps = sem(f"{name}_hT_ps")
                self.hT_sb = sem(f"{name}_hT_sb")
                self.y_ps = sem(f"{name}_y_ps")
                self.y_sb = sem(f"{name}_y_sb")
                self.y_out = sem(f"{name}_y_out")
                self.up_read = sem(f"{name}_up_read") if up_read else self.h_sb

        S0, S1, S23 = Stage("l0"), Stage("l1"), Stage("l23", True)

        class Steps:

            def __init__(self, engine, semaphore):
                self.engine, self.semaphore, self.base, self.n = engine, semaphore, 0, 0

            def link(self, instruction):
                self.n += 1
                instruction.then_inc(self.semaphore, 1)
                self.engine.wait_ge(self.semaphore, self.base + self.n)

            def pair(self, instruction):
                self.n += 1
                instruction.then_inc(self.semaphore, 1)

            def but_last(self):
                self.engine.wait_ge(self.semaphore, self.base + self.n - 1)

            def all(self):
                self.engine.wait_ge(self.semaphore, self.base + self.n)

            def enter(self, index, per):
                self.start, self.n0, self.per = self.base + self.n, self.n, per
                self.base, self.n = self.start + index * per, 0

            def leave(self, rounds):
                assert self.n == self.per, (self.n, self.per)
                self.base, self.n = self.start + rounds * self.per, 0

        def col(tile, i):
            return tile[:, bass.ds(i, 1)]

        def row(tile, i):
            return tile[:, bass.ds(i, 1), :].rearrange("p a t -> p (a t)")

        def ratio_of(layer):
            return ratio[:, layer * GROUPS:(layer + 1) * GROUPS, :].rearrange("p g t -> p (g t)")\
                .rearrange("p (k t c) -> p t k c", k=KT, t=TILES)

        block = ctx.enter_context(nc.Block())

        @block.sync
        def _(sp):
            sp.dma_start(wu[:, :, :, :], wu_in).then_inc(ld_small, 16)
            sp.dma_start(cond, cond_in).then_inc(ld_small, 16)
            sp.dma_start(v_cb[:, :, :], side_in).then_inc(ld_side, 16)
            sp.dma_start(x_tok[:, :, :], x_in.rearrange("(t p) c -> p t c", p=P)).then_inc(ld_x, 16)
            sp.dma_start(gw[0][:, :, :], gw0_in).then_inc(ld_gate, 16)
            sp.dma_start(gw[1][:, :, :], gw1_in).then_inc(ld_gate, 16)
            sp.dma_start(idx2[:, :], idx2_in).then_inc(ld_idx2, 16)
            sp.wait_ge(zeros_set, 1)
            for i in range(T0 // TILES):
                sp.dma_start(slots0[i * TOK:(i + 1) * TOK, :].rearrange("(p r) c -> p (r c)", p=P), zeros)\
                  .then_inc(zeros_put, 16)
            sp.dma_start(slots1[0:TOK, :].rearrange("(p r) c -> p (r c)", p=P), zeros).then_inc(zeros_put, 16)
            for src, dst in ((w1_0_in, w1_0), (w3_0_in, w3_0), (w2_0_in, w2_0)):
                sp.dma_start(dst, src).then_inc(ld_w0, 16)

            def load_slots(S, slots, t, turned):
                if turned is not None:
                    sp.wait_ge(S.xT_ps, turned)
                sp.dma_start(xg[:, :], slots[bass.ds(t * P, P), :]).then_inc(S.x_in, 16)

            def store_results(S, ys, t, made):
                sp.wait_ge(S.y_sb, made)
                sp.dma_start(ys[bass.ds(t * P, P), :], y_b[:, :]).then_inc(S.y_out, 16)

            sp.wait_ge(scattered0, 16 * 2 * TILES)
            load_slots(S0, slots0, 0, None)
            load_slots(S0, slots0, 1, 1)
            with sp.Fori(0, T0 - 2) as t:
                load_slots(S0, slots0, t + 2, t + 2)
                store_results(S0, ys0, t, t + 1)
            for t in (T0 - 2, T0 - 1):
                store_results(S0, ys0, t, t + 1)

            for e0, e1 in ((0, 1), (1, 3), (3, 6), (6, 9)):
                for src, dst in ((w1_1_in, w1_1), (w3_1_in, w3_1), (w2_1_in, w2_1)):
                    sp.dma_start(dst[:, :, e0:e1, :], src[:, :, e0:e1, :]).then_inc(ld_w1, 16)
            sp.wait_ge(scattered1, 16 * TILES)
            load_slots(S1, slots1, 0, AHEAD)
            load_slots(S1, slots1, 1, AHEAD + 1)
            with sp.Fori(0, E - 2) as t:
                load_slots(S1, slots1, t + 2, t + AHEAD + 2)
                store_results(S1, ys1, t, t + AHEAD + 1)
            for t in (E - 2, E - 1):
                store_results(S1, ys1, t, t + AHEAD + 1)

            with sp.Fori(0, TILES) as t:
                sp.wait_ge(S23.y_sb, t + TILES + 1)
                sp.dma_start(out[bass.ds(t * P, P), :], x_tok[:, bass.ds(t, 1), :].rearrange("p a c -> p (a c)"))\
                  .then_inc(out_put, 16)
            sp.wait_ge(out_put, 16 * TILES)

        @block.gpsimd
        def _(pool):
            steps = Steps(pool, pool_step)
            pool.memset(zeros, 0.0).then_inc(zeros_set, 1)
            steps.link(pool.memset(ident[:, :], 0.0))
            steps.link(pool.memset(ones[:, :], 1.0))
            steps.link(pool.memset(ones_row, 1.0))
            pool.memset(one_hot[:, :, :], 0.0).then_inc(consts, 1)
            pool.memset(later[:, :, TIME:TIME + 1], 0.0).then_inc(consts, 1)
            pool.affine_select(out=ident[:, :], in_=ident[:, :], compare_op=ALU.not_equal, fill=1.0, base=0,
                               pattern=[[-1, P]], channel_multiplier=1).then_inc(consts, 1)
            pool.affine_select(out=tri[:, :], in_=ones[:, :], compare_op=ALU.is_ge, fill=0.0, base=-1,
                               pattern=[[1, P]], channel_multiplier=-1).then_inc(consts, 1)
            for tile, base, pattern, mult in (
                    (rev8[:, :], E, [[-1, E]], 0), (e128[:, :], 0, [[P, E]], 0), (tile_no[:, :], 0, [[1, T0]], 0),
                    (tok_no[:, :], TOK, [[P, TILES]], 1), (row_no[:, :], 0, [[P, GU2]], 1)):
                pool.iota(tile, pattern=pattern, base=base, channel_multiplier=mult,
                          allow_small_or_imprecise_dtypes=True).then_inc(consts, 1)

            def wkv_inputs(j, g, first=False):
                if not first:
                    pool.wait_ge(bwd_scanned[1], j)
                pool.tensor_tensor(scan_in[:, 0, :], row(ek, g), row(v_cb, g), ALU.mult).then_inc(scan_ready, 1)
                pool.tensor_tensor(scan_in[:, 1, :], row(ek, g), ones_row, ALU.mult).then_inc(scan_ready, 1)
                if not first:
                    pool.wait_ge(own_added, j)
                pool.tensor_tensor(own, row(ratio, j), row(v_cb, g), ALU.mult).then_inc(own_ready, 1)

            def gather2(r):
                pool.indirect_dma_start(
                    out=raw2[:, r, :], out_offset=None, in_=gu2_in,
                    in_offset=bass.IndirectOffsetOnAxis(ap=idx2[:, r:r + 1].bitcast(U32), axis=0)).then_inc(ld_raw2, 16)

            pool.wait_ge(ek_exp, 1)
            pool.wait_ge(euk_exp, KT)
            wkv_inputs(0, 0, first=True)
            with pool.Fori(1, GROUPS) as g:
                wkv_inputs(g, g)
            pool.wait_ge(zeros_put, 16 * (T0 // TILES + 1))
            pool.wait_ge(routed, 1)
            for t in range(TILES):
                for slot in (slot_a, slot_b):
                    pool.indirect_dma_start(
                        out=slots0, out_offset=bass.IndirectOffsetOnAxis(ap=slot[:, t:t + 1].bitcast(U32), axis=0),
                        in_=c0[:, t, :], in_offset=None).then_inc(scattered0, 16)
            pool.wait_ge(euk_exp, LAYERS * KT)
            for g in range(EARLY, GROUPS):
                wkv_inputs(GROUPS + g, g)
                if g == EARLY:
                    pool.wait_ge(scattered0, 16 * 2 * TILES)
                    pool.wait_ge(idx2_set, 1)
                for r in range((g - EARLY) * 3, (g - EARLY) * 3 + 3):
                    gather2(r)
            for r in range((GROUPS - EARLY) * 3, GU2):
                gather2(r)
            pool.dma_start(rawd2, down2_in).then_inc(ld_rawd2, 16)
            for layer in (2, 3):
                with pool.Fori(0, GROUPS) as g:
                    wkv_inputs(layer * GROUPS + g, g)
            pool.wait_ge(S0.y_out, 16 * T0)
            pool.wait_ge(grp_made, LAYERS * GROUPS)
            pool.wait_ge(own_ready, LAYERS * GROUPS)
            for t in range(TILES):
                for rows, slot in ((back_a, slot_a), (back_b, slot_b)):
                    pool.indirect_dma_start(
                        out=rows[:, t, :], out_offset=None, in_=ys0,
                        in_offset=bass.IndirectOffsetOnAxis(ap=slot[:, t:t + 1].bitcast(U32), axis=0))\
                        .then_inc(gathered[t], 16)
            pool.wait_ge(routed, 2)
            for t in range(TILES):
                pool.indirect_dma_start(
                    out=slots1, out_offset=bass.IndirectOffsetOnAxis(ap=slot_w1[:, t:t + 1].bitcast(U32), axis=0),
                    in_=c_tok[:, t, :], in_offset=None).then_inc(scattered1, 16)
            def load_unit3(u, i, quantised):
                pool.wait_ge(wq_made, quantised)
                pool.dma_start(raw3[:, i, :], w3q_in[bass.ds(u, 1), :, :].rearrange("a p c -> (a p) c"))\
                    .then_inc(ld_raw3[i], 16)

            for i in range(2):
                load_unit3(i, i, U2 + 3)
            with pool.Fori(1, U3 // 2) as pair:
                for i in range(2):
                    load_unit3(2 * pair + i, i, U2 + 3 + 2 * pair + i - 1)
            pool.wait_ge(S1.y_out, 16 * E)
            for t in range(TILES):
                pool.indirect_dma_start(
                    out=back1[:, t, :], out_offset=None, in_=ys1,
                    in_offset=bass.IndirectOffsetOnAxis(ap=slot_r1[:, t:t + 1].bitcast(U32), axis=0))\
                    .then_inc(gathered[t], 16)
            pool.wait_ge(S1.x_copied, TILES)
            for layer in (2, 3):
                with pool.Fori(0, TILES) as t:
                    pool.wait_ge(sig_done, 1 + TILES * (layer - 1) + t + 1)
                    if layer == 3:
                        pool.wait_ge(S23.x_copied, t + 1)
                    pool.tensor_tensor(row(c_tok, t).rearrange("p (k c) -> p k c", k=KT),
                                       row(sig, t).rearrange("p (k c) -> p k c", k=KT),
                                       ratio_of(layer)[:, bass.ds(t, 1), :, :].rearrange("p a k c -> p (a k) c"),
                                       ALU.mult).then_inc(c_tile_made, 1)

        @block.tensor
        def _(pe):
            def turn(dst, src, rows=P):
                return pe.transpose(dst, src, ident[0:rows, 0:rows])

            def turn_group(j):
                pe.wait_ge(grp_made, j + 1)
                pe.wait_ge(grp_kept, j)
                for h in range(2):
                    mm = turn(psR[:, h * P:(h + 1) * P], rbuf[:, h * P:(h + 1) * P])
                mm.then_inc(grp_turned, 1)

            def turn_weights(n, pieces):
                pe.wait_ge(wq_made, n + 1)
                pe.wait_ge(wq_kept, n)
                for k, cols in enumerate(pieces):
                    mm = turn(psW[0:cols, k, :], wq[:, k * P:k * P + cols])
                mm.then_inc(wq_turned, 1)

            def score(layer, c):
                cT = ratio[:, layer * GROUPS:(layer + 1) * GROUPS, :].rearrange("p g t -> p (g t)")\
                    .rearrange("p (k n) -> p k n", k=KT)
                pe.wait_ge(c_made, layer + 1)
                banks = ((psA, 0), (psB, 0), (psH, 0), (psH, 512))
                for i, (ps, o) in enumerate(banks):
                    for t in range(4):
                        mm = turn(ps[:, o + t * P:o + (t + 1) * P],
                                  c[:, (i % 2) * 4 + t, (i // 2) * P:(i // 2 + 1) * P])
                    mm.then_inc(cT_turned, 1)
                pe.wait_ge(cT_kept, 4 * (layer + 1))
                for t in range(TILES):
                    for k in range(KT):
                        mm = pe.matmul(psS[:, t, :], cT[:, k, t * P:(t + 1) * P], gw[layer][:, k, :],
                                       start=(k == 0), stop=(k == KT - 1))
                mm.then_inc(scored, 1)

            def rank(layer):
                pe.wait_ge(hot_set, layer + 1)
                mm = pe.matmul(psK[:, :, :], tri[:, :], one_hot[:, :, :], start=True, stop=False)
                for i in range(TILES):
                    n = TILES - i
                    mm = pe.matmul(psK[:, i + 1:TILES + 1, :], ones[:, :],
                                   one_hot[:, i:i + 1, :].to_broadcast([P, n, E]), start=False, stop=(i == TILES - 1))
                mm.then_inc(ranked, 1)

            def x_turn(S, t, ready, first=False):
                ready(t)
                if not first:
                    pe.wait_ge(S.xT_sb, t)
                for k in range(KT):
                    mm = turn(psX[:, k, :], xg[:, k * P:(k + 1) * P])
                mm.then_inc(S.xT_ps, 1)

            def in_product(S, ps, F, weights, done):
                for c in range(0, F, 512):
                    n = min(512, F - c)
                    for k in range(KT):
                        mm = pe.matmul(ps[:, c:c + n], xgT[:, k, :], weights(k, c, n), start=(k == 0), stop=(k == KT - 1))
                mm.then_inc(done, 1)

            def gate_up(S, t, F, wg, wu_, first=False):
                pe.wait_ge(S.xT_sb, t + 1)
                if not first:
                    pe.wait_ge(S.silu_sb, t)
                in_product(S, psA, F, wg, S.gate_ps)
                if not first:
                    pe.wait_ge(S.up_read, t)
                in_product(S, psB, F, wu_, S.up_ps)

            def h_turn(S, t, h, F, first=False):
                pe.wait_ge(S.h_sb, t + 1)
                if not first:
                    pe.wait_ge(S.hT_sb, t)
                for j in range((F + P - 1) // P):
                    n = min(P, F - j * P)
                    mm = turn(psH[0:n, j * P:(j + 1) * P], h[:, j * P:j * P + n])
                mm.then_inc(S.hT_ps, 1)

            def down(S, t, hT, F, wd, first=False):
                pe.wait_ge(S.hT_sb, t + 1)
                if not first:
                    pe.wait_ge(S.y_sb, t)
                J = (F + P - 1) // P
                for j in range(J):
                    n = min(P, F - j * P)
                    mm = pe.matmul(psY[:, :], hT[0:n, j, :], wd(j, n), start=(j == 0), stop=(j == J - 1))
                mm.then_inc(S.y_ps, 1)

            pe.wait_ge(consts, 9)
            pe.wait_ge(grp_made, 1)
            for h in range(2):
                mm = turn(psR[:, h * P:(h + 1) * P], rbuf[:, h * P:(h + 1) * P])
            mm.then_inc(grp_turned, 1)
            with pe.Fori(1, GROUPS) as j:
                turn_group(j)
            pe.wait_ge(ld_gate, 32)
            score(0, c0)
            rank(0)
            with pe.Fori(GROUPS, GROUPS + EARLY) as j:
                turn_group(j)

            def slots_in(S):
                return lambda t: pe.wait_ge(S.x_in, 16 * t + 16)

            def w0(t):
                e = pe.value_load(eid[0:1, bass.ds(t, 1)], min_val=0, max_val=E - 1)
                return [lambda k, c, n, w=w: w[:, k, bass.ds(e, 1), c:c + n].rearrange("p a f -> p (a f)")
                        for w in (w1_0, w3_0)]

            def wd0(t):
                e = pe.value_load(eid[0:1, bass.ds(t, 1)], min_val=0, max_val=E - 1)
                return lambda j, n: w2_0[0:n, j, bass.ds(e, 1), :].rearrange("p a f -> p (a f)")

            pe.wait_ge(ld_w0, 48)
            pe.wait_ge(routed, 1)
            x_turn(S0, 0, slots_in(S0), first=True)
            gate_up(S0, 0, F0, *w0(0), first=True)
            x_turn(S0, 1, slots_in(S0))

            def step0(t, job, first=False, last=False):
                h_turn(S0, t - 1, h_b, F0, first=first)
                gate_up(S0, t, F0, *w0(t))
                if not last:
                    x_turn(S0, t + 1, slots_in(S0))
                down(S0, t - 1, hT_b, F0, wd0(t - 1), first=first)
                job()

            def turn_unit2(u, first=False):
                pe.wait_ge(wq_made, u + 1)
                if not first:
                    pe.wait_ge(wq_kept, u)
                for k in range(KT):
                    for r in range(2):
                        mm = turn(psW[:, 2 * k + r, :], wq[:, r * CH + k * P:r * CH + (k + 1) * P])
                mm.then_inc(wq_turned, 1)

            J0_ = GROUPS + EARLY
            G0 = LAYERS * GROUPS - J0_
            step0(1, lambda: turn_group(J0_), first=True)
            with pe.Fori(2, G0 + 1) as t:
                step0(t, lambda: turn_group(t + J0_ - 1))
            step0(G0 + 1, lambda: turn_unit2(0, first=True))
            with pe.Fori(G0 + 2, T0 - 1) as t:
                step0(t, lambda: turn_unit2(t - G0 - 1))
            step0(T0 - 1, lambda: turn_unit2(T0 - 2 - G0), last=True)
            h_turn(S0, T0 - 1, h_b, F0)
            down(S0, T0 - 1, hT_b, F0, wd0(T0 - 1))

            turn_unit2(U2 - 1)
            turn_weights(U2, [P, P])
            for r in range(2):
                for i in range(J2 // 2):
                    n = U2 + 1 + r * J2 // 2 + i
                    pe.wait_ge(wq_made, U2 + 1 + r + 1)
                    pe.wait_ge(wq_kept, n)
                    for k in range(2):
                        j = 2 * i + k
                        cols = min(P, F2 - j * P)
                        mm = turn(psW[0:cols, k, :], wq[:, j * P:j * P + cols])
                    mm.then_inc(wq_turned, 1)
            N2 = U2 + 1 + J2
            M2 = U2 + 3

            score(1, c_tok)
            rank(1)

            def turn_unit3(u):
                pe.wait_ge(wq_made, M2 + u + 1)
                pe.wait_ge(wq_kept, N2 + u)
                for k in range(4):
                    mm = turn(psW[:, k, :], wq[:, k * P:(k + 1) * P])
                mm.then_inc(wq_turned, 1)

            def w1e(e):
                return [lambda k, c, n, w=w: w[:, k, bass.ds(e, 1), c:c + n].rearrange("p a f -> p (a f)")
                        for w in (w1_1, w3_1)]

            def wd1(e):
                return lambda j, n: w2_1[0:n, j, bass.ds(e, 1), :].rearrange("p a f -> p (a f)")

            def shared(t):
                pe.wait_ge(S1.x_copied, t + 1)

            def expert(t):
                pe.wait_ge(S1.x_in, (t - AHEAD) * 16 + 16)

            def shared_late(t):
                pe.wait_ge(S1.x_copied, t - E + 1)

            pe.wait_ge(ld_w1, 16 * 3 * 4)
            x_turn(S1, 0, shared, first=True)
            gate_up(S1, 0, F1, *w1e(0), first=True)
            x_turn(S1, 1, shared)

            def step1(t, e_in, e_down, ready, unit=None, first=False, last=False):
                h_turn(S1, t - 1, h_b, F1, first=first)
                gate_up(S1, t, F1, *w1e(e_in))
                if not last:
                    x_turn(S1, t + 1, ready)
                down(S1, t - 1, hT_b, F1, wd1(e_down), first=first)
                if unit is not None:
                    turn_unit3(unit)

            step1(1, 0, 0, shared, 0, first=True)
            with pe.Fori(2, AHEAD - 1) as t:
                step1(t, 0, 0, shared, t - 1)
            step1(AHEAD - 1, 0, 0, expert, AHEAD - 2)
            with pe.Fori(AHEAD, AHEAD + E - 1) as t:
                step1(t, t - AHEAD + 1, t - AHEAD, expert, t - 1)
            step1(AHEAD + E - 1, E, E - 1, shared_late, AHEAD + E - 2)
            assert U3 == AHEAD + E
            step1(AHEAD + E, 0, E, shared_late, U3 - 1)
            with pe.Fori(AHEAD + E + 1, T1 - 1) as t:
                step1(t, 0, 0, shared_late)
            step1(T1 - 1, 0, 0, shared_late, last=True)
            h_turn(S1, T1 - 1, h_b, F1)
            down(S1, T1 - 1, hT_b, F1, wd1(0))

            L2 = (F2, lambda k, c, n: gu2[:, k, c:c + n], lambda k, c, n: gu2[:, k, F2 + c:F2 + c + n],
                  lambda j, n: down2[0:n, j, :])
            L3 = (F3, lambda k, c, n: gate3[:, k, c:c + n], lambda k, c, n: up3[:, k, c:c + n],
                  lambda j, n: down3[0:n, j, :])

            def tile_ready(t):
                pe.wait_ge(S23.x_copied, t + 1)

            def step(t, now, before, first=False, last=False):
                gate_up(S23, t, now[0], now[1], now[2])
                if not last:
                    x_turn(S23, t + 1, tile_ready)
                h_turn(S23, t - 1, h_q, before[0], first=first)
                down(S23, t - 1, hT_w, before[0], before[3], first=first)

            x_turn(S23, 0, tile_ready, first=True)
            gate_up(S23, 0, L2[0], L2[1], L2[2], first=True)
            x_turn(S23, 1, tile_ready)
            step(1, L2, L2, first=True)
            with pe.Fori(2, TILES) as t:
                step(t, L2, L2)
            step(TILES, L3, L2)
            with pe.Fori(TILES + 1, 2 * TILES - 1) as t:
                step(t, L3, L3)
            step(2 * TILES - 1, L3, L3, last=True)
            h_turn(S23, 2 * TILES - 1, h_q, F3)
            down(S23, 2 * TILES - 1, hT_w, F3, L3[3])

        @block.scalar
        def _(act):
            def keep_group(j):
                act.wait_ge(grp_turned, j + 1)
                act.activation(ratio[:, bass.ds(j, 1), :].rearrange("p a t -> p (a t)"), psR, ACT.Copy)\
                   .then_inc(grp_kept, 1)

            def keep_cT(layer):
                cT = ratio[:, layer * GROUPS:(layer + 1) * GROUPS, :].rearrange("p g t -> p (g t)")
                for i, (ps, o) in enumerate(((psA, 0), (psB, 0), (psH, 0), (psH, 512))):
                    act.wait_ge(cT_turned, 4 * layer + i + 1)
                    act.activation(cT[:, i * 512:(i + 1) * 512], ps[:, o:o + 512], ACT.Copy).then_inc(cT_kept, 1)

            def keep_xT(S, t, first=False):
                act.wait_ge(S.xT_ps, t + 1)
                if not first:
                    act.wait_ge(S.up_ps, t)
                act.activation(xgT[:, :, :], psX[:, :, :], ACT.Copy).then_inc(S.xT_sb, 1)

            def silu(S, t, dst, F, first=False):
                act.wait_ge(S.gate_ps, t + 1)
                if not first:
                    act.wait_ge(S.up_read, t)
                act.activation(dst[:, 0:F], psA[:, 0:F], ACT.Silu).then_inc(S.silu_sb, 1)

            def keep_hT(S, t, hT, F, first=False):
                act.wait_ge(S.hT_ps, t + 1)
                if not first:
                    act.wait_ge(S.y_ps, t)
                full, rest = F // P, F % P
                done = act.activation(hT[:, 0:full, :].rearrange("p j t -> p (j t)"), psH[:, 0:full * P], ACT.Copy)
                if rest:
                    done = act.activation(hT[0:rest, full, :], psH[0:rest, full * P:(full + 1) * P], ACT.Copy)
                done.then_inc(S.hT_sb, 1)

            act.wait_ge(tf_sum, 1)
            act.activation(tf[:, 1, :], tf[:, 0, :], ACT.Exp, scale=-1.0).then_inc(tf_exp, 1)
            act.activation(wu[:, 0, :, :], wu[:, 0, :, :], ACT.Exp).then_inc(w_exp, 1)
            act.wait_ge(w_exp, 1)
            act.activation(dec[:, :], wu[:, 0, :, :].rearrange("p l k -> p (l k)"), ACT.Exp, scale=-1.0)\
               .then_inc(dec_exp, 1)
            act.wait_ge(ek_min, 1)
            act.activation(ek[:, :, :], ek[:, :, :], ACT.Exp).then_inc(ek_exp, 1)
            for i in range(LAYERS * KT):
                act.wait_ge(euk_min, i + 1)
                part = ratio[:, i * BATCH:(i + 1) * BATCH, :]
                act.activation(part, part, ACT.Exp).then_inc(euk_exp, 1)
            act.wait_ge(ld_x, 16)
            act.activation(sig0[:, :, :], x_tok[:, :, :], ACT.Sigmoid).then_inc(sig_done, 1)
            with act.Fori(0, GROUPS) as j:
                keep_group(j)
            keep_cT(0)
            act.wait_ge(exps_in, 1)
            act.activation(rt0[:, 10:12, :, :], rt0[:, 8:10, :, :], ACT.Exp, scale=-1.0).then_inc(exps_out, 1)
            with act.Fori(GROUPS, GROUPS + EARLY) as j:
                keep_group(j)

            keep_xT(S0, 0, first=True)
            silu(S0, 0, silu_b, F0, first=True)
            keep_xT(S0, 1)

            def keep_y(S, t, stored):
                act.wait_ge(S.y_ps, t + 1)
                if stored is not None:
                    act.wait_ge(S.y_out, 16 * stored)
                act.activation(y_b[:, :], psY[:, :], ACT.Copy).then_inc(S.y_sb, 1)

            def keep_unit2(u):
                act.wait_ge(wq_turned, u + 1)
                act.activation(gu2[:, :, bass.ds(u * 2 * P, 2 * P)], psW.rearrange("p (k r) c -> p k (r c)", k=KT), ACT.Copy)\
                   .then_inc(wq_kept, 1)

            def step0(t, job, first=False, last=False):
                keep_hT(S0, t - 1, hT_b, F0, first=first)
                silu(S0, t, silu_b, F0)
                if not last:
                    keep_xT(S0, t + 1)
                keep_y(S0, t - 1, None if first else t - 1)
                job()

            J0_ = GROUPS + EARLY
            G0 = LAYERS * GROUPS - J0_
            step0(1, lambda: keep_group(J0_), first=True)
            with act.Fori(2, G0 + 1) as t:
                step0(t, lambda: keep_group(t + J0_ - 1))
            with act.Fori(G0 + 1, T0 - 1) as t:
                step0(t, lambda: keep_unit2(t - G0 - 1))
            step0(T0 - 1, lambda: keep_unit2(T0 - 2 - G0), last=True)
            keep_hT(S0, T0 - 1, hT_b, F0)
            keep_y(S0, T0 - 1, T0 - 1)

            keep_unit2(U2 - 1)
            act.wait_ge(wq_turned, U2 + 1)
            act.activation(gu2[:, :, U2 * 2 * P:GU2 * P], psW[:, 0:KT, :], ACT.Copy).then_inc(wq_kept, 1)
            for r in range(2):
                for i in range(J2 // 2):
                    act.wait_ge(wq_turned, U2 + 1 + r * J2 // 2 + i + 1)
                    if 2 * i + 2 < J2:
                        done = act.activation(down2[:, 2 * i:2 * i + 2, r * P:(r + 1) * P], psW[:, 0:2, :], ACT.Copy)
                    else:
                        act.activation(down2[:, 2 * i, r * P:(r + 1) * P], psW[:, 0, :], ACT.Copy)
                        done = act.activation(down2[0:F2 % P, 2 * i + 1, r * P:(r + 1) * P], psW[0:F2 % P, 1, :],
                                              ACT.Copy)
                    done.then_inc(wq_kept, 1)

            def sigmoid_x(t, semaphore, n):
                act.wait_ge(semaphore, n)
                act.activation(sig[:, t, :], x_tok[:, t, :], ACT.Sigmoid).then_inc(sig_done, 1)

            for t in range(TILES):
                sigmoid_x(t, gather_used, t + 1)
            keep_cT(1)
            act.wait_ge(exps_in, 2)
            act.activation(rt1[:, 10, :, :], rt1[:, 8, :, :], ACT.Exp, scale=-1.0).then_inc(exps_out, 1)
            N2 = U2 + 1 + J2

            def keep_gu3(i):
                act.wait_ge(wq_turned, N2 + i + 1)
                act.activation(r3[:, 0:4096].rearrange("p (m f) -> p m f", f=F3)[:, :, bass.ds(i * P, P)], psW[:, :, :],
                               ACT.Copy).then_inc(wq_kept, 1)

            def keep_down3(r, c):
                act.wait_ge(wq_turned, N2 + TILES + 2 * r + c + 1)
                act.activation(down3[:, 4 * c:4 * c + 4, r * P:(r + 1) * P], psW[:, :, :], ACT.Copy).then_inc(wq_kept, 1)

            def copy_x1(t):
                act.activation(xg[:, :], row(c_tok, t), ACT.Copy).then_inc(S1.x_copied, 1)

            copy_x1(0)
            keep_xT(S1, 0, first=True)
            copy_x1(1)
            silu(S1, 0, silu_b, F1, first=True)
            keep_xT(S1, 1)
            copy_x1(2)

            def step1(t, unit=None, copy=None, keep=None, first=False, last=False):
                keep_hT(S1, t - 1, hT_b, F1, first=first)
                silu(S1, t, silu_b, F1)
                if not last:
                    keep_xT(S1, t + 1)
                if copy is not None:
                    copy_x1(copy)
                if keep is not None:
                    keep()
                if unit:
                    unit()

            step1(1, lambda: keep_gu3(0), copy=3, first=True)
            with act.Fori(2, AHEAD + 1) as t:
                step1(t, lambda: keep_gu3(t - 1))
            step1(AHEAD + 1, lambda: keep_gu3(AHEAD), keep=lambda: keep_y(S1, AHEAD, None))
            with act.Fori(AHEAD + 2, TILES + 1) as t:
                step1(t, lambda: keep_gu3(t - 1), keep=lambda: keep_y(S1, t - 1, t - 1 - AHEAD))
            for t in range(TILES + 1, U3 + 1):
                step1(t, lambda: keep_down3((t - 1 - TILES) // 2, (t - 1 - TILES) % 2),
                      copy=(t + 2 - E if t + 2 >= AHEAD + E else None), keep=lambda: keep_y(S1, t - 1, t - 1 - AHEAD))
            for t in range(U3 + 1, T1 - 1):
                step1(t, copy=(t + 2 - E if t + 2 < T1 else None))
            step1(T1 - 1, last=True)
            keep_hT(S1, T1 - 1, hT_b, F1)

            for t in range(TILES):
                sigmoid_x(t, gather_used, TILES + t + 1)
            keep_xT(S23, 0, first=True)
            silu(S23, 0, silu_w, F2, first=True)
            keep_xT(S23, 1)

            def sigmoid3(t):
                act.wait_ge(c_tile_made, t + 1)
                act.wait_ge(S23.y_sb, t + 1)
                act.activation(row(sig, t), row(x_tok, t), ACT.Sigmoid).then_inc(sig_done, 1)

            def step(t, F, F_before, sigmoid=None, first=False, last=False):
                silu(S23, t, silu_w, F)
                if not last:
                    keep_xT(S23, t + 1)
                keep_hT(S23, t - 1, hT_w, F_before, first=first)
                if sigmoid is not None:
                    sigmoid3(sigmoid)

            step(1, F2, F2, first=True)
            with act.Fori(2, TILES) as t:
                step(t, F2, F2, t - 2)
            step(TILES, F3, F2, TILES - 2)
            step(TILES + 1, F3, F3, TILES - 1)
            with act.Fori(TILES + 2, 2 * TILES - 1) as t:
                step(t, F3, F3)
            step(2 * TILES - 1, F3, F3, last=True)
            keep_hT(S23, 2 * TILES - 1, hT_w, F3)

        @block.vector
        def _(dve):
            steps = Steps(dve, dve_step)
            link = steps.link
            tt, ts, stt = dve.tensor_tensor, dve.tensor_scalar, dve.scalar_tensor_tensor

            def wkv_group(j, g, first=False, reads=None):
                reads = reads or [scan_in[:, i, :] for i in range(2)]
                backwards = [x[:, TIME - 1::-1] for x in reads]
                d = col(decay, j)
                d_all = d.to_broadcast([P, TIME])
                if not first:
                    dve.wait_ge(grp_made, j)
                for i in range(2):
                    dve.wait_ge(scan_ready, 2 * j + i + 1)
                    dve.tensor_tensor_scan(acc[:, i, :], d_all, reads[i], 0.0, ALU.mult, ALU.add)\
                        .then_inc(fwd_scanned, 1)
                    dve.tensor_tensor_scan(later[:, i, TIME - 1::-1], d_all, backwards[i], 0.0,
                                           ALU.mult, ALU.add).then_inc(bwd_scanned[i], 1)
                dve.wait_ge(fwd_scanned, 2 * j + 2)
                dve.wait_ge(bwd_scanned[0], j + 1)
                dve.wait_ge(bwd_scanned[1], j + 1)
                link(stt(acc[:, :, :], later[:, :, 1:TIME + 1], d, acc[:, :, :], ALU.mult, ALU.add))
                dve.wait_ge(own_ready, j + 1)
                link(tt(acc[:, 1, :], acc[:, 1, :], row(ratio, j), ALU.add))
                tt(acc[:, 0, :], acc[:, 0, :], own, ALU.add).then_inc(own_added, 1)
                link(ts(acc[:, 1, :], acc[:, 1, :], 1e-8, None, ALU.max))
                link(dve.reciprocal(acc[:, 1, :], acc[:, 1, :]))
                dve.wait_ge(own_added, j + 1)
                if not first:
                    dve.wait_ge(grp_turned, j)
                stt(rbuf[:, :], acc[:, 0, :], col(tfo, g), acc[:, 1, :], ALU.mult, ALU.mult).then_inc(grp_made, 1)

            WKV_STEPS = 4

            def early_group(j, g):
                dve.wait_ge(bwd_scanned[0], j)
                tt(scan_in[:, 0, :], ek[:, g, :], v_cb[:, g, :], ALU.mult).then_inc(scan_ready, 2)
                dve.wait_ge(own_added, j)
                tt(own, ratio[:, j, :], v_cb[:, g, :], ALU.mult).then_inc(own_ready, 1)
                wkv_group(j, g, reads=[scan_in[:, 0, :], ek[:, g, :]])

            def make_c(layer, c, sg, sigmoids):
                dve.wait_ge(sig_done, sigmoids)
                dve.wait_ge(grp_kept, GROUPS * (layer + 1))
                s4 = sg.rearrange("p t (k c) -> p t k c", k=KT)
                c4 = c.rearrange("p t (k c) -> p t k c", k=KT)
                link(tt(c4[:, :, 0, :], s4[:, :, 0, :], ratio_of(layer)[:, :, 0, :], ALU.mult))
                return tt(c4[:, :, 1, :], s4[:, :, 1, :], ratio_of(layer)[:, :, 1, :], ALU.mult)

            V = [rs[:, i, :] for i in range(16)]

            def over_e(vec):
                return vec.rearrange("p (t o) -> p t o", o=1).to_broadcast([P, TILES, E])

            def over_t(vec):
                return vec.rearrange("p (o e) -> p o e", o=1).to_broadcast([P, TILES, E])

            def reduce_e(dst, src, op):
                link(dve.tensor_reduce(out=dst, in_=src, axis=AX.X, op=op))

            def first_max(score, top, hot, tmp):
                reduce_e(top, score, ALU.max)
                link(tt(tmp, score, over_e(top), ALU.is_equal))
                link(tt(tmp, tmp, over_t(rev8[:, :]), ALU.mult))
                reduce_e(V[15], tmp, ALU.max)
                link(tt(hot, tmp, over_e(V[15]), ALU.is_equal))

            def route0():
                R = [rt0[:, i, :, :] for i in range(NR)]
                s, hot1, hot2, tmp, ab, s_rest, keep1, keep2 = R[0:8]
                dve.wait_ge(scored, 1)
                link(dve.tensor_copy(s, psS[:, :, :]))
                first_max(s, V[0], hot1, tmp)
                link(stt(s_rest, hot1, -1e30, s, ALU.mult, ALU.add))
                first_max(s_rest, V[1], hot2, tmp)
                dve.wait_ge(consts, 9)
                tt(one_hot[:, 0:TILES, :], hot1, hot2, ALU.add).then_inc(hot_set, 1)
                link(stt(ab, s, -1.0, s, ALU.mult, ALU.max))
                for top, keep, diff in ((V[0], keep1, R[8]), (V[1], keep2, R[9])):
                    link(tt(diff, over_e(top), s, ALU.subtract))
                    link(tt(tmp, ab, over_e(top), ALU.max))
                    link(ts(tmp, tmp, 0.02, None, ALU.mult))
                    link(tt(keep, diff, tmp, ALU.is_le))
                link(ts(R[9], R[9], 0.0, None, ALU.max))
                link(ts(tmp, hot1, -1.0, 1.0, ALU.mult, ALU.add))
                tt(keep2, keep2, tmp, ALU.mult).then_inc(exps_in, 1)
                dve.wait_ge(exps_in, 1)
                dve.wait_ge(exps_out, 1)
                for keep, ex, m in ((keep1, R[10], V[2]), (keep2, R[11], V[3])):
                    link(tt(ex, ex, keep, ALU.mult))
                    reduce_e(m, ex, ALU.add)
                    link(dve.reciprocal(m, m))
                dve.wait_ge(ranked, 1)
                link(dve.tensor_copy(cnt[:, 0, :], psK[:, TILES, :]))
                link(tt(cmpb[:, :, :], cnt[:, 0, :].rearrange("p (e o) -> p e o", o=1).to_broadcast([P, E, TILES]),
                        e128[:, :].rearrange("p (o t) -> p o t", o=1).to_broadcast([P, E, TILES]), ALU.is_gt))
                link(dve.tensor_reduce(out=cnt[:, 1, :], in_=cmpb[:, :, :], axis=AX.X, op=ALU.add))
                link(dve.memset(cnt[:, 3, :], 1.0))
                link(dve.tensor_tensor_scan(cnt[:, 2, :], cnt[:, 3, :], cnt[:, 1, :], 0.0, ALU.mult, ALU.add))
                link(tt(cnt[:, 3, :], cnt[:, 2, :], cnt[:, 1, :], ALU.subtract))
                link(ts(cnt[:, 3, :], cnt[:, 3, :], float(P), None, ALU.mult))
                link(tt(tmp, psK[:, 0:TILES, :], over_t(cnt[:, 3, :]), ALU.add))
                for hot, v, slot in ((hot1, V[4], slot_a), (hot2, V[5], slot_b)):
                    link(tt(ab, hot, tmp, ALU.mult))
                    reduce_e(v, ab, ALU.add)
                    link(dve.tensor_copy(slot[:, :], v))
                link(tt(cmpt[:, :, :], cnt[0:1, 2, :].rearrange("p (o e) -> p o e", o=1).to_broadcast([1, T0, E]),
                        tile_no[:, :].rearrange("p (t o) -> p t o", o=1).to_broadcast([1, T0, E]), ALU.is_le))
                link(dve.tensor_reduce(out=eid_f[:, :], in_=cmpt[:, :, :], axis=AX.X, op=ALU.add))
                link(ts(eid_f[:, :], eid_f[:, :], float(E - 1), None, ALU.min))
                dve.tensor_copy(eid[:, :], eid_f[:, :]).then_inc(routed, 1)

            def route1():
                R = [rt1[:, i, :, :] for i in range(NR)]
                s, hot1, _, tmp, ab = R[0:5]
                dve.wait_ge(scored, 2)
                link(dve.tensor_copy(s, psS[:, :, :]))
                first_max(s, V[6], hot1, tmp)
                dve.tensor_copy(one_hot[:, 0:TILES, :], hot1).then_inc(hot_set, 1)
                tt(R[8], over_e(V[6]), s, ALU.subtract).then_inc(exps_in, 1)
                dve.wait_ge(exps_out, 2)
                reduce_e(V[7], R[10], ALU.add)
                link(dve.reciprocal(V[7], V[7]))
                dve.wait_ge(ranked, 2)
                link(tt(ab, hot1, psK[:, 0:TILES, :], ALU.mult))
                reduce_e(V[8], ab, ALU.add)
                link(tt(ab, hot1, over_t(e128[:, :]), ALU.mult))
                reduce_e(V[9], ab, ALU.add)
                link(ts(V[10], V[8], float(CAP), None, ALU.is_lt))
                link(tt(V[7], V[7], V[10], ALU.mult))
                link(tt(V[11], V[8], V[9], ALU.add))
                link(tt(V[11], V[11], V[10], ALU.mult))
                link(ts(V[12], V[10], -1.0, 1.0, ALU.mult, ALU.add))
                link(tt(V[13], V[12], tok_no[:, :], ALU.mult))
                link(tt(V[13], V[13], V[11], ALU.add))
                link(dve.tensor_copy(slot_w1[:, :], V[13]))
                link(stt(V[14], V[12], float(TOK - 1), V[11], ALU.mult, ALU.add))
                dve.tensor_copy(slot_r1[:, :], V[14]).then_inc(routed, 1)

            class Quant:
                def __init__(self, src, dst, a, b, q, size, least):
                    self.src, self.dst, self.a, self.b, self.q = src, dst, a, b, q
                    self.size, self.least, self.blocks = size, least, src.shape[-1] // size

                def scaled(self, dst, src, i):
                    if self.blocks == 1:
                        return ts(dst, src, self.q[:, i, 0:1], None, ALU.mult)
                    per_block = self.q[:, i, 0:self.blocks].rearrange("p (b o) -> p b o", o=1)
                    return tt(dst.rearrange("p (b c) -> p b c", c=self.size), src.rearrange("p (b c) -> p b c", c=self.size),
                              per_block.to_broadcast([P, self.blocks, self.size]), ALU.mult)

                def largest(self):
                    return dve.tensor_reduce(out=self.q[:, 0, 0:self.blocks],
                                             in_=self.src.rearrange("p (b c) -> p b c", c=self.size),
                                             axis=AX.X, op=ALU.max, apply_absolute_value=True)

                def scale(self):
                    q = self.q[:, :, 0:self.blocks]
                    if self.least is None:
                        return ts(q[:, 1, :], q[:, 0, :], 1.0 / FP8_MAX, None, ALU.mult)
                    return ts(q[:, 1, :], q[:, 0, :], 1.0 / FP8_MAX, self.least, ALU.mult, ALU.max)

                def inverse(self):
                    return dve.reciprocal(self.q[:, 2, 0:self.blocks], self.q[:, 1, 0:self.blocks])

                def divided(self):
                    return self.scaled(self.b, self.src, 2)

                def exponent(self):
                    return ts(self.a.bitcast(U32), self.b.bitcast(U32), EXPONENT, None, ALU.bitwise_and)

                def magic(self):
                    return ts(self.a, self.a, MIN_NORMAL, ROUND, ALU.max, ALU.mult)

                def add(self):
                    return tt(self.b, self.b, self.a, ALU.add)

                def subtract(self):
                    return tt(self.b, self.b, self.a, ALU.subtract)

                def result(self):
                    return self.scaled(self.dst, self.b, 1)

            def quantise(z):
                link(z.largest())
                link(z.scale())
                link(z.inverse())
                link(z.divided())
                link(z.exponent())
                link(z.magic())
                link(z.add())
                link(z.subtract())

            QUANT_STEPS = 8

            def make_h(S, t, src, dst, F, first=False):
                dve.wait_ge(S.silu_sb, t + 1)
                dve.wait_ge(S.up_ps, t + 1)
                if not first:
                    dve.wait_ge(S.hT_ps, t)
                return tt(dst[:, 0:F], src[:, 0:F], psB[:, 0:F], ALU.mult)

            dve.wait_ge(ld_small, 32)
            dve.tensor_reduce(out=tf[:, 0, :], in_=cond, axis=AX.X, op=ALU.add).then_inc(tf_sum, 1)
            dve.wait_ge(ld_side, 16)
            ts(ek[:, :, :], v_cb[:, :, :], 30.0, None, ALU.min).then_inc(ek_min, 1)

            def clamp_euk(layer):
                for k in range(KT):
                    g = layer * GROUPS + k * BATCH
                    ts(ratio[:, g:g + BATCH, :], v_cb[:, k * BATCH:(k + 1) * BATCH, :], wu[:, 1, layer, k:k + 1], 30.0,
                       ALU.add, ALU.min).then_inc(euk_min, 1)

            clamp_euk(0)
            dve.wait_ge(tf_exp, 1)
            link(ts(tf[:, 1, :], tf[:, 1, :], 1.0, None, ALU.add))
            link(dve.reciprocal(tf[:, 1, :], tf[:, 1, :]))
            link(ts(tf[:, 2, :], tf[:, 1, :], 0.5, 0.5, ALU.mult, ALU.add))
            link(ts(tf[:, 3, :], tf[:, 1, :], 0.2, 0.8, ALU.mult, ALU.add))
            link(dve.tensor_copy(tfo[:, :].rearrange("p (k b) -> p k b", k=KT),
                                 tf[:, 3:4, :].to_broadcast([P, KT, BATCH])))
            dve.wait_ge(dec_exp, 1)
            link(tt(decay[:, :].rearrange("p (l b) -> p l b", b=BATCH),
                    dec[:, :].rearrange("p (l o) -> p l o", o=1).to_broadcast([P, LAYERS * KT, BATCH]),
                    tf[:, 2:3, :].to_broadcast([P, LAYERS * KT, BATCH]), ALU.mult))
            for layer in range(1, LAYERS):
                clamp_euk(layer)
            dve.wait_ge(consts, 9)
            dve.wait_ge(ld_idx2, 16)
            link(ts(row_no[:, :], row_no[:, :], float(F2), float(F2), ALU.is_ge, ALU.mult))
            link(dve.tensor_copy(idx2f[:, :], idx2[:, :]))
            link(tt(idx2f[:, :], idx2f[:, :], row_no[:, :], ALU.add))
            dve.tensor_copy(idx2[:, :], idx2f[:, :]).then_inc(idx2_set, 1)

            wkv_group(0, 0, first=True)
            with dve.Fori(1, GROUPS) as g:
                steps.enter(g - 1, WKV_STEPS)
                wkv_group(g, g)
            steps.leave(GROUPS - 1)
            make_c(0, c0, sig0, 1).then_inc(c_made, 1)
            route0()

            dve.wait_ge(euk_exp, LAYERS * KT)
            for g in range(EARLY):
                early_group(GROUPS + g, g)

            def h0(t, first=False):
                make_h(S0, t, silu_b, h_b, F0, first=first).then_inc(S0.h_sb, 1)

            for g in range(EARLY, GROUPS):
                h0(g - EARLY, first=(g == EARLY))
                wkv_group(GROUPS + g, g)
            for layer in (2, 3):
                with dve.Fori(0, GROUPS) as g:
                    steps.enter(g, WKV_STEPS)
                    h0(g + (layer - 1) * GROUPS - EARLY)
                    wkv_group(layer * GROUPS + g, g)
                steps.leave(GROUPS)
            G0 = LAYERS * GROUPS - GROUPS - EARLY
            assert G0 + U2 == T0

            def quant2(u, first=False):
                z = Quant(r3[:, bass.ds(u * WU, WU)], wq[:, 0:WU], wt_a[:, 0:WU], wt_b[:, 0:WU], qs, CH, None)
                quantise(z)
                if not first:
                    dve.wait_ge(wq_turned, u)
                z.result().then_inc(wq_made, 1)

            h0(G0)
            dve.wait_ge(ld_raw2, 16 * GU2)
            quant2(0, first=True)
            with dve.Fori(1, U2) as u:
                steps.enter(u - 1, QUANT_STEPS)
                h0(G0 + u)
                quant2(u)
            steps.leave(U2 - 1)
            dve.wait_ge(ld_rawd2, 16)
            for n, src in ((U2, row(raw2, GU2 - 1)), (U2 + 1, rawd2[:, 0, :]), (U2 + 1 + J2 // 2, rawd2[:, 1, :])):
                w = src.shape[-1]
                z = Quant(src, wq[:, 0:w], wt_a[:, 0:w], wt_b[:, 0:w], qs, w, None)
                quantise(z)
                dve.wait_ge(wq_turned, n)
                z.result().then_inc(wq_made, 1)
            N2 = U2 + 1 + J2

            for t in range(TILES):
                dve.wait_ge(gathered[t], 32)
                link(stt(x_tok[:, t, :], back_a[:, t, :], V[2][:, t:t + 1], x_tok[:, t, :], ALU.mult, ALU.add))
                stt(x_tok[:, t, :], back_b[:, t, :], V[3][:, t:t + 1], x_tok[:, t, :], ALU.mult, ALU.add)\
                    .then_inc(gather_used, 1)

            make_c(1, c_tok, sig, 1 + TILES).then_inc(c_made, 1)
            route1()

            def quant3(u, i, pair):
                dve.wait_ge(ld_raw3[i], 16 * pair + 16)
                z = Quant(raw3[:, i, :], wq[:, 0:WU], wt_a[:, 0:WU], wt_b[:, 0:WU], qs, 32, 1e-30)
                quantise(z)
                dve.wait_ge(wq_turned, N2 + u)
                z.result().then_inc(wq_made, 1)

            def add_y(S, t, tile):
                dve.wait_ge(S.y_ps, t + 1)
                tt(row(x_tok, tile), row(x_tok, tile), psY[:, :], ALU.add).then_inc(S.y_sb, 1)

            def h1(t, first=False):
                make_h(S1, t, silu_b, h_b, F1, first=first).then_inc(S1.h_sb, 1)

            for t in range(AHEAD + 2):
                h1(t, first=(t == 0))
                quant3(t, t % 2, t // 2)
                if 1 <= t <= AHEAD:
                    add_y(S1, t - 1, t - 1)
            with dve.Fori((AHEAD + 2) // 2, U3 // 2) as pair:
                steps.enter(pair - (AHEAD + 2) // 2, 2 * QUANT_STEPS)
                for i in range(2):
                    h1(2 * pair + i)
                    quant3(2 * pair + i, i, pair)
            steps.leave(U3 // 2 - (AHEAD + 2) // 2)
            h1(U3)
            with dve.Fori(U3 + 1, T1) as t:
                h1(t)
                add_y(S1, t - 1, t - 1 - E)
            add_y(S1, T1 - 1, TILES - 1)
            dve.wait_ge(S1.y_sb, T1)
            for t in range(TILES):
                dve.wait_ge(gathered[t], 48)
                stt(x_tok[:, t, :], back1[:, t, :], V[7][:, t:t + 1], x_tok[:, t, :], ALU.mult, ALU.add)\
                    .then_inc(gather_used, 1)

            def x_quant(tile, size, least):
                return Quant(row(c_tok, tile), xg[:, :], x_a, x_b, xs, size, least)

            def h_quant(F, size, least):
                return Quant(h_w[:, 0:F], h_q[:, 0:F], q_a[:, 0:F], q_b[:, 0:F], qs, size, least)

            def make_h23(t, F):
                dve.wait_ge(S23.silu_sb, t + 1)
                dve.wait_ge(S23.up_ps, t + 1)
                tt(h_w[:, 0:F], silu_w[:, 0:F], psB[:, 0:F], ALU.mult).then_inc(S23.up_read, 1)

            X2, X3 = (CH, None), (32, 1e-30)
            H2, H3 = (F2, F2, None), (F3, 32, 1e-30)

            def only_x(t, first=False):
                z = x_quant(t, *X2)
                dve.wait_ge(c_tile_made, t + 1)
                quantise(z)
                if not first:
                    dve.wait_ge(S23.xT_ps, t)
                z.result().then_inc(S23.x_copied, 1)

            def h_and_x(t, H, X, tile, tile_y, first=False):
                h, x = h_quant(*H), x_quant(tile, *X)
                make_h23(t, H[0])
                dve.wait_ge(c_tile_made, t + 3)
                steps.pair(x.largest())
                dve.wait_ge(S23.up_read, t + 1)
                steps.pair(h.largest())
                for step in (Quant.scale, Quant.inverse, Quant.divided, Quant.exponent, Quant.magic, Quant.add,
                             Quant.subtract):
                    for z in (x, h):
                        steps.but_last()
                        steps.pair(step(z))
                if not first:
                    add_y(S23, t - 1, tile_y)
                steps.all()
                dve.wait_ge(S23.xT_ps, t + 2)
                x.result().then_inc(S23.x_copied, 1)
                if not first:
                    dve.wait_ge(S23.hT_ps, t)
                h.result().then_inc(S23.h_sb, 1)

            def only_h(t, tile_y):
                z = h_quant(*H3)
                make_h23(t, H3[0])
                dve.wait_ge(S23.up_read, t + 1)
                quantise(z)
                dve.wait_ge(S23.hT_ps, t)
                z.result().then_inc(S23.h_sb, 1)
                add_y(S23, t - 1, tile_y)

            only_x(0, first=True)
            only_x(1)
            h_and_x(0, H2, X2, 2, 0, first=True)
            with dve.Fori(1, TILES - 2) as t:
                steps.enter(t - 1, 2 * QUANT_STEPS)
                h_and_x(t, H2, X2, t + 2, t - 1)
            steps.leave(TILES - 3)
            for t in (TILES - 2, TILES - 1):
                h_and_x(t, H2, X3, t + 2 - TILES, t - 1)
            h_and_x(TILES, H3, X3, 2, TILES - 1)
            with dve.Fori(TILES + 1, 2 * TILES - 2) as t:
                steps.enter(t - TILES - 1, 2 * QUANT_STEPS)
                h_and_x(t, H3, X3, t + 2 - TILES, t - 1 - TILES)
            steps.leave(TILES - 3)
            for t in (2 * TILES - 2, 2 * TILES - 1):
                only_h(t, t - 1 - TILES)
            add_y(S23, 2 * TILES - 1, TILES - 1)


def kernel(**inputs):
    import numpy as np
    import concourse.bacc as bacc
    from concourse.bass_utils import run_bass_kernel_spmd

    a = {k: np.asarray(v) for k, v in inputs.items()}

    def k_first(w, k):
        e, rows, n = w.shape
        padded = np.zeros((e, k * P, n), w.dtype)
        padded[:, :rows] = w
        return padded.reshape(e, k, P, n).transpose(2, 1, 0, 3)

    def with_shared(w, shared):
        return np.concatenate([shared[None], w], axis=0)

    def gate(w):
        return w.reshape(KT, P, E).transpose(1, 0, 2)

    wu = np.stack([np.stack([a[f"L{i}_cond_{n}"].reshape(KT, P) for i in range(LAYERS)]) for n in "wu"])
    down3 = a["L3_ffn_down_w"].reshape(KT, P, F3 // WU, WU).transpose(0, 2, 1, 3).reshape(-1, P, WU)
    gate3, up3 = (a[f"L3_ffn_{n}_w"].reshape(F3 // P, P, CH) for n in ("gate", "up"))
    index = np.concatenate([a["L2_ffn_down_reorder_index"]] * 2)
    arrays = {
        "x_in": a["x"].reshape(TOK, CH),
        "side_in": a["fside_BxSxS_0"].reshape(BATCH, TIME, KT, P).transpose(3, 2, 0, 1).reshape(P, GROUPS, TIME),
        "cond_in": np.broadcast_to(a["cond_512"], (P, BATCH, 64)),
        "wu_in": wu.transpose(3, 0, 1, 2),
        "gw0_in": gate(a["L0_ffn_gate_w"].T),
        "w1_0_in": k_first(a["L0_ffn_w1"].transpose(0, 2, 1), KT),
        "w3_0_in": k_first(a["L0_ffn_w3"].transpose(0, 2, 1), KT),
        "w2_0_in": k_first(a["L0_ffn_w2"].transpose(0, 2, 1), J0),
        "gw1_in": gate(a["L1_ffn_Wg"]),
        "w1_1_in": k_first(with_shared(a["L1_ffn_W1"], a["L1_ffn_sw1"]), KT),
        "w3_1_in": k_first(with_shared(a["L1_ffn_W3"], a["L1_ffn_sw3"]), KT),
        "w2_1_in": k_first(with_shared(a["L1_ffn_W2"], a["L1_ffn_sw2"]), J1),
        "gu2_in": np.concatenate([a["L2_ffn_w_gate"], a["L2_ffn_w_up"]]),
        "down2_in": a["L2_ffn_w_down"].reshape(KT, P, F2).transpose(1, 0, 2),
        "idx2_in": index.reshape(GU2, P).T,
        "w3q_in": np.concatenate([np.concatenate([gate3, up3], axis=2), down3]),
    }
    arrays = {n: np.ascontiguousarray(v) for n, v in arrays.items()}
    nc = bacc.Bacc("TRN2", target_bir_lowering=False, num_devices=1)
    args = [nc.dram_tensor(n, v.shape, mybir.dt.from_np(v.dtype), kind="ExternalInput").ap() for n, v in arrays.items()]
    out = nc.dram_tensor("out", (TOK, CH), FP32, kind="ExternalOutput").ap()
    program(nc, *args, out)
    r = run_bass_kernel_spmd(nc, [arrays], core_ids=[0])
    return r.results[0]["out"].reshape(BATCH, TIME, CH)
```

```python
import concourse.bass as bass
from concourse import mybir
from contextlib import ExitStack

FP32 = mybir.dt.float32
BF16 = mybir.dt.bfloat16
I32 = mybir.dt.int32
U32 = mybir.dt.uint32
ALU = mybir.AluOpType
ACT = mybir.ActivationFunctionType
AX = mybir.AxisListType

P = 128
BATCH, TIME, CH = 4, 256, 256
TOK = BATCH * TIME
TILES = TOK // P
KT = CH // P
LAYERS = 4
E = 8
GROUPS = KT * BATCH
F0, F1, F2, F3 = 512, 352, 704, 1024
J0, J1, J2, J3 = 4, 3, 6, 8
CAP = TOK // E
T0 = (2 * TOK + E * (P - 1)) // P + 1
T1 = TILES + E
GU2 = 2 * F2 // P
WU = 512
U2 = GU2 * CH // WU
U3 = 3 * F3 * CH // (P * WU)
EARLY = 3
AHEAD = 4
FP8_MAX = 448.0
EXPONENT = 0x7F800000
MIN_NORMAL = 2.0 ** -6
ROUND = 1.5 * 2.0 ** 20


def program(nc, x_in, side_in, cond_in, wu_in, gw0_in, w1_0_in, w3_0_in, w2_0_in, gw1_in, w1_1_in, w3_1_in,
            w2_1_in, gu2_in, down2_in, idx2_in, w3q_in, out):
    ctx = ExitStack()
    with ctx:
        def sb(name, shape, dt=FP32):
            return ctx.enter_context(nc.sbuf_tensor(name, shape, dt))

        def sem(name):
            return ctx.enter_context(nc.semaphore(name))

        slots0 = nc.dram_tensor("slots0", [T0 * P, CH], FP32, kind="Internal").ap()
        ys0 = nc.dram_tensor("ys0", [T0 * P, CH], FP32, kind="Internal").ap()
        slots1 = nc.dram_tensor("slots1", [2 * TOK, CH], FP32, kind="Internal").ap()
        ys1 = nc.dram_tensor("ys1", [TOK, CH], FP32, kind="Internal").ap()

        big = sb("big", [P, 24576])
        r3 = sb("r3", [P, 6144])
        x_tok = sb("x_tok", [P, TILES, CH])
        ratio = sb("ratio", [P, LAYERS * GROUPS, TIME])
        v_cb = sb("v_cb", [P, GROUPS, TIME])
        ek = sb("ek", [P, GROUPS, TIME])
        spare = sb("spare", [P, 2432])
        scan_in = spare[:, 0:2 * TIME].rearrange("p (i t) -> p i t", i=2)
        own = spare[:, 2 * TIME:3 * TIME]

        BATCH_PARTS = (slice(0, 1), slice(1, BATCH))

        def by_batch(x):
            return x.rearrange("p (k b) t -> p k b t", k=KT)

        w1_0 = big[:, 0:8192].rearrange("p (k e f) -> p k e f", k=KT, e=E)
        w3_0 = big[:, 8192:16384].rearrange("p (k e f) -> p k e f", k=KT, e=E)
        w2_0 = big[:, 16384:24576].rearrange("p (k e f) -> p k e f", k=J0, e=E)
        NE1 = E + 1
        a1 = KT * NE1 * F1
        w1_1 = big[:, 0:a1].rearrange("p (k e f) -> p k e f", k=KT, e=NE1)
        w3_1 = big[:, a1:2 * a1].rearrange("p (k e f) -> p k e f", k=KT, e=NE1)
        w2_1 = big[:, 2 * a1:2 * a1 + J1 * NE1 * CH].rearrange("p (k e f) -> p k e f", k=J1, e=NE1)
        o2 = 2 * a1 + J1 * NE1 * CH
        gu2 = big[:, o2:o2 + KT * 2 * F2].rearrange("p (k f) -> p k f", k=KT)
        down2 = big[:, o2 + KT * 2 * F2:o2 + KT * 2 * F2 + J2 * CH].rearrange("p (k f) -> p k f", k=J2)
        gate3 = r3[:, 0:2048].rearrange("p (k f) -> p k f", k=KT)
        up3 = r3[:, 2048:4096].rearrange("p (k f) -> p k f", k=KT)
        down3 = r3[:, 4096:6144].rearrange("p (k f) -> p k f", k=J3)

        zeros = r3[:, 0:2048]
        c0 = r3[:, 2048:4096].rearrange("p (t c) -> p t c", t=TILES)
        sig0 = r3[:, 4096:6144].rearrange("p (t c) -> p t c", t=TILES)
        raw2 = r3[:, 0:2 * U2 * CH].rearrange("p (t c) -> p t c", t=2 * U2)
        c_tok = v_cb[:, :, :].rearrange("p g t -> p (g t)").rearrange("p (t c) -> p t c", t=TILES)
        sig = ek[:, :, :].rearrange("p g t -> p (g t)").rearrange("p (t c) -> p t c", t=TILES)
        raw3 = spare[:, 0:2 * WU].rearrange("p (i c) -> p i c", i=2)
        last2 = spare[:, 0:CH]
        wt_a, wt_b = spare[:, 1024:1728], spare[:, 1728:2432]
        wq = sb("wq", [P, F2])

        xg = sb("xg", [P, CH])
        xgT = sb("xgT", [P, KT, P])
        both_b = sb("both_b", [P, 2 * F0])
        silu_b, h_b = both_b[:, 0:F0], both_b[:, F0:2 * F0]
        hT_b = sb("hT_b", [P, J0, P])
        y_b = sb("y_b", [P, CH])
        back_a, back_b = (x[:, :, :].rearrange("p g t -> p (g t)").rearrange("p (t c) -> p t c", t=TILES)
                          for x in (v_cb, ek))
        back1 = w1_1[:, 0, 1:E + 1, :].rearrange("p e f -> p (e f)")[:, 0:TILES * CH]\
            .rearrange("p (t c) -> p t c", t=TILES)
        rawd2 = w1_1[:, 1, 1:E + 1, :].rearrange("p e f -> p (e f)")[:, 0:2 * F2].rearrange("p (r c) -> p r c", r=2)
        silu_w, h_w, h_q, q_a, q_b, hT_flat = (big[:, a1 + i * F3:a1 + (i + 1) * F3] for i in range(6))
        hT_w = hT_flat.rearrange("p (j t) -> p j t", j=J3)
        x_a, x_b = (w2_1[:, 0, 1 + i, :] for i in range(2))

        acc = sb("acc", [P, 2, TIME])
        later = sb("later", [P, 2, TIME + 1])
        ones_row = spare[:, 3 * TIME:4 * TIME]
        accs = [acc, spare[:, 1024:1024 + 2 * TIME].rearrange("p (i t) -> p i t", i=2)]
        laters = [later, spare[:, 1536:1536 + 2 * (TIME + 1)].rearrange("p (i t) -> p i t", i=2)]
        inverse0 = spare[:, 2432 - TIME:2432]
        rbuf = sb("rbuf", [P, TIME])
        cond = acc[:, 0, :].rearrange("p (b d) -> p b d", b=BATCH)
        wu = sb("wu", [P, 2, LAYERS, KT])
        tf = sb("tf", [P, 4, BATCH])
        tfo = sb("tfo", [P, GROUPS])
        dec = sb("dec", [P, LAYERS * KT])
        decay = sb("decay", [P, LAYERS * GROUPS])
        gw = [sb("gw0", [P, KT, E]), sb("gw1", [P, KT, E])]

        ident = sb("ident", [P, P])
        ones = sb("ones", [P, P], BF16)
        tri = sb("tri", [P, P], BF16)
        rev8 = sb("rev8", [P, E])
        e128 = sb("e128", [P, E])
        tile_no = sb("tile_no", [1, T0])
        tok_no = sb("tok_no", [P, TILES])
        row_no = sb("row_no", [P, GU2])
        idx2 = sb("idx2", [P, GU2], I32)
        idx2f = sb("idx2f", [P, GU2])
        one_hot = sb("one_hot", [P, TILES + 1, E], BF16)
        NR = 12
        rt0, rt1 = (x.rearrange("p (n t e) -> p n t e", n=NR, t=TILES)
                    for x in (both_b[:, 0:NR * TILES * E], r3[:, 6144 - NR * TILES * E:6144]))
        rs = sb("rs", [P, 16, TILES])
        cnt = sb("cnt", [P, 4, E])
        cmpb = sb("cmpb", [P, E, TILES])
        cmpt = sb("cmpt", [1, T0, E])
        eid_f = sb("eid_f", [1, T0])
        eid = sb("eid", [1, T0], I32)
        slot_a = sb("slot_a", [P, TILES], I32)
        slot_b = sb("slot_b", [P, TILES], I32)
        slot_w1 = sb("slot_w1", [P, TILES], I32)
        slot_r1 = sb("slot_r1", [P, TILES], I32)
        qs = sb("qs", [P, 3, 32])
        xs = sb("xs", [P, 3, 32])

        psA = ctx.enter_context(nc.psum_tensor("psA", [P, 1024], FP32))
        psB = ctx.enter_context(nc.psum_tensor("psB", [P, 1024], FP32))
        psH = ctx.enter_context(nc.psum_tensor("psH", [P, 1024], FP32))
        psX = ctx.enter_context(nc.psum_tensor("psX", [P, KT, P], FP32))
        psY = ctx.enter_context(nc.psum_tensor("psY", [P, CH], FP32))
        psR = psA[:, 512:768]
        ps_den = [psH[:, 512 * i:512 * i + TIME] for i in range(2)]
        ps_num = [psX[:, :, :].rearrange("p k t -> p (k t)"), psY[:, 0:TIME]]
        psW = psH[:, 512:1024].rearrange("p (k c) -> p k c", k=4)
        psS = psB[:, 512:576].rearrange("p (t e) -> p t e", t=TILES)
        psK = psB[:, 768:840].rearrange("p (t e) -> p t e", t=TILES + 1)

        ld_x, ld_small, ld_gate, ld_w0, ld_shared1, ld_w1, ld_idx2 = (sem(n) for n in (
            "x_loaded", "small_loaded", "router_loaded", "w0_loaded", "shared1_loaded", "w1_loaded",
            "idx2_loaded"))
        consts, zeros_set, zeros_put, ld_raw2 = (sem(n) for n in (
            "consts_set", "zeros_set", "slots_zeroed", "raw2_gathered"))
        ld_rawd2 = sem("raw_down2_loaded")
        ld_side = [sem("side_first_batch_loaded"), sem("side_loaded")]
        ld_last2 = sem("last_raw2_gathered")
        ld_raw3 = [sem("raw3_loaded_even"), sem("raw3_loaded_odd")]
        pool_step = sem("pool_step")
        dve_step = sem("dve_step")
        tf_sum, tf_exp, w_exp, dec_exp, ek_min, ek_exp, euk_min, euk_exp, sig_done = (sem(n) for n in (
            "tf_summed", "tf_exp", "w_exp", "decay_exp", "k_clamped", "ek_done", "euk_clamped",
            "euk_done", "sigmoid_done"))
        grp_made, grp_turned, grp_kept = sem("wkv_group_made"), sem("wkv_group_transposed"), sem("wkv_group_kept")
        c_made = sem("c_made")
        c_tile_made = sem("c_tile_made")
        cT_turned, cT_kept = sem("cT_transposed"), sem("cT_kept")
        scored, logits_out, exps_in, exps_out, hot_set, ranked, routed = (sem(n) for n in (
            "scored", "scores_read", "exp_args_made", "exps_made", "one_hot_made", "ranked", "routed"))
        scattered0, scattered1 = sem("scattered0"), sem("scattered1")
        gathered, gather_used = [sem(f"gathered_{t}") for t in range(TILES)], sem("gathered_rows_used")
        scan_ready, own_ready, scanned, own_added, fwd_scanned = (sem(n) for n in (
            "wkv_scan_inputs_made", "wkv_own_terms_made", "wkv_scanned", "wkv_own_terms_added", "wkv_forward_scanned"))
        sums_joined = sem("wkv_forward_and_backward_sums_joined")
        bwd_scanned = [scanned, sem("wkv_backward_scanned_k")]
        wq_made, wq_turned, wq_kept = sem("weights_quantised"), sem("weights_transposed"), sem("weights_kept")
        idx2_set = sem("idx2_set")
        wq_rounded = sem("layer3_units_rounded")
        out_put = sem("out_stored")

        class Stage:

            def __init__(self, name, up_read=None):
                self.x_in = sem(f"{name}_x_in")
                self.x_copied = sem(f"{name}_x_copied")
                self.xT_ps = sem(f"{name}_xT_ps")
                self.xT_sb = sem(f"{name}_xT_sb")
                self.gate_ps = sem(f"{name}_gate_ps")
                self.up_ps = sem(f"{name}_up_ps")
                self.silu_sb = sem(f"{name}_silu_sb")
                self.h_sb = sem(f"{name}_h_sb")
                self.hT_ps = sem(f"{name}_hT_ps")
                self.hT_sb = sem(f"{name}_hT_sb")
                self.y_ps = sem(f"{name}_y_ps")
                self.y_sb = sem(f"{name}_y_sb")
                self.y_out = sem(f"{name}_y_out")
                self.up_read = sem(f"{name}_up_read") if up_read else self.h_sb

        S0, S1, S23 = Stage("l0"), Stage("l1"), Stage("l23", True)

        EUK0 = KT * len(BATCH_PARTS)

        class Steps:

            def __init__(self, engine, semaphore):
                self.engine, self.semaphore, self.base, self.n = engine, semaphore, 0, 0

            def link(self, instruction):
                self.n += 1
                instruction.then_inc(self.semaphore, 1)
                self.engine.wait_ge(self.semaphore, self.base + self.n)

            def pair(self, instruction):
                self.n += 1
                instruction.then_inc(self.semaphore, 1)

            def but_last(self):
                self.engine.wait_ge(self.semaphore, self.base + self.n - 1)

            def all(self):
                self.engine.wait_ge(self.semaphore, self.base + self.n)

            def enter(self, index, per):
                self.start, self.n0, self.per = self.base + self.n, self.n, per
                self.base, self.n = self.start + index * per, 0

            def leave(self, rounds):
                assert self.n == self.per, (self.n, self.per)
                self.base, self.n = self.start + rounds * self.per, 0

        def col(tile, i):
            return tile[:, bass.ds(i, 1)]

        def row(tile, i):
            return tile[:, bass.ds(i, 1), :].rearrange("p a t -> p (a t)")

        def ratio_of(layer):
            return ratio[:, layer * GROUPS:(layer + 1) * GROUPS, :].rearrange("p g t -> p (g t)")\
                .rearrange("p (k t c) -> p t k c", k=KT, t=TILES)

        block = ctx.enter_context(nc.Block())

        @block.sync
        def _(sp):
            sp.dma_start(wu[:, :, :, :], wu_in).then_inc(ld_small, 16)
            sp.dma_start(cond, cond_in).then_inc(ld_small, 16)
            for i, part in enumerate(BATCH_PARTS):
                sp.dma_start(by_batch(v_cb[:, :, :])[:, :, part, :], by_batch(side_in)[:, :, part, :])\
                  .then_inc(ld_side[i], 16)
            sp.dma_start(x_tok[:, :, :], x_in.rearrange("(t p) c -> p t c", p=P)).then_inc(ld_x, 16)
            sp.dma_start(gw[0][:, :, :], gw0_in).then_inc(ld_gate, 16)
            sp.dma_start(gw[1][:, :, :], gw1_in).then_inc(ld_gate, 16)
            sp.dma_start(idx2[:, :], idx2_in).then_inc(ld_idx2, 16)
            sp.wait_ge(zeros_set, 1)
            for i in range(T0 // TILES):
                sp.dma_start(slots0[i * TOK:(i + 1) * TOK, :].rearrange("(p r) c -> p (r c)", p=P), zeros)\
                  .then_inc(zeros_put, 16)
            sp.dma_start(slots1[0:TOK, :].rearrange("(p r) c -> p (r c)", p=P), zeros).then_inc(zeros_put, 16)
            for src, dst in ((w1_0_in, w1_0), (w3_0_in, w3_0), (w2_0_in, w2_0)):
                sp.dma_start(dst, src).then_inc(ld_w0, 16)

            def load_slots(S, slots, t, turned):
                if turned is not None:
                    sp.wait_ge(S.xT_ps, turned)
                sp.dma_start(xg[:, :], slots[bass.ds(t * P, P), :]).then_inc(S.x_in, 16)

            def store_results(S, ys, t, made):
                sp.wait_ge(S.y_sb, made)
                sp.dma_start(ys[bass.ds(t * P, P), :], y_b[:, :]).then_inc(S.y_out, 16)

            sp.wait_ge(scattered0, 16 * 2 * TILES)
            load_slots(S0, slots0, 0, None)
            load_slots(S0, slots0, 1, 1)
            with sp.Fori(0, T0 - 2) as t:
                load_slots(S0, slots0, t + 2, t + 2)
                store_results(S0, ys0, t, t + 1)
            for t in (T0 - 2, T0 - 1):
                store_results(S0, ys0, t, t + 1)

            for src, dst in ((w1_1_in, w1_1), (w3_1_in, w3_1), (w2_1_in, w2_1)):
                sp.dma_start(dst[:, :, 0:1, :], src[:, :, 0:1, :]).then_inc(ld_shared1, 16)
            for t, e0, e1 in ((0, 1, 2), (2, 2, 3), (TILES - 1, 3, 5), (TILES - 1, 5, 7), (TILES - 1, 7, 9)):
                sp.wait_ge(gathered[t], 32)
                for src, dst in ((w1_1_in, w1_1), (w3_1_in, w3_1), (w2_1_in, w2_1)):
                    sp.dma_start(dst[:, :, e0:e1, :], src[:, :, e0:e1, :]).then_inc(ld_w1, 16)
            sp.wait_ge(scattered1, 16 * TILES)
            for t in range(2):
                load_slots(S1, slots1, t, AHEAD + t)
            with sp.Fori(0, E - 2) as t:
                load_slots(S1, slots1, t + 2, t + AHEAD + 2)
            sp.wait_ge(S1.up_ps, AHEAD + E)
            sp.dma_start(rawd2, down2_in).then_inc(ld_rawd2, 16)

            with sp.Fori(0, TILES) as t:
                sp.wait_ge(S23.y_sb, t + TILES + 1)
                sp.dma_start(out[bass.ds(t * P, P), :], x_tok[:, bass.ds(t, 1), :].rearrange("p a c -> p (a c)"))\
                  .then_inc(out_put, 16)
            sp.wait_ge(out_put, 16 * TILES)

        @block.gpsimd
        def _(pool):
            steps = Steps(pool, pool_step)
            pool.memset(zeros, 0.0).then_inc(zeros_set, 1)
            steps.link(pool.memset(ident[:, :], 0.0))
            steps.link(pool.memset(ones[:, :], 1.0))
            steps.link(pool.memset(ones_row, 1.0))
            pool.memset(one_hot[:, :, :], 0.0).then_inc(consts, 1)
            for x in laters:
                pool.memset(x[:, :, TIME:TIME + 1], 0.0).then_inc(consts, 1)
            pool.affine_select(out=ident[:, :], in_=ident[:, :], compare_op=ALU.not_equal, fill=1.0, base=0,
                               pattern=[[-1, P]], channel_multiplier=1).then_inc(consts, 1)
            pool.affine_select(out=tri[:, :], in_=ones[:, :], compare_op=ALU.is_ge, fill=0.0, base=-1,
                               pattern=[[1, P]], channel_multiplier=-1).then_inc(consts, 1)
            for tile, base, pattern, mult in (
                    (rev8[:, :], E, [[-1, E]], 0), (e128[:, :], 0, [[P, E]], 0), (tile_no[:, :], 0, [[1, T0]], 0),
                    (tok_no[:, :], TOK, [[P, TILES]], 1), (row_no[:, :], 0, [[P, GU2]], 1)):
                pool.iota(tile, pattern=pattern, base=base, channel_multiplier=mult,
                          allow_small_or_imprecise_dtypes=True).then_inc(consts, 1)

            def gather2(r, dst, semaphore):
                pool.indirect_dma_start(
                    out=dst, out_offset=None, in_=gu2_in,
                    in_offset=bass.IndirectOffsetOnAxis(ap=idx2[:, r:r + 1].bitcast(U32), axis=0)).then_inc(semaphore, 16)

            def wkv_inputs(n, j, g, first=False, meanwhile=(), add_own=True):
                if not first:
                    pool.wait_ge(bwd_scanned[1], n)
                pool.tensor_tensor(scan_in[:, 1, :], row(ek, g), ones_row, ALU.mult).then_inc(scan_ready, 1)
                if not first:
                    pool.wait_ge(bwd_scanned[0], n)
                pool.tensor_tensor(scan_in[:, 0, :], row(ek, g), row(v_cb, g), ALU.mult).then_inc(scan_ready, 1)
                if not first:
                    pool.wait_ge(own_added, n)
                pool.tensor_tensor(own, row(ratio, j), row(v_cb, g), ALU.mult).then_inc(own_ready, 1)
                for r in meanwhile:
                    gather2(r, raw2[:, r, :], ld_raw2)
                if add_own:
                    pool.wait_ge(own_ready, n + 1)
                    pool.wait_ge(sums_joined, n + 1)
                    pool.tensor_tensor(acc[:, 0, :], acc[:, 0, :], own, ALU.add).then_inc(own_added, 1)

            pool.wait_ge(ek_exp, 1)
            pool.wait_ge(euk_exp, KT)
            wkv_inputs(0, 0, 0, first=True, add_own=False)
            wkv_inputs(1, BATCH, BATCH, add_own=False)
            pool.wait_ge(ek_exp, 2)
            pool.wait_ge(euk_exp, EUK0)
            with pool.Fori(1, BATCH) as b:
                for k in range(KT):
                    wkv_inputs(KT * b + k, k * BATCH + b, k * BATCH + b, add_own=False)
            pool.wait_ge(zeros_put, 16 * (T0 // TILES + 1))
            pool.wait_ge(routed, 1)
            for t in range(TILES):
                for slot in (slot_a, slot_b):
                    pool.indirect_dma_start(
                        out=slots0, out_offset=bass.IndirectOffsetOnAxis(ap=slot[:, t:t + 1].bitcast(U32), axis=0),
                        in_=c0[:, t, :], in_offset=None).then_inc(scattered0, 16)
            pool.wait_ge(euk_exp, EUK0 + KT)
            pool.wait_ge(scattered0, 16 * 2 * TILES)
            pool.wait_ge(idx2_set, 1)
            assert GROUPS - EARLY == U2
            for g in range(EARLY, GROUPS):
                wkv_inputs(GROUPS + g, GROUPS + g, g, meanwhile=(2 * (g - EARLY), 2 * (g - EARLY) + 1))
            pool.wait_ge(euk_exp, EUK0 + (LAYERS - 1) * KT)
            for layer in (2, 3):
                with pool.Fori(0, GROUPS) as g:
                    wkv_inputs(layer * GROUPS + g, layer * GROUPS + g, g)
            pool.wait_ge(S0.y_out, 16 * T0)
            pool.wait_ge(grp_made, LAYERS * GROUPS)
            pool.wait_ge(own_ready, LAYERS * GROUPS)
            for t in range(TILES):
                for rows, slot in ((back_a, slot_a), (back_b, slot_b)):
                    pool.indirect_dma_start(
                        out=rows[:, t, :], out_offset=None, in_=ys0,
                        in_offset=bass.IndirectOffsetOnAxis(ap=slot[:, t:t + 1].bitcast(U32), axis=0))\
                        .then_inc(gathered[t], 16)
            def load_unit3(u, i):
                pool.dma_start(raw3[:, i, :], w3q_in[bass.ds(u, 1), :, :].rearrange("a p c -> (a p) c"))\
                    .then_inc(ld_raw3[i], 16)

            pool.wait_ge(wq_made, U2)
            for i in range(2):
                load_unit3(i, i)
            pool.wait_ge(routed, 2)
            for t in range(TILES):
                pool.indirect_dma_start(
                    out=slots1, out_offset=bass.IndirectOffsetOnAxis(ap=slot_w1[:, t:t + 1].bitcast(U32), axis=0),
                    in_=c_tok[:, t, :], in_offset=None).then_inc(scattered1, 16)
            def unit3_result(u):
                pool.wait_ge(wq_rounded, u + 1)
                pool.wait_ge(wq_turned, U2 + u)
                blocks, s = (x.rearrange("p (b c) -> p b c", c=c) for x, c in ((wt_b[:, 0:WU], 32), (qs[:, 1, 0:WU // 32], 1)))
                pool.tensor_tensor(wq[:, 0:WU].rearrange("p (b c) -> p b c", c=32), blocks,
                                   s.to_broadcast([P, WU // 32, 32]), ALU.mult).then_inc(wq_made, 1)

            with pool.Fori(1, U3 // 2) as pair:
                for i in range(2):
                    unit3_result(2 * pair + i - 2)
                    load_unit3(2 * pair + i, i)
            unit3_result(U3 - 2)
            gather2(GU2 - 1, last2, ld_last2)
            unit3_result(U3 - 1)
            pool.wait_ge(S1.y_out, 16 * E)
            for t in range(TILES):
                pool.indirect_dma_start(
                    out=back1[:, t, :], out_offset=None, in_=ys1,
                    in_offset=bass.IndirectOffsetOnAxis(ap=slot_r1[:, t:t + 1].bitcast(U32), axis=0))\
                    .then_inc(gathered[t], 16)
            pool.wait_ge(S1.x_copied, TILES)
            for layer in (2, 3):
                with pool.Fori(0, TILES) as t:
                    pool.wait_ge(sig_done, 1 + TILES * (layer - 1) + t + 1)
                    if layer == 3:
                        pool.wait_ge(S23.x_copied, t + 1)
                    pool.tensor_tensor(row(c_tok, t).rearrange("p (k c) -> p k c", k=KT),
                                       row(sig, t).rearrange("p (k c) -> p k c", k=KT),
                                       ratio_of(layer)[:, bass.ds(t, 1), :, :].rearrange("p a k c -> p (a k) c"),
                                       ALU.mult).then_inc(c_tile_made, 1)

        @block.tensor
        def _(pe):
            def turn(dst, src, rows=P):
                return pe.transpose(dst, src, ident[0:rows, 0:rows])

            def turn_group(j):
                pe.wait_ge(grp_made, j + 1)
                pe.wait_ge(grp_kept, j)
                for h in range(2):
                    mm = turn(psR[:, h * P:(h + 1) * P], rbuf[:, h * P:(h + 1) * P])
                mm.then_inc(grp_turned, 1)

            cT = [hT_b[:, KT * i:KT * (i + 1), :] for i in range(2)]
            psC = [psA[:, 0:CH].rearrange("p (k t) -> p k t", k=KT), psB[:, 0:CH].rearrange("p (k t) -> p k t", k=KT)]

            def turn_c(layer, c, t):
                n = layer * TILES + t
                pe.wait_ge(c_made, n + 1)
                if t >= 2:
                    pe.wait_ge(cT_kept, n - 1)
                for k in range(KT):
                    mm = turn(psC[t % 2][:, k, :], c[:, t, k * P:(k + 1) * P])
                mm.then_inc(cT_turned, 1)

            def score(layer, t):
                pe.wait_ge(cT_kept, layer * TILES + t + 1)
                for k in range(KT):
                    mm = pe.matmul(psS[:, t, :], cT[t % 2][:, k, :], gw[layer][:, k, :],
                                   start=(k == 0), stop=(k == KT - 1))
                mm.then_inc(scored, 1)

            def rank(layer):
                pe.wait_ge(hot_set, layer + 1)
                mm = pe.matmul(psK[:, :, :], tri[:, :], one_hot[:, :, :], start=True, stop=False)
                for i in range(TILES):
                    n = TILES - i
                    mm = pe.matmul(psK[:, i + 1:TILES + 1, :], ones[:, :],
                                   one_hot[:, i:i + 1, :].to_broadcast([P, n, E]), start=False, stop=(i == TILES - 1))
                mm.then_inc(ranked, 1)

            def x_turn(S, t, ready, first=False):
                ready(t)
                if not first:
                    pe.wait_ge(S.xT_sb, t)
                for k in range(KT):
                    mm = turn(psX[:, k, :], xg[:, k * P:(k + 1) * P])
                mm.then_inc(S.xT_ps, 1)

            def in_product(S, ps, F, weights, done):
                for c in range(0, F, 512):
                    n = min(512, F - c)
                    for k in range(KT):
                        mm = pe.matmul(ps[:, c:c + n], xgT[:, k, :], weights(k, c, n), start=(k == 0), stop=(k == KT - 1))
                mm.then_inc(done, 1)

            def gate_up(S, t, F, wg, wu_, first=False):
                pe.wait_ge(S.xT_sb, t + 1)
                if not first:
                    pe.wait_ge(S.silu_sb, t)
                in_product(S, psA, F, wg, S.gate_ps)
                if not first:
                    pe.wait_ge(S.up_read, t)
                in_product(S, psB, F, wu_, S.up_ps)

            def h_turn(S, t, h, F, first=False):
                pe.wait_ge(S.h_sb, t + 1)
                if not first:
                    pe.wait_ge(S.hT_sb, t)
                for j in range((F + P - 1) // P):
                    n = min(P, F - j * P)
                    mm = turn(psH[0:n, j * P:(j + 1) * P], h[:, j * P:j * P + n])
                mm.then_inc(S.hT_ps, 1)

            def down(S, t, hT, F, wd, first=False):
                pe.wait_ge(S.hT_sb, t + 1)
                if not first:
                    pe.wait_ge(S.y_sb, t)
                J = (F + P - 1) // P
                for j in range(J):
                    n = min(P, F - j * P)
                    mm = pe.matmul(psY[:, :], hT[0:n, j, :], wd(j, n), start=(j == 0), stop=(j == J - 1))
                mm.then_inc(S.y_ps, 1)

            pe.wait_ge(consts, 10)

            def sum_group(n):
                k, b = n % KT, n // KT
                i, j = n % 2, k * BATCH + b
                if n >= 2:
                    pe.wait_ge(grp_made, n - 1)
                pe.wait_ge(fwd_scanned, 2 * n + 1)
                pe.wait_ge(bwd_scanned[1], n + 1)
                pe.matmul(ps_den[i], ident[:, :], accs[i][:, 1, :], start=True, stop=False)
                pe.matmul(ps_den[i], ident[:, :], laters[i][:, 1, 1:TIME + 1], start=False, stop=False)
                pe.wait_ge(euk_exp, KT if b == 0 else EUK0)
                pe.matmul(ps_den[i], ident[:, :], ratio[:, j, :], start=False, stop=True).then_inc(sums_joined, 1)
                pe.wait_ge(fwd_scanned, 2 * n + 2)
                pe.wait_ge(bwd_scanned[0], n + 1)
                pe.matmul(ps_num[i], ident[:, :], accs[i][:, 0, :], start=True, stop=False)
                pe.matmul(ps_num[i], ident[:, :], laters[i][:, 0, 1:TIME + 1], start=False, stop=False)
                pe.wait_ge(own_ready, n + 1)
                pe.matmul(ps_num[i], ident[:, :], own, start=False, stop=True).then_inc(own_added, 1)

            sum_group(0)
            sum_group(1)
            pe.wait_ge(grp_made, 1)
            for h in range(2):
                mm = turn(psR[:, h * P:(h + 1) * P], rbuf[:, h * P:(h + 1) * P])
            mm.then_inc(grp_turned, 1)
            pe.wait_ge(ld_gate, 32)
            for b in range(1, BATCH + 1):
                if b < BATCH:
                    for n in (KT * b, KT * b + 1):
                        sum_group(n)
                        turn_group(n - 1)
                else:
                    turn_group(GROUPS - 1)
                for t in (2 * b - 2, 2 * b - 1):
                    turn_c(0, c0, t)
                for t in (2 * b - 2, 2 * b - 1):
                    score(0, t)
            rank(0)
            for j in range(GROUPS, GROUPS + EARLY - 1):
                turn_group(j)

            def slots_in(S):
                return lambda t: pe.wait_ge(S.x_in, 16 * t + 16)

            def w0(t):
                e = pe.value_load(eid[0:1, bass.ds(t, 1)], min_val=0, max_val=E - 1)
                return [lambda k, c, n, w=w: w[:, k, bass.ds(e, 1), c:c + n].rearrange("p a f -> p (a f)")
                        for w in (w1_0, w3_0)]

            def wd0(t):
                e = pe.value_load(eid[0:1, bass.ds(t, 1)], min_val=0, max_val=E - 1)
                return lambda j, n: w2_0[0:n, j, bass.ds(e, 1), :].rearrange("p a f -> p (a f)")

            pe.wait_ge(ld_w0, 48)
            pe.wait_ge(routed, 1)
            x_turn(S0, 0, slots_in(S0), first=True)
            gate_up(S0, 0, F0, *w0(0), first=True)
            x_turn(S0, 1, slots_in(S0))
            turn_group(GROUPS + EARLY - 1)

            def step0(t, job, first=False, last=False):
                w_down, w_in = wd0(t - 1), w0(t)
                h_turn(S0, t - 1, h_b, F0, first=first)
                gate_up(S0, t, F0, *w_in)
                if not last:
                    x_turn(S0, t + 1, slots_in(S0))
                down(S0, t - 1, hT_b, F0, w_down, first=first)
                job()

            def turn_unit2(u, first=False):
                pe.wait_ge(wq_made, u + 1)
                if not first:
                    pe.wait_ge(wq_kept, u)
                for k in range(KT):
                    for r in range(2):
                        mm = turn(psW[:, 2 * k + r, :], wq[:, r * CH + k * P:r * CH + (k + 1) * P])
                mm.then_inc(wq_turned, 1)

            J0_ = GROUPS + EARLY
            G0 = LAYERS * GROUPS - J0_
            step0(1, lambda: turn_group(J0_), first=True)
            with pe.Fori(2, G0 + 1) as t:
                step0(t, lambda: turn_group(t + J0_ - 1))
            assert G0 == T0 - 3
            step0(T0 - 2, lambda: turn_unit2(0, first=True))
            step0(T0 - 1, lambda: turn_unit2(1), last=True)
            h_turn(S0, T0 - 1, h_b, F0)
            down(S0, T0 - 1, hT_b, F0, wd0(T0 - 1))
            for u in range(2, U2):
                turn_unit2(u)

            def turn_unit3(u):
                pe.wait_ge(wq_made, U2 + u + 1)
                pe.wait_ge(wq_kept, U2 + u)
                for k in range(4):
                    mm = turn(psW[:, k, :], wq[:, k * P:(k + 1) * P])
                mm.then_inc(wq_turned, 1)

            def w1e(e):
                return [lambda k, c, n, w=w: w[:, k, bass.ds(e, 1), c:c + n].rearrange("p a f -> p (a f)")
                        for w in (w1_1, w3_1)]

            def wd1(e):
                return lambda j, n: w2_1[0:n, j, bass.ds(e, 1), :].rearrange("p a f -> p (a f)")

            def turn_last2(i):
                pe.wait_ge(wq_made, U2 + U3 + i + 1)
                pe.wait_ge(wq_kept, U2 + U3 + i)
                for k in range(KT if i == 0 else J2):
                    cols = min(P, F2 - k * P)
                    dst = psW[0:cols, k, :] if k < 4 else psR[0:cols, (k - 4) * P:(k - 3) * P]
                    mm = turn(dst, wq[:, k * P:k * P + cols])
                mm.then_inc(wq_turned, 1)

            def shared(t):
                pe.wait_ge(S1.x_copied, t + 1)

            def expert(t):
                pe.wait_ge(S1.x_in, (t - AHEAD) * 16 + 16)

            def shared_late(t):
                pe.wait_ge(S1.x_copied, t - E + 1)

            for t in range(TILES):
                turn_c(1, c_tok, t)
                if t > 0:
                    score(1, t - 1)
                if t == TILES // 2 - 1:
                    x_turn(S1, 0, shared, first=True)
            score(1, TILES - 1)
            rank(1)
            pe.wait_ge(ld_shared1, 16 * 3)
            gate_up(S1, 0, F1, *w1e(0), first=True)
            x_turn(S1, 1, shared)

            def step1(t, e_in, e_down, ready, unit=None, rest=None, first=False, last=False):
                h_turn(S1, t - 1, h_b, F1, first=first)
                gate_up(S1, t, F1, *w1e(e_in))
                if not last:
                    x_turn(S1, t + 1, ready)
                down(S1, t - 1, hT_b, F1, wd1(e_down), first=first)
                if unit is not None:
                    turn_unit3(unit)
                if rest is not None:
                    turn_last2(rest)

            step1(1, 0, 0, shared, 0, first=True)
            with pe.Fori(2, AHEAD - 1) as t:
                step1(t, 0, 0, shared, t - 1)
            step1(AHEAD - 1, 0, 0, expert, AHEAD - 2)
            pe.wait_ge(ld_w1, 16 * 3 * 5)
            with pe.Fori(AHEAD, AHEAD + E - 1) as t:
                step1(t, t - AHEAD + 1, t - AHEAD, expert, t - 1)
            step1(AHEAD + E - 1, E, E - 1, shared_late, AHEAD + E - 2)
            assert U3 == AHEAD + E
            step1(AHEAD + E, 0, E, shared_late, U3 - 1)
            for t in range(U3 + 1, T1 - 1):
                step1(t, 0, 0, shared_late, rest=t - U3 - 1)
            assert T1 - 1 - U3 - 1 == 2
            step1(T1 - 1, 0, 0, shared_late, last=True)
            h_turn(S1, T1 - 1, h_b, F1)
            down(S1, T1 - 1, hT_b, F1, wd1(0))

            L2 = (F2, lambda k, c, n: gu2[:, k, c:c + n], lambda k, c, n: gu2[:, k, F2 + c:F2 + c + n],
                  lambda j, n: down2[0:n, j, :])
            L3 = (F3, lambda k, c, n: gate3[:, k, c:c + n], lambda k, c, n: up3[:, k, c:c + n],
                  lambda j, n: down3[0:n, j, :])

            def tile_ready(t):
                pe.wait_ge(S23.x_copied, t + 1)

            def gate(t, layer, first=False):
                pe.wait_ge(S23.xT_sb, t + 1)
                if not first:
                    pe.wait_ge(S23.silu_sb, t)
                in_product(S23, psA, layer[0], layer[1], S23.gate_ps)

            def up(t, layer, first=False):
                if not first:
                    pe.wait_ge(S23.up_read, t)
                in_product(S23, psB, layer[0], layer[2], S23.up_ps)

            def step(t, layers, first=False):
                before, now, then = layers
                up(t, now)
                x_turn(S23, t + 1, tile_ready)
                h_turn(S23, t - 1, h_q, before[0], first=first)
                gate(t + 1, then)
                down(S23, t - 1, hT_w, before[0], before[3], first=first)

            turn_last2(2)
            x_turn(S23, 0, tile_ready, first=True)
            pe.wait_ge(wq_kept, U2 + U3 + 3)
            gate(0, L2, first=True)
            up(0, L2, first=True)
            x_turn(S23, 1, tile_ready)
            gate(1, L2)
            step(1, (L2, L2, L2), first=True)
            with pe.Fori(2, TILES - 1) as t:
                step(t, (L2, L2, L2))
            step(TILES - 1, (L2, L2, L3))
            step(TILES, (L2, L3, L3))
            with pe.Fori(TILES + 1, 2 * TILES - 1) as t:
                step(t, (L3, L3, L3))
            up(2 * TILES - 1, L3)
            h_turn(S23, 2 * TILES - 2, h_q, F3)
            down(S23, 2 * TILES - 2, hT_w, F3, L3[3])
            for i in range(2):
                js = range(i * J3 // 2, (i + 1) * J3 // 2)
                pe.wait_ge(S23.h_sb, 2 * TILES + i)
                pe.wait_ge(S23.hT_sb, 2 * TILES - 1 + i)
                for j in js:
                    mm = turn(psH[:, j * P:(j + 1) * P], h_q[:, j * P:(j + 1) * P])
                mm.then_inc(S23.hT_ps, 1)
                pe.wait_ge(S23.hT_sb, 2 * TILES + i)
                pe.wait_ge(S23.y_sb, 2 * TILES - 1)
                for j in js:
                    mm = pe.matmul(psY[:, :], hT_w[:, j, :], L3[3](j, P), start=(j == 0), stop=(j == J3 - 1))
            mm.then_inc(S23.y_ps, 1)

        @block.scalar
        def _(act):
            def keep_group(n, j):
                act.wait_ge(grp_turned, n + 1)
                act.activation(ratio[:, bass.ds(j, 1), :].rearrange("p a t -> p (a t)"), psR, ACT.Copy)\
                   .then_inc(grp_kept, 1)

            def keep_cT(layer, t):
                n = layer * TILES + t
                act.wait_ge(cT_turned, n + 1)
                if t >= 2:
                    act.wait_ge(scored, n - 1)
                ps = (psA, psB)[t % 2]
                act.activation(hT_b[:, KT * (t % 2):KT * (t % 2 + 1), :].rearrange("p k t -> p (k t)"), ps[:, 0:CH], ACT.Copy)\
                   .then_inc(cT_kept, 1)

            def keep_xT(S, t, first=False):
                act.wait_ge(S.xT_ps, t + 1)
                if not first:
                    act.wait_ge(S.up_ps, t)
                act.activation(xgT[:, :, :], psX[:, :, :], ACT.Copy).then_inc(S.xT_sb, 1)

            def silu(S, t, dst, F, first=False):
                act.wait_ge(S.gate_ps, t + 1)
                if not first:
                    act.wait_ge(S.up_read, t)
                act.activation(dst[:, 0:F], psA[:, 0:F], ACT.Silu).then_inc(S.silu_sb, 1)

            def keep_hT(S, t, hT, F, first=False):
                act.wait_ge(S.hT_ps, t + 1)
                if not first:
                    act.wait_ge(S.y_ps, t)
                full, rest = F // P, F % P
                done = act.activation(hT[:, 0:full, :].rearrange("p j t -> p (j t)"), psH[:, 0:full * P], ACT.Copy)
                if rest:
                    done = act.activation(hT[0:rest, full, :], psH[0:rest, full * P:(full + 1) * P], ACT.Copy)
                done.then_inc(S.hT_sb, 1)

            act.wait_ge(tf_sum, 1)
            act.activation(tf[:, 1, :], tf[:, 0, :], ACT.Exp, scale=-1.0).then_inc(tf_exp, 1)
            act.activation(wu[:, 0, :, :], wu[:, 0, :, :], ACT.Exp).then_inc(w_exp, 1)
            act.wait_ge(w_exp, 1)
            act.activation(dec[:, :], wu[:, 0, :, :].rearrange("p l k -> p (l k)"), ACT.Exp, scale=-1.0)\
               .then_inc(dec_exp, 1)
            for i, part in enumerate(BATCH_PARTS):
                act.wait_ge(ek_min, i + 1)
                x = by_batch(ek[:, :, :])[:, :, part, :]
                act.activation(x, x, ACT.Exp).then_inc(ek_exp, 1)
                for k in range(KT):
                    act.wait_ge(euk_min, i * KT + k + 1)
                    x = ratio[:, k * BATCH + part.start:k * BATCH + part.stop, :]
                    act.activation(x, x, ACT.Exp).then_inc(euk_exp, 1)

            def exp_euk(layer):
                for k in range(KT):
                    act.wait_ge(euk_min, EUK0 + (layer - 1) * KT + k + 1)
                    x = ratio[:, (layer * KT + k) * BATCH:(layer * KT + k + 1) * BATCH, :]
                    act.activation(x, x, ACT.Exp).then_inc(euk_exp, 1)

            act.wait_ge(ld_x, 16)
            act.activation(sig0[:, :, :], x_tok[:, :, :], ACT.Sigmoid).then_inc(sig_done, 1)
            keep_group(0, 0)
            for b in range(1, BATCH + 1):
                for n in range(KT * b - 1, min(KT * b + 1, GROUPS)):
                    keep_group(n, n % KT * BATCH + n // KT)
                for t in (2 * b - 2, 2 * b - 1):
                    keep_cT(0, t)
            for layer in range(1, LAYERS):
                exp_euk(layer)
            act.wait_ge(exps_in, 1)
            act.activation(rt0[:, 10:12, :, :], rt0[:, 8:10, :, :], ACT.Exp, scale=-1.0).then_inc(exps_out, 1)
            for j in range(GROUPS, GROUPS + EARLY - 1):
                keep_group(j, j)

            keep_xT(S0, 0, first=True)
            silu(S0, 0, silu_b, F0, first=True)
            keep_xT(S0, 1)
            keep_group(GROUPS + EARLY - 1, GROUPS + EARLY - 1)

            def keep_y(S, t, stored):
                act.wait_ge(S.y_ps, t + 1)
                if stored is not None:
                    act.wait_ge(S.y_out, 16 * stored)
                act.activation(y_b[:, :], psY[:, :], ACT.Copy).then_inc(S.y_sb, 1)

            def keep_unit2(u):
                act.wait_ge(wq_turned, u + 1)
                act.activation(gu2[:, :, bass.ds(u * 2 * P, 2 * P)], psW.rearrange("p (k r) c -> p k (r c)", k=KT), ACT.Copy)\
                   .then_inc(wq_kept, 1)

            def step0(t, job, first=False, last=False):
                keep_hT(S0, t - 1, hT_b, F0, first=first)
                silu(S0, t, silu_b, F0)
                if not last:
                    keep_xT(S0, t + 1)
                keep_y(S0, t - 1, None if first else t - 1)
                job()

            J0_ = GROUPS + EARLY
            G0 = LAYERS * GROUPS - J0_
            step0(1, lambda: keep_group(J0_, J0_), first=True)
            with act.Fori(2, G0 + 1) as t:
                step0(t, lambda: keep_group(t + J0_ - 1, t + J0_ - 1))
            step0(T0 - 2, lambda: keep_unit2(0))
            step0(T0 - 1, lambda: keep_unit2(1), last=True)
            keep_hT(S0, T0 - 1, hT_b, F0)
            keep_y(S0, T0 - 1, T0 - 1)
            for u in range(2, U2):
                keep_unit2(u)

            def sigmoid_x(t, semaphore, n):
                act.wait_ge(semaphore, n)
                act.activation(sig[:, t, :], x_tok[:, t, :], ACT.Sigmoid).then_inc(sig_done, 1)

            def copy_x1(t):
                act.wait_ge(c_made, TILES + t + 1)
                act.activation(xg[:, :], row(c_tok, t), ACT.Copy).then_inc(S1.x_copied, 1)

            for t in range(TILES):
                sigmoid_x(t, gather_used, t + 1)
                if t > 1:
                    keep_cT(1, t - 2)
                if t == TILES // 2:
                    copy_x1(0)
                    keep_xT(S1, 0, first=True)
            for t in (TILES - 2, TILES - 1):
                keep_cT(1, t)
            copy_x1(1)
            act.wait_ge(exps_in, 2)
            act.activation(rt1[:, 10, :, :], rt1[:, 8, :, :], ACT.Exp, scale=-1.0).then_inc(exps_out, 1)

            def keep_gu3(i):
                act.wait_ge(wq_turned, U2 + i + 1)
                act.activation(r3[:, 0:4096].rearrange("p (m f) -> p m f", f=F3)[:, :, bass.ds(i * P, P)], psW[:, :, :],
                               ACT.Copy).then_inc(wq_kept, 1)

            def keep_down3(r, c):
                act.wait_ge(wq_turned, U2 + TILES + 2 * r + c + 1)
                act.activation(down3[:, 4 * c:4 * c + 4, r * P:(r + 1) * P], psW[:, :, :], ACT.Copy).then_inc(wq_kept, 1)

            def keep_last2(i):
                act.wait_ge(wq_turned, U2 + U3 + i + 1)
                if i == 0:
                    done = act.activation(gu2[:, :, (GU2 - 1) * P:GU2 * P], psW[:, 0:KT, :], ACT.Copy)
                else:
                    r, rest = i - 1, F2 % P
                    act.activation(down2[:, 0:4, r * P:(r + 1) * P], psW[:, :, :], ACT.Copy)
                    act.activation(down2[:, 4, r * P:(r + 1) * P], psR[:, 0:P], ACT.Copy)
                    done = act.activation(down2[0:rest, 5, r * P:(r + 1) * P], psR[0:rest, P:2 * P], ACT.Copy)
                done.then_inc(wq_kept, 1)

            silu(S1, 0, silu_b, F1, first=True)
            keep_xT(S1, 1)
            copy_x1(2)

            def keep_y1(t, stored):
                keep_y(S1, t, stored)
                act.wait_ge(S1.y_sb, t + 1)
                act.dma_start(ys1[bass.ds((t - AHEAD) * P, P), :], y_b[:, :]).then_inc(S1.y_out, 16)

            def step1(t, unit=None, copy=None, keep=None, first=False, last=False):
                keep_hT(S1, t - 1, hT_b, F1, first=first)
                silu(S1, t, silu_b, F1)
                if not last:
                    keep_xT(S1, t + 1)
                if copy is not None:
                    copy_x1(copy)
                if keep is not None:
                    keep()
                if unit:
                    unit()

            step1(1, lambda: keep_gu3(0), copy=3, first=True)
            with act.Fori(2, AHEAD + 1) as t:
                step1(t, lambda: keep_gu3(t - 1))
            step1(AHEAD + 1, lambda: keep_gu3(AHEAD), keep=lambda: keep_y1(AHEAD, None))
            with act.Fori(AHEAD + 2, TILES + 1) as t:
                step1(t, lambda: keep_gu3(t - 1), keep=lambda: keep_y1(t - 1, t - 1 - AHEAD))
            for t in range(TILES + 1, U3 + 1):
                step1(t, lambda: keep_down3((t - 1 - TILES) // 2, (t - 1 - TILES) % 2),
                      copy=(t + 2 - E if t + 2 >= AHEAD + E else None), keep=lambda: keep_y1(t - 1, t - 1 - AHEAD))
            for t in range(U3 + 1, T1 - 1):
                step1(t, lambda: keep_last2(t - U3 - 1), copy=(t + 2 - E if t + 2 < T1 else None))
            step1(T1 - 1, last=True)
            for t in range(AHEAD):
                sigmoid_x(t, gather_used, TILES + t + 1)
            keep_hT(S1, T1 - 1, hT_b, F1)

            keep_last2(2)
            keep_xT(S23, 0, first=True)
            for t in range(AHEAD, TILES):
                sigmoid_x(t, gather_used, TILES + t + 1)
            silu(S23, 0, silu_w, F2, first=True)
            keep_xT(S23, 1)
            silu(S23, 1, silu_w, F2)

            def sigmoid3(t):
                act.wait_ge(c_tile_made, t + 1)
                act.wait_ge(S23.y_sb, t + 1)
                act.activation(row(sig, t), row(x_tok, t), ACT.Sigmoid).then_inc(sig_done, 1)

            def step(t, F_before, F_then, sigmoid=None, first=False):
                if sigmoid is not None:
                    sigmoid3(sigmoid)
                keep_xT(S23, t + 1)
                keep_hT(S23, t - 1, hT_w, F_before, first=first)
                silu(S23, t + 1, silu_w, F_then)

            step(1, F2, F2, first=True)
            step(2, F2, F2)
            with act.Fori(3, TILES - 1) as t:
                step(t, F2, F2, t - 3)
            step(TILES - 1, F2, F3, TILES - 4)
            step(TILES, F2, F3, TILES - 3)
            step(TILES + 1, F3, F3, TILES - 2)
            step(TILES + 2, F3, F3, TILES - 1)
            with act.Fori(TILES + 3, 2 * TILES - 1) as t:
                step(t, F3, F3)
            keep_hT(S23, 2 * TILES - 2, hT_w, F3)
            act.wait_ge(S23.y_ps, 2 * TILES - 1)
            for i in range(2):
                act.wait_ge(S23.hT_ps, 2 * TILES + i)
                c = slice(i * F3 // 2, (i + 1) * F3 // 2)
                act.activation(hT_w.rearrange("p j t -> p (j t)")[:, c], psH[:, c], ACT.Copy).then_inc(S23.hT_sb, 1)

        @block.vector
        def _(dve):
            steps = Steps(dve, dve_step)
            link = steps.link
            tt, ts, stt = dve.tensor_tensor, dve.tensor_scalar, dve.scalar_tensor_tensor

            def wkv_group(n, j, g, first=False, reads=None):
                alone = reads is not None
                reads = reads or [scan_in[:, i, :] for i in range(2)]
                backwards = [x[:, TIME - 1::-1] for x in reads]
                d = col(decay, j)
                d_all = d.to_broadcast([P, TIME])
                if not first:
                    dve.wait_ge(grp_made, n)
                for made, i in enumerate((1, 0)):
                    dve.wait_ge(scan_ready, 2 * n + made + 1)
                    dve.tensor_tensor_scan(acc[:, i, :], d_all, reads[i], 0.0, ALU.mult, ALU.add)\
                        .then_inc(fwd_scanned, 1)
                    dve.tensor_tensor_scan(later[:, i, TIME - 1::-1], d_all, backwards[i], 0.0,
                                           ALU.mult, ALU.add).then_inc(bwd_scanned[i], 1)
                dve.wait_ge(fwd_scanned, 2 * n + 1)
                dve.wait_ge(bwd_scanned[1], n + 1)
                steps.pair(stt(acc[:, 1, :], later[:, 1, 1:TIME + 1], d, acc[:, 1, :], ALU.mult, ALU.add))
                dve.wait_ge(fwd_scanned, 2 * n + 2)
                dve.wait_ge(bwd_scanned[0], n + 1)
                stt(acc[:, 0, :], later[:, 0, 1:TIME + 1], d, acc[:, 0, :], ALU.mult, ALU.add).then_inc(sums_joined, 1)
                steps.all()
                link(tt(acc[:, 1, :], acc[:, 1, :], row(ratio, j), ALU.add))
                if alone:
                    dve.wait_ge(own_ready, n + 1)
                    dve.wait_ge(sums_joined, n + 1)
                    tt(acc[:, 0, :], acc[:, 0, :], own, ALU.add).then_inc(own_added, 1)
                link(ts(acc[:, 1, :], acc[:, 1, :], 1e-8, None, ALU.max))
                link(dve.reciprocal(acc[:, 1, :], acc[:, 1, :]))
                dve.wait_ge(own_added, n + 1)
                if not first:
                    dve.wait_ge(grp_turned, n)
                stt(rbuf[:, :], acc[:, 0, :], col(tfo, g), acc[:, 1, :], ALU.mult, ALU.mult).then_inc(grp_made, 1)

            WKV_STEPS = 4

            def scan_group0(n, k, j, first=False):
                if not first:
                    dve.wait_ge(own_added, n - 1)
                d = col(decay, j).to_broadcast([P, TIME])
                for made, i in enumerate((1, 0)):
                    dve.wait_ge(scan_ready, 2 * n + made + 1)
                    dve.tensor_tensor_scan(accs[k][:, i, :], d, scan_in[:, i, :], 0.0, ALU.mult, ALU.add)\
                        .then_inc(fwd_scanned, 1)
                    dve.tensor_tensor_scan(laters[k][:, i, TIME - 1::-1], scan_in[:, i, TIME - 1::-1], d, 0.0,
                                           ALU.add, ALU.mult).then_inc(bwd_scanned[i], 1)

            def divide_group0(n, k, g, first=False):
                if not first:
                    dve.wait_ge(grp_made, n)
                dve.wait_ge(sums_joined, n + 1)
                link(ts(inverse0, ps_den[k], 1e-8, None, ALU.max))
                link(dve.reciprocal(inverse0, inverse0))
                dve.wait_ge(own_added, n + 1)
                if not first:
                    dve.wait_ge(grp_turned, n)
                stt(rbuf[:, :], ps_num[k], col(tfo, g), inverse0, ALU.mult, ALU.mult).then_inc(grp_made, 1)

            def early_group(j, g):
                dve.wait_ge(bwd_scanned[0], j)
                tt(scan_in[:, 0, :], ek[:, g, :], v_cb[:, g, :], ALU.mult).then_inc(scan_ready, 2)
                dve.wait_ge(own_added, j)
                tt(own, ratio[:, j, :], v_cb[:, g, :], ALU.mult).then_inc(own_ready, 1)
                wkv_group(j, j, g, reads=[scan_in[:, 0, :], ek[:, g, :]])

            def make_c(layer, c, sg, t):
                tt(row(c, t).rearrange("p (k c) -> p k c", k=KT), row(sg, t).rearrange("p (k c) -> p k c", k=KT),
                   ratio_of(layer)[:, bass.ds(t, 1), :, :].rearrange("p a k c -> p (a k) c"), ALU.mult)\
                    .then_inc(c_made, 1)

            V = [rs[:, i, :] for i in range(16)]

            def over_e(vec):
                return vec.rearrange("p (t o) -> p t o", o=1).to_broadcast([P, TILES, E])

            def over_t(vec):
                return vec.rearrange("p (o e) -> p o e", o=1).to_broadcast([P, TILES, E])

            def reduce_e(dst, src, op):
                link(dve.tensor_reduce(out=dst, in_=src, axis=AX.X, op=op))

            def first_max(score, top, hot, tmp):
                reduce_e(top, score, ALU.max)
                link(tt(tmp, score, over_e(top), ALU.is_equal))
                link(tt(tmp, tmp, over_t(rev8[:, :]), ALU.mult))
                reduce_e(V[15], tmp, ALU.max)
                link(tt(hot, tmp, over_e(V[15]), ALU.is_equal))

            def route0():
                R = [rt0[:, i, :, :] for i in range(NR)]
                s, hot1, hot2, tmp, ab, s_rest, keep1, keep2 = R[0:8]
                dve.wait_ge(scored, TILES)
                link(dve.tensor_copy(s, psS[:, :, :]))
                first_max(s, V[0], hot1, tmp)
                link(stt(s_rest, hot1, -1e30, s, ALU.mult, ALU.add))
                first_max(s_rest, V[1], hot2, tmp)
                dve.wait_ge(consts, 10)
                tt(one_hot[:, 0:TILES, :], hot1, hot2, ALU.add).then_inc(hot_set, 1)
                dve.wait_ge(ranked, 1)
                link(dve.tensor_copy(cnt[:, 0, :], psK[:, TILES, :]))
                link(tt(cmpb[:, :, :], cnt[:, 0, :].rearrange("p (e o) -> p e o", o=1).to_broadcast([P, E, TILES]),
                        e128[:, :].rearrange("p (o t) -> p o t", o=1).to_broadcast([P, E, TILES]), ALU.is_gt))
                link(dve.tensor_reduce(out=cnt[:, 1, :], in_=cmpb[:, :, :], axis=AX.X, op=ALU.add))
                link(dve.memset(cnt[:, 3, :], 1.0))
                link(dve.tensor_tensor_scan(cnt[:, 2, :], cnt[:, 3, :], cnt[:, 1, :], 0.0, ALU.mult, ALU.add))
                link(tt(cnt[:, 3, :], cnt[:, 2, :], cnt[:, 1, :], ALU.subtract))
                link(ts(cnt[:, 3, :], cnt[:, 3, :], float(P), None, ALU.mult))
                link(tt(tmp, psK[:, 0:TILES, :], over_t(cnt[:, 3, :]), ALU.add))
                for hot, v, slot in ((hot1, V[4], slot_a), (hot2, V[5], slot_b)):
                    link(tt(ab, hot, tmp, ALU.mult))
                    reduce_e(v, ab, ALU.add)
                    link(dve.tensor_copy(slot[:, :], v))
                link(tt(cmpt[:, :, :], cnt[0:1, 2, :].rearrange("p (o e) -> p o e", o=1).to_broadcast([1, T0, E]),
                        tile_no[:, :].rearrange("p (t o) -> p t o", o=1).to_broadcast([1, T0, E]), ALU.is_le))
                link(dve.tensor_reduce(out=eid_f[:, :], in_=cmpt[:, :, :], axis=AX.X, op=ALU.add))
                link(ts(eid_f[:, :], eid_f[:, :], float(E - 1), None, ALU.min))
                dve.tensor_copy(eid[:, :], eid_f[:, :]).then_inc(routed, 1)
                link(stt(ab, s, -1.0, s, ALU.mult, ALU.max))
                for top, keep, diff in ((V[0], keep1, R[8]), (V[1], keep2, R[9])):
                    link(tt(diff, over_e(top), s, ALU.subtract))
                    link(tt(tmp, ab, over_e(top), ALU.max))
                    link(ts(tmp, tmp, 0.02, None, ALU.mult))
                    link(tt(keep, diff, tmp, ALU.is_le))
                link(ts(R[9], R[9], 0.0, None, ALU.max))
                link(ts(tmp, hot1, -1.0, 1.0, ALU.mult, ALU.add))
                tt(keep2, keep2, tmp, ALU.mult).then_inc(exps_in, 1)
                dve.wait_ge(exps_in, 1)
                dve.wait_ge(exps_out, 1)
                for keep, ex, m in ((keep1, R[10], V[2]), (keep2, R[11], V[3])):
                    link(tt(ex, ex, keep, ALU.mult))
                    reduce_e(m, ex, ALU.add)
                    link(dve.reciprocal(m, m))

            def route1():
                R = [rt1[:, i, :, :] for i in range(NR)]
                s, hot1, _, tmp, ab = R[0:5]
                dve.wait_ge(scored, 2 * TILES)
                link(dve.tensor_copy(s, psS[:, :, :]))
                first_max(s, V[6], hot1, tmp)
                dve.tensor_copy(one_hot[:, 0:TILES, :], hot1).then_inc(hot_set, 1)
                tt(R[8], over_e(V[6]), s, ALU.subtract).then_inc(exps_in, 1)
                dve.wait_ge(exps_out, 2)
                reduce_e(V[7], R[10], ALU.add)
                link(dve.reciprocal(V[7], V[7]))
                dve.wait_ge(ranked, 2)
                link(tt(ab, hot1, psK[:, 0:TILES, :], ALU.mult))
                reduce_e(V[8], ab, ALU.add)
                link(tt(ab, hot1, over_t(e128[:, :]), ALU.mult))
                reduce_e(V[9], ab, ALU.add)
                link(ts(V[10], V[8], float(CAP), None, ALU.is_lt))
                link(tt(V[7], V[7], V[10], ALU.mult))
                link(tt(V[11], V[8], V[9], ALU.add))
                link(tt(V[11], V[11], V[10], ALU.mult))
                link(ts(V[12], V[10], -1.0, 1.0, ALU.mult, ALU.add))
                link(tt(V[13], V[12], tok_no[:, :], ALU.mult))
                link(tt(V[13], V[13], V[11], ALU.add))
                link(dve.tensor_copy(slot_w1[:, :], V[13]))
                link(stt(V[14], V[12], float(TOK - 1), V[11], ALU.mult, ALU.add))
                dve.tensor_copy(slot_r1[:, :], V[14]).then_inc(routed, 1)

            class Quant:
                def __init__(self, src, dst, a, b, q, size, least):
                    self.src, self.dst, self.a, self.b, self.q = src, dst, a, b, q
                    self.size, self.least, self.blocks = size, least, src.shape[-1] // size

                def scaled(self, dst, src, i):
                    if self.blocks == 1:
                        return ts(dst, src, self.q[:, i, 0:1], None, ALU.mult)
                    per_block = self.q[:, i, 0:self.blocks].rearrange("p (b o) -> p b o", o=1)
                    return tt(dst.rearrange("p (b c) -> p b c", c=self.size), src.rearrange("p (b c) -> p b c", c=self.size),
                              per_block.to_broadcast([P, self.blocks, self.size]), ALU.mult)

                def largest(self):
                    return dve.tensor_reduce(out=self.q[:, 0, 0:self.blocks],
                                             in_=self.src.rearrange("p (b c) -> p b c", c=self.size),
                                             axis=AX.X, op=ALU.max, apply_absolute_value=True)

                def scale(self):
                    q = self.q[:, :, 0:self.blocks]
                    if self.least is None:
                        return ts(q[:, 1, :], q[:, 0, :], 1.0 / FP8_MAX, None, ALU.mult)
                    return ts(q[:, 1, :], q[:, 0, :], 1.0 / FP8_MAX, self.least, ALU.mult, ALU.max)

                def inverse(self):
                    return dve.reciprocal(self.q[:, 2, 0:self.blocks], self.q[:, 1, 0:self.blocks])

                def divided(self):
                    return self.scaled(self.b, self.src, 2)

                def exponent(self):
                    return ts(self.a.bitcast(U32), self.b.bitcast(U32), EXPONENT, None, ALU.bitwise_and)

                def magic(self):
                    return ts(self.a, self.a, MIN_NORMAL, ROUND, ALU.max, ALU.mult)

                def add(self):
                    return tt(self.b, self.b, self.a, ALU.add)

                def subtract(self):
                    return tt(self.b, self.b, self.a, ALU.subtract)

                def result(self):
                    return self.scaled(self.dst, self.b, 1)

            def quantise(z):
                link(z.largest())
                link(z.scale())
                link(z.inverse())
                link(z.divided())
                link(z.exponent())
                link(z.magic())
                link(z.add())
                link(z.subtract())

            QUANT_STEPS = 8

            def make_h(S, t, src, dst, F, first=False):
                dve.wait_ge(S.silu_sb, t + 1)
                dve.wait_ge(S.up_ps, t + 1)
                if not first:
                    dve.wait_ge(S.hT_ps, t)
                return tt(dst[:, 0:F], src[:, 0:F], psB[:, 0:F], ALU.mult)

            dve.wait_ge(ld_small, 32)
            dve.tensor_reduce(out=tf[:, 0, :], in_=cond, axis=AX.X, op=ALU.add).then_inc(tf_sum, 1)
            for i, part in enumerate(BATCH_PARTS):
                dve.wait_ge(ld_side[i], 16)
                ts(by_batch(ek[:, :, :])[:, :, part, :], by_batch(v_cb[:, :, :])[:, :, part, :], 30.0, None, ALU.min)\
                    .then_inc(ek_min, 1)
                for k in range(KT):
                    g = slice(k * BATCH + part.start, k * BATCH + part.stop)
                    ts(ratio[:, g, :], v_cb[:, g, :], wu[:, 1, 0, k:k + 1], 30.0, ALU.add, ALU.min).then_inc(euk_min, 1)

            dve.wait_ge(tf_exp, 1)
            link(ts(tf[:, 1, :], tf[:, 1, :], 1.0, None, ALU.add))
            link(dve.reciprocal(tf[:, 1, :], tf[:, 1, :]))
            link(ts(tf[:, 2, :], tf[:, 1, :], 0.5, 0.5, ALU.mult, ALU.add))
            link(ts(tf[:, 3, :], tf[:, 1, :], 0.2, 0.8, ALU.mult, ALU.add))
            link(dve.tensor_copy(tfo[:, :].rearrange("p (k b) -> p k b", k=KT),
                                 tf[:, 3:4, :].to_broadcast([P, KT, BATCH])))
            dve.wait_ge(dec_exp, 1)
            link(tt(decay[:, :].rearrange("p (l b) -> p l b", b=BATCH),
                    dec[:, :].rearrange("p (l o) -> p l o", o=1).to_broadcast([P, LAYERS * KT, BATCH]),
                    tf[:, 2:3, :].to_broadcast([P, LAYERS * KT, BATCH]), ALU.mult))
            dve.wait_ge(consts, 10)

            assert KT == 2
            scan_group0(0, 0, 0, first=True)
            scan_group0(1, 1, BATCH, first=True)
            divide_group0(0, 0, 0, first=True)
            dve.wait_ge(sig_done, 1)
            with dve.Fori(1, BATCH) as b:
                steps.enter(b - 1, KT * 2)
                scan_group0(KT * b, 0, b)
                divide_group0(KT * b - 1, 1, BATCH + b - 1)
                scan_group0(KT * b + 1, 1, BATCH + b)
                divide_group0(KT * b, 0, b)
                dve.wait_ge(grp_kept, KT * b)
                for i in range(TILES // BATCH):
                    make_c(0, c0, sig0, TILES // BATCH * (b - 1) + i)
            steps.leave(BATCH - 1)
            divide_group0(GROUPS - 1, 1, GROUPS - 1)
            dve.wait_ge(grp_kept, GROUPS)
            for t in range(TILES - TILES // BATCH, TILES):
                make_c(0, c0, sig0, t)
            for layer in range(1, LAYERS):
                for k in range(KT):
                    g = layer * GROUPS + k * BATCH
                    ts(ratio[:, g:g + BATCH, :], v_cb[:, k * BATCH:(k + 1) * BATCH, :], wu[:, 1, layer, k:k + 1], 30.0,
                       ALU.add, ALU.min).then_inc(euk_min, 1)
            route0()

            dve.wait_ge(ld_idx2, 16)
            link(ts(row_no[:, :], row_no[:, :], float(F2), float(F2), ALU.is_ge, ALU.mult))
            link(dve.tensor_copy(idx2f[:, :], idx2[:, :]))
            link(tt(idx2f[:, :], idx2f[:, :], row_no[:, :], ALU.add))
            dve.tensor_copy(idx2[:, :], idx2f[:, :]).then_inc(idx2_set, 1)

            dve.wait_ge(euk_exp, EUK0 + KT)
            for g in range(EARLY):
                early_group(GROUPS + g, g)

            def h0(t, first=False):
                make_h(S0, t, silu_b, h_b, F0, first=first).then_inc(S0.h_sb, 1)

            for g in range(EARLY, GROUPS):
                h0(g - EARLY, first=(g == EARLY))
                wkv_group(GROUPS + g, GROUPS + g, g)
            for layer in (2, 3):
                with dve.Fori(0, GROUPS) as g:
                    steps.enter(g, WKV_STEPS)
                    h0(g + (layer - 1) * GROUPS - EARLY)
                    wkv_group(layer * GROUPS + g, layer * GROUPS + g, g)
                steps.leave(GROUPS)
            G0 = LAYERS * GROUPS - GROUPS - EARLY

            def quant2(u, first=False):
                z = Quant(r3[:, bass.ds(u * WU, WU)], wq[:, 0:WU], wt_a[:, 0:WU], wt_b[:, 0:WU], qs, CH, None)
                quantise(z)
                if not first:
                    dve.wait_ge(wq_turned, u)
                z.result().then_inc(wq_made, 1)

            dve.wait_ge(ld_raw2, 16 * 2 * U2)
            for u in range(U2):
                if G0 + u < T0:
                    h0(G0 + u)
                quant2(u, first=(u == 0))

            for t in range(TILES):
                dve.wait_ge(gathered[t], 32)
                link(stt(x_tok[:, t, :], back_a[:, t, :], V[2][:, t:t + 1], x_tok[:, t, :], ALU.mult, ALU.add))
                stt(x_tok[:, t, :], back_b[:, t, :], V[3][:, t:t + 1], x_tok[:, t, :], ALU.mult, ALU.add)\
                    .then_inc(gather_used, 1)
                if t > 0:
                    dve.wait_ge(sig_done, 1 + t)
                    make_c(1, c_tok, sig, t - 1)

            dve.wait_ge(sig_done, 1 + TILES)
            make_c(1, c_tok, sig, TILES - 1)
            route1()

            def quant3(u, i, pair):
                dve.wait_ge(ld_raw3[i], 16 * pair + 16)
                z = Quant(raw3[:, i, :], wq[:, 0:WU], wt_a[:, 0:WU], wt_b[:, 0:WU], qs, 32, 1e-30)
                link(z.largest())
                dve.wait_ge(wq_made, U2 + u)
                link(z.scale())
                link(z.inverse())
                link(z.divided())
                link(z.exponent())
                link(z.magic())
                link(z.add())
                z.subtract().then_inc(wq_rounded, 1)

            def add_y(S, t, tile):
                dve.wait_ge(S.y_ps, t + 1)
                tt(row(x_tok, tile), row(x_tok, tile), psY[:, :], ALU.add).then_inc(S.y_sb, 1)

            def h1(t, first=False):
                make_h(S1, t, silu_b, h_b, F1, first=first).then_inc(S1.h_sb, 1)

            for t in range(AHEAD + 2):
                h1(t, first=(t == 0))
                quant3(t, t % 2, t // 2)
                if 1 <= t <= AHEAD:
                    add_y(S1, t - 1, t - 1)
            with dve.Fori((AHEAD + 2) // 2, U3 // 2) as pair:
                steps.enter(pair - (AHEAD + 2) // 2, 2 * (QUANT_STEPS - 1))
                for i in range(2):
                    h1(2 * pair + i)
                    quant3(2 * pair + i, i, pair)
            steps.leave(U3 // 2 - (AHEAD + 2) // 2)
            def rest2(src, q):
                w = src.shape[-1]
                return Quant(src, wq[:, 0:w], wt_a[:, 0:w], wt_b[:, 0:w], q, w, None)

            last_up, down_a, down_b = rest2(last2, qs), rest2(rawd2[:, 0, :], qs), rest2(rawd2[:, 1, :], qs)

            def finish(z, n):
                dve.wait_ge(wq_turned, n)
                z.result().then_inc(wq_made, 1)

            def combine1(t):
                dve.wait_ge(gathered[t], 48)
                stt(x_tok[:, t, :], back1[:, t, :], V[7][:, t:t + 1], x_tok[:, t, :], ALU.mult, ALU.add)\
                    .then_inc(gather_used, 1)

            h1(U3)
            dve.wait_ge(ld_last2, 16)
            dve.wait_ge(wq_made, U2 + U3)
            quantise(last_up)
            finish(last_up, U2 + U3)
            dve.wait_ge(ld_rawd2, 16)
            link(down_a.largest())
            link(down_a.scale())
            link(down_a.inverse())
            h1(U3 + 1)
            add_y(S1, U3, U3 - E)
            link(down_a.divided())
            link(down_a.exponent())
            link(down_a.magic())
            link(down_a.add())
            link(down_a.subtract())
            finish(down_a, U2 + U3 + 1)
            h1(U3 + 2)
            add_y(S1, U3 + 1, U3 + 1 - E)
            dve.wait_ge(S1.y_sb, AHEAD)
            for t in range(AHEAD):
                combine1(t)
            link(down_b.largest())
            link(down_b.scale())
            link(down_b.inverse())
            link(down_b.divided())
            link(down_b.exponent())
            link(down_b.magic())
            h1(U3 + 3)
            add_y(S1, U3 + 2, U3 + 2 - E)
            def x_quant(tile, size, least):
                return Quant(row(c_tok, tile), xg[:, :], x_a, x_b, xs, size, least)

            def h_quant(F, size, least):
                return Quant(h_w[:, 0:F], h_q[:, 0:F], q_a[:, 0:F], q_b[:, 0:F], qs, size, least)

            def make_h23(t, F):
                dve.wait_ge(S23.silu_sb, t + 1)
                dve.wait_ge(S23.up_ps, t + 1)
                tt(h_w[:, 0:F], silu_w[:, 0:F], psB[:, 0:F], ALU.mult).then_inc(S23.up_read, 1)

            X2, X3 = (CH, None), (32, 1e-30)
            H2, H3 = (F2, F2, None), (F3, 32, 1e-30)

            def only_x(t):
                z = x_quant(t, *X2)
                dve.wait_ge(c_tile_made, t + 1)
                quantise(z)
                dve.wait_ge(S23.xT_ps, t)
                z.result().then_inc(S23.x_copied, 1)

            def h_and_x(t, H, X, tile, tile_y, first=False):
                h, x = h_quant(*H), x_quant(tile, *X)
                make_h23(t, H[0])
                dve.wait_ge(c_tile_made, t + 3)
                steps.pair(x.largest())
                dve.wait_ge(S23.up_read, t + 1)
                steps.pair(h.largest())
                for step in (Quant.scale, Quant.inverse, Quant.divided, Quant.exponent, Quant.magic, Quant.add,
                             Quant.subtract):
                    for z in (x, h):
                        steps.but_last()
                        steps.pair(step(z))
                if not first:
                    add_y(S23, t - 1, tile_y)
                steps.all()
                dve.wait_ge(S23.xT_ps, t + 2)
                x.result().then_inc(S23.x_copied, 1)
                if not first:
                    dve.wait_ge(S23.hT_ps, t)
                h.result().then_inc(S23.h_sb, 1)

            def only_h(t, tile_y):
                z = h_quant(*H3)
                make_h23(t, H3[0])
                dve.wait_ge(S23.up_read, t + 1)
                quantise(z)
                dve.wait_ge(S23.hT_ps, t)
                z.result().then_inc(S23.h_sb, 1)
                add_y(S23, t - 1, tile_y)

            def last_h(t, tile_y):
                make_h23(t, F3)
                dve.wait_ge(S23.up_read, t + 1)
                half = F3 // 2
                for i in range(2):
                    c = slice(i * half, (i + 1) * half)
                    z = Quant(h_w[:, c], h_q[:, c], q_a[:, c], q_b[:, c], qs, 32, 1e-30)
                    quantise(z)
                    if i == 0:
                        dve.wait_ge(S23.hT_ps, t)
                    z.result().then_inc(S23.h_sb, 1)
                    if i == 0:
                        add_y(S23, t - 1, tile_y)

            first_x = x_quant(0, *X2)
            dve.wait_ge(c_tile_made, 1)
            steps.pair(first_x.largest())
            steps.pair(down_b.add())
            steps.but_last()
            steps.pair(first_x.scale())
            steps.but_last()
            steps.pair(down_b.subtract())
            steps.but_last()
            steps.pair(first_x.inverse())
            steps.but_last()
            finish(down_b, U2 + U3 + 2)
            steps.all()
            link(first_x.divided())
            link(first_x.exponent())
            link(first_x.magic())
            link(first_x.add())
            link(first_x.subtract())
            first_x.result().then_inc(S23.x_copied, 1)
            add_y(S1, T1 - 1, TILES - 1)
            dve.wait_ge(S1.y_sb, T1)
            for t in range(AHEAD, TILES):
                combine1(t)
            only_x(1)
            h_and_x(0, H2, X2, 2, 0, first=True)
            with dve.Fori(1, TILES - 2) as t:
                steps.enter(t - 1, 2 * QUANT_STEPS)
                h_and_x(t, H2, X2, t + 2, t - 1)
            steps.leave(TILES - 3)
            for t in (TILES - 2, TILES - 1):
                h_and_x(t, H2, X3, t + 2 - TILES, t - 1)
            h_and_x(TILES, H3, X3, 2, TILES - 1)
            with dve.Fori(TILES + 1, 2 * TILES - 2) as t:
                steps.enter(t - TILES - 1, 2 * QUANT_STEPS)
                h_and_x(t, H3, X3, t + 2 - TILES, t - 1 - TILES)
            steps.leave(TILES - 3)
            only_h(2 * TILES - 2, TILES - 3)
            last_h(2 * TILES - 1, TILES - 2)
            add_y(S23, 2 * TILES - 1, TILES - 1)


def kernel(**inputs):
    import numpy as np
    import concourse.bacc as bacc
    from concourse.bass_utils import run_bass_kernel_spmd

    a = {k: np.asarray(v) for k, v in inputs.items()}

    def k_first(w, k):
        e, rows, n = w.shape
        padded = np.zeros((e, k * P, n), w.dtype)
        padded[:, :rows] = w
        return padded.reshape(e, k, P, n).transpose(2, 1, 0, 3)

    def with_shared(w, shared):
        return np.concatenate([shared[None], w], axis=0)

    def gate(w):
        return w.reshape(KT, P, E).transpose(1, 0, 2)

    wu = np.stack([np.stack([a[f"L{i}_cond_{n}"].reshape(KT, P) for i in range(LAYERS)]) for n in "wu"])
    down3 = a["L3_ffn_down_w"].reshape(KT, P, F3 // WU, WU).transpose(0, 2, 1, 3).reshape(-1, P, WU)
    gate3, up3 = (a[f"L3_ffn_{n}_w"].reshape(F3 // P, P, CH) for n in ("gate", "up"))
    index = np.concatenate([a["L2_ffn_down_reorder_index"]] * 2)
    arrays = {
        "x_in": a["x"].reshape(TOK, CH),
        "side_in": a["fside_BxSxS_0"].reshape(BATCH, TIME, KT, P).transpose(3, 2, 0, 1).reshape(P, GROUPS, TIME),
        "cond_in": np.broadcast_to(a["cond_512"], (P, BATCH, 64)),
        "wu_in": wu.transpose(3, 0, 1, 2),
        "gw0_in": gate(a["L0_ffn_gate_w"].T),
        "w1_0_in": k_first(a["L0_ffn_w1"].transpose(0, 2, 1), KT),
        "w3_0_in": k_first(a["L0_ffn_w3"].transpose(0, 2, 1), KT),
        "w2_0_in": k_first(a["L0_ffn_w2"].transpose(0, 2, 1), J0),
        "gw1_in": gate(a["L1_ffn_Wg"]),
        "w1_1_in": k_first(with_shared(a["L1_ffn_W1"], a["L1_ffn_sw1"]), KT),
        "w3_1_in": k_first(with_shared(a["L1_ffn_W3"], a["L1_ffn_sw3"]), KT),
        "w2_1_in": k_first(with_shared(a["L1_ffn_W2"], a["L1_ffn_sw2"]), J1),
        "gu2_in": np.concatenate([a["L2_ffn_w_gate"], a["L2_ffn_w_up"]]),
        "down2_in": a["L2_ffn_w_down"].reshape(KT, P, F2).transpose(1, 0, 2),
        "idx2_in": index.reshape(GU2, P).T,
        "w3q_in": np.concatenate([np.concatenate([gate3, up3], axis=2), down3]),
    }
    arrays = {n: np.ascontiguousarray(v) for n, v in arrays.items()}
    nc = bacc.Bacc("TRN2", target_bir_lowering=False, num_devices=1)
    args = [nc.dram_tensor(n, v.shape, mybir.dt.from_np(v.dtype), kind="ExternalInput").ap() for n, v in arrays.items()]
    out = nc.dram_tensor("out", (TOK, CH), FP32, kind="ExternalOutput").ap()
    program(nc, *args, out)
    r = run_bass_kernel_spmd(nc, [arrays], core_ids=[0])
    return r.results[0]["out"].reshape(BATCH, TIME, CH)
```
